# Optimizing a Trainium2 kernel written in Bass

```python
import numpy as np
import jax
import jax.numpy as jnp

def _softmax(x, axis=-1):
    return jax.nn.softmax(x, axis=axis)

def _gelu(x):
    return jax.nn.gelu(x, approximate=True)

def _silu(x):
    return jax.nn.silu(x)

def _sigmoid(x):
    return jax.nn.sigmoid(x)

def _layernorm(x, axis=-1, eps=1e-05):
    m = jnp.mean(x, axis=axis, keepdims=True)
    v = jnp.var(x, axis=axis, keepdims=True)
    return (x - m) / jnp.sqrt(v + eps)

def _scatter_add(tgt, idx, src, axis=0):
    return tgt.at[idx].add(src)

def _segment_sum(src, seg, n):
    return jax.ops.segment_sum(src, seg, n)
kernel_name = 'mk_gnn_resnorm_d2_gnn_r8_832459'

def setup_inputs(seed: int=0):
    np.random.seed(seed)
    _w = jnp.asarray

    def _rec_inputs():
        import jax
        import jax.numpy as jnp
        _gk = jax.random.key(seed)
        x = 0.0001712 + 1 * jax.random.normal(jax.random.fold_in(_gk, 1), (12500, 16), jnp.float32)
        _s = jax.random.randint(jax.random.fold_in(_gk, 2), (200000,), 0, 12500, jnp.int32)
        _d = jax.random.randint(jax.random.fold_in(_gk, 3), (200000,), 0, 12500, jnp.int32)
        _loop = jnp.arange(12500, dtype=jnp.int32)
        src = jnp.concatenate([_s, _d, _loop])
        dst = jnp.concatenate([_d, _s, _loop])
        _o = jnp.argsort(dst, stable=True)
        src = src[_o]
        dst = dst[_o]
        edge_attr_16 = -0.00010739 + 0.99994 * jax.random.normal(jax.random.fold_in(_gk, 12), (412500, 16), jnp.float32)
        edge_type_8 = jax.random.randint(jax.random.fold_in(_gk, 13), (412500,), 0, 8, jnp.int32)
        edge_type_90 = jax.random.randint(jax.random.fold_in(_gk, 14), (412500,), 0, 90, jnp.int32)
        return (x, src, dst, edge_attr_16, edge_type_8, edge_type_90)
    x, src, dst, edge_attr_16, edge_type_8, edge_type_90 = _rec_inputs()

    def _L0_gnn_setup():
        import jax, jax.numpy as jnp
        import numpy as np
        N, E, IN, OUT, R, B = (6250, 100000, 16, 16, 90, 30)
        key = jax.random.key(seed)
        ks = jax.random.split(key, 9)
        h = jax.random.normal(ks[0], (N, IN), dtype=jnp.float32)
        he = jax.random.normal(ks[1], (E, IN), dtype=jnp.float32)
        Ws = jax.random.normal(ks[2], (OUT, IN), dtype=jnp.float32) * 0.1
        Wa = jax.random.normal(ks[3], (1, 3 * OUT), dtype=jnp.float32) * 0.1
        weight = jax.random.normal(ks[4], (B, IN, OUT), dtype=jnp.float32) * 0.1
        w_comp = jax.random.normal(ks[5], (R, B), dtype=jnp.float32) * 0.1
        src = jax.random.randint(ks[6], (E,), 0, N)
        dst = jax.random.randint(ks[7], (E,), 0, N)
        rel_type = jax.random.randint(ks[8], (E,), 0, R)
        return {'h': h, 'he': he, 'Ws': Ws, 'Wa': Wa, 'weight': weight, 'w_comp': w_comp, 'src': src, 'dst': dst, 'rel_type': rel_type}
    _L0_gnn_all = _L0_gnn_setup()
    _L0_gnn_in = {k: v for k, v in _L0_gnn_all.items() if k in ('Ws', 'Wa', 'weight', 'w_comp')}
    del _L0_gnn_all

    def _L1_gnn_setup():
        import jax, jax.numpy as jnp
        import numpy as np
        N_NODES = 12500
        N_EDGES = 125000
        MSG_DIM = 16
        HID_DIM = 16
        N_EDGE_TYPE = 8
        key = jax.random.key(seed)
        ks = jax.random.split(key, 9)
        features = jax.random.normal(ks[0], (N_NODES, HID_DIM), dtype=jnp.float32)
        edge_src = jax.random.randint(ks[1], (N_EDGES,), 0, N_NODES, dtype=jnp.int32)
        edge_dst = jax.random.randint(ks[2], (N_EDGES,), 0, N_NODES, dtype=jnp.int32)
        edge_type = jax.random.randint(ks[3], (N_EDGES,), 0, N_EDGE_TYPE, dtype=jnp.int32)
        edge_emb = jax.random.normal(ks[4], (N_EDGE_TYPE, MSG_DIM * HID_DIM), dtype=jnp.float32) * 0.1
        s = 1.0 / np.sqrt(HID_DIM)
        w_ih = jax.random.uniform(ks[5], (3 * HID_DIM, MSG_DIM), minval=-s, maxval=s, dtype=jnp.float32)
        w_hh = jax.random.uniform(ks[6], (3 * HID_DIM, HID_DIM), minval=-s, maxval=s, dtype=jnp.float32)
        b_ih = jax.random.uniform(ks[7], (3 * HID_DIM,), minval=-s, maxval=s, dtype=jnp.float32)
        b_hh = jax.random.uniform(ks[8], (3 * HID_DIM,), minval=-s, maxval=s, dtype=jnp.float32)
        return {'features': features, 'edge_src': edge_src, 'edge_dst': edge_dst, 'edge_type': edge_type, 'edge_emb': edge_emb, 'w_ih': w_ih, 'w_hh': w_hh, 'b_ih': b_ih, 'b_hh': b_hh}
    _L1_gnn_all = _L1_gnn_setup()
    _L1_gnn_in = {k: v for k, v in _L1_gnn_all.items() if k in ('edge_emb', 'w_ih', 'w_hh', 'b_ih', 'b_hh')}
    del _L1_gnn_all
    return {'x': x, 'src': src, 'dst': dst, 'edge_attr_16': edge_attr_16, 'edge_type_8': edge_type_8, 'edge_type_90': edge_type_90, 'L0_gnn_Ws': _L0_gnn_in['Ws'], 'L0_gnn_Wa': _L0_gnn_in['Wa'], 'L0_gnn_weight': _L0_gnn_in['weight'], 'L0_gnn_w_comp': _L0_gnn_in['w_comp'], 'L1_gnn_edge_emb': _L1_gnn_in['edge_emb'], 'L1_gnn_w_ih': _L1_gnn_in['w_ih'], 'L1_gnn_w_hh': _L1_gnn_in['w_hh'], 'L1_gnn_b_ih': _L1_gnn_in['b_ih'], 'L1_gnn_b_hh': _L1_gnn_in['b_hh']}

def reference(x, src, dst, edge_attr_16, edge_type_8, edge_type_90, L0_gnn_Ws, L0_gnn_Wa, L0_gnn_weight, L0_gnn_w_comp, L1_gnn_edge_emb, L1_gnn_w_ih, L1_gnn_w_hh, L1_gnn_b_ih, L1_gnn_b_hh):
    import jax
    import jax.numpy as jnp

    def _L0_gnn_ref(h, he, Ws, Wa, weight, w_comp, src, dst, rel_type):
        import jax, jax.numpy as jnp
        import numpy as np
        N, E, IN, OUT, R, B = (6250, 100000, 16, 16, 90, 30)
        n_nodes, in_dim = h.shape
        num_bases, _, out_dim = weight.shape
        num_rels = w_comp.shape[0]
        V = weight.reshape(in_dim, num_bases, out_dim)
        W_rel = jnp.matmul(w_comp, V).reshape(num_rels, in_dim, out_dim)
        h_src = h[src]
        z_src = h_src @ Ws.T
        z_dst = h[dst] @ Ws.T
        z_e = he @ Ws.T
        e = jnp.concatenate([z_src, z_e, z_dst], axis=1) @ Wa.T
        msg = jnp.einsum('ei,eio->eo', h_src, W_rel[rel_type]) * e
        h_out = jax.ops.segment_sum(msg, dst, num_segments=n_nodes)
        return h_out

    def _L1_gnn_ref(features, edge_src, edge_dst, edge_type, edge_emb, w_ih, w_hh, b_ih, b_hh):
        import jax, jax.numpy as jnp
        import numpy as np
        N_NODES = 12500
        N_EDGES = 125000
        MSG_DIM = 16
        HID_DIM = 16
        N_EDGE_TYPE = 8
        n_nodes = features.shape[0]
        A = edge_emb[edge_type].reshape(-1, MSG_DIM, HID_DIM)
        h_src = features[edge_src]
        msg = jnp.einsum('emh,eh->em', A, h_src)
        m = jax.ops.segment_sum(msg, edge_dst, num_segments=n_nodes)
        gi = m @ w_ih.T + b_ih
        gh = features @ w_hh.T + b_hh
        i_r, i_z, i_n = jnp.split(gi, 3, axis=-1)
        h_r, h_z, h_n = jnp.split(gh, 3, axis=-1)
        r = jax.nn.sigmoid(i_r + h_r)
        z = jax.nn.sigmoid(i_z + h_z)
        n = jnp.tanh(i_n + r * h_n)
        h_new = (1.0 - z) * n + z * features
        return h_new
    x = _layernorm(x + _L0_gnn_ref(x, edge_attr_16, L0_gnn_Ws, L0_gnn_Wa, L0_gnn_weight, L0_gnn_w_comp, src, dst, edge_type_90), axis=-1)
    x = _layernorm(x + _L1_gnn_ref(x, src, dst, edge_type_8, L1_gnn_edge_emb, L1_gnn_w_ih, L1_gnn_w_hh, L1_gnn_b_ih, L1_gnn_b_hh), axis=-1)
    return x

_drawn_inputs = setup_inputs


def setup_inputs(seed=0):
    import zlib

    import numpy as np

    out = dict(_drawn_inputs(seed))
    spreads = {}
    factors = {}
    for name, (base, spread) in spreads.items():
        noise = np.random.default_rng([zlib.crc32(name.encode()), seed]).standard_normal(out[name].shape)
        drawn = base * np.exp(spread * noise) if base else spread * noise
        out[name] = jnp.asarray(drawn.astype(out[name].dtype))
    for name, factor in factors.items():
        out[name] = (out[name] * factor).astype(out[name].dtype)
    return out
```

```python
import concourse.bass as bass
from concourse import mybir
from contextlib import ExitStack

F32 = mybir.dt.float32
I32 = mybir.dt.int32
BF16 = mybir.dt.bfloat16
ALU = mybir.AluOpType
ACT = mybir.ActivationFunctionType
AX = mybir.AxisListType.X

P = 128
D = 16
EPS = 1e-5


def build(nc, x, src, dst, edge_attr, type_8, type_90, Ws, Wa, weight, w_comp,
          edge_emb, w_ih, w_hh, b_ih, b_hh, out):
    NODES, EDGES = x.shape[0], src.shape[0]
    RELS, BASES = w_comp.shape
    TYPES = edge_emb.shape[0]
    CHUNK = 52
    CHUNKS = -(-EDGES // (P * CHUNK))
    CHUNKS += CHUNKS % 2
    COLS = CHUNKS * CHUNK
    LAST = EDGES - (P - 1) * COLS
    FULL = LAST // CHUNK // 2 * 2
    ROWS = P * COLS
    TILES = -(-NODES // P)
    TAIL = NODES - (TILES - 1) * P
    GROUP = 7
    GROUPS = TILES // GROUP
    REST = 112
    RD = D + 1
    RW = RELS * RD
    BANKS = 3
    BW = RW // BANKS
    HOT = 13
    HOTS = CHUNK // HOT
    assert TILES % GROUP == 0 and GROUPS % 2 == 0 and CHUNK % HOT == 0 and RW % BANKS == 0 and BW <= 512
    assert 0 < LAST <= COLS and TILES <= P
    PAIRS = CHUNKS // 2

    ctx = ExitStack()
    with ctx:
        def sb(name, shape, dt=F32):
            return ctx.enter_context(nc.sbuf_tensor(name, shape, dt))

        def ps(name, shape, dt=F32):
            return ctx.enter_context(nc.psum_tensor(name, shape, dt))

        def sem(name):
            return ctx.enter_context(nc.semaphore(name))

        def sems(name):
            return [sem(f"{name}_{h}") for h in range(2)]

        relation_dram = nc.dram_tensor("relation_mats", (D * RELS, D), F32).ap()
        table0 = nc.dram_tensor("relation_table", (TILES * P * RELS, RD), F32).ap()
        table1 = nc.dram_tensor("type_table", (TILES * P * TYPES, D), F32).ap()
        scan0 = nc.dram_tensor("scanned_0", (ROWS + 1, 2 * D), F32).ap()
        scan1 = nc.dram_tensor("scanned_1", (ROWS + 1, D), F32).ap()

        x_sb = sb("x_sb", [P, TILES + 2, D])
        x_tile = sb("x_tile", [P, 2, D])
        state = sb("state", [P, TILES, D])
        cat = sb("cat", [P, 2, GROUP, 2 * D])
        src_sb = sb("src_sb", [P, COLS + 2 * CHUNK], I32)
        t90_sb = sb("t90_sb", [P, COLS + 2 * CHUNK], I32)
        t8_sb = sb("t8_sb", [P, COLS + 2 * CHUNK], I32)
        dst_sb = sb("dst_sb", [P, COLS + 1], I32)
        dst_before = sb("dst_before", [P, 1], I32)
        whole = sb("whole", [P, COLS])
        ident = sb("ident", [P, P])
        ones = sb("ones", [P, P])
        earlier = sb("earlier", [P, P])
        iota_i = sb("iota_i", [P, P], I32)
        run_start = sb("run_start", [P, 1], I32)
        iota_bf = sb("iota_bf", [P, P], BF16)
        zeros_bf = sb("zeros_bf", [P, P], BF16)
        zero_row = sb("zero_row", [1, 2 * D])
        wcT = sb("wcT", [BASES, RELS])
        basis = sb("basis", [BASES, D * D])
        mats = sb("mats", [RELS, D * D])
        Ws_sb = sb("Ws_sb", [D, D])
        WaT = sb("WaT", [D, 3])
        WaB = sb("WaB", [D, 2, P])
        rel_w = sb("rel_w", [D, RELS, RD])
        he_w = sb("he_w", [P, D])
        dst_w = sb("dst_w", [P, D])
        dst_score = sb("dst_score", [P, TILES])
        type_w = sb("type_w", [D, TYPES, D])
        gate_w = sb("gate_w", [2 * D + 2, 4 * D])
        xT = sb("xT", [D, 2, P])
        t0_buf = sb("t0_buf", [P, 2, RW])
        idx = sb("idx", [P, 2, CHUNK], I32)
        he = sb("he", [P, 2, CHUNK, D])
        rows0 = sb("rows0", [P, 2, CHUNK, RD])
        rows1 = sb("rows1", [P, 2, CHUNK, D])
        he_dot = sb("he_dot", [P, CHUNK, D])
        score = sb("score", [P, CHUNK])
        weighted = sb("weighted", [P, CHUNK, D])
        cont = sb("cont", [P, CHUNK])
        scanned = sb("scanned", [P, 2, CHUNK, 2 * D])
        dst_lo_i = sb("dst_lo_i", [P, CHUNK], I32)
        dst_hi_i = sb("dst_hi_i", [P, CHUNK], I32)
        dst_lo = sb("dst_lo", [P, CHUNK], BF16)
        dst_hi = sb("dst_hi", [P, CHUNK], BF16)
        hot_lo = sb("hot_lo", [P, 2, HOT, P], BF16)
        hot_hi = sb("hot_hi", [P, 2, HOT, TILES], BF16)
        first = sb("first", [P, 4])
        flag_cols = sb("flag_cols", [P, 2, 2 * D])
        fix_row = sb("fix_row", [P, 1], I32)
        pass_on = sb("pass_on", [2 * D, P])
        take_in = sb("take_in", [2 * D, P])
        endsT = sb("endsT", [2 * D, P])
        carryT = sb("carryT", [2 * D, P])
        carry = sb("carry", [P, 2 * D])
        last_state = sb("last_state", [P, 2 * D])
        degree = sb("degree", [TILES, P])
        node_end = sb("node_end", [TILES, P])
        node_row = sb("node_row", [P, TILES + 2 * GROUP], I32)
        group_row = sb("group_row", [P, 2, GROUP], I32)
        sums0 = sb("sums0", [P, 2, GROUP, 2 * D])
        sums1 = sb("sums1", [P, 2, GROUP, D])
        val = sb("val", [P, GROUP, D])
        tmp = sb("tmp", [P, GROUP, D])
        stat = sb("stat", [P, 4, GROUP])
        std = sb("std", [P, GROUP])
        catT = sb("catT", [2 * D + 2, GROUP * P])
        t1_buf = sb("t1_buf", [P, 2, GROUP * TYPES * D])
        gates = sb("gates", [P, GROUP, 2 * D])
        cand = sb("cand", [P, GROUP, D])
        out_buf = sb("out_buf", [P, 2, GROUP, D])

        ps_table = [ps(f"ps_table_{h}", [P, BANKS, 512]) for h in range(2)]
        ps_misc = ps("ps_misc", [P, 512])
        ps_hist = ps("ps_hist", [P, 512])

        def gate_view(h):
            return ps_table[h][:, 0, 0:GROUP * 4 * D].rearrange("p (t g) -> p t g", g=4 * D)

        pads_set = sem("pads_set")
        consts_set = sem("consts_set")
        weights_in, x_in, edges_in, late_in = sem("weights_in"), sem("x_in"), sem("edges_in"), sem("late_in")
        wab_set, mats_ps, mats_sb, mats_out = sem("wab_set"), sem("mats_ps"), sem("mats_sb"), sem("mats_out")
        rel_in, scores_ps, rel_set = sem("rel_in"), sem("scores_ps"), sem("rel_set")
        prep = sem("prep")
        flags_set, flags_ps = sem("flags_set"), sem("flags_ps")
        x_tile_set = sem("x_tile_set")
        xT_ps, xT_sb, t0_ps = sem("xT_ps"), sem("xT_sb"), sem("t0_ps")
        t0_dve, t0_act, t0_out = sems("t0_dve"), sems("t0_act"), sems("t0_out")
        idx0_set, rows0_in, rows0_used = sems("idx0_set"), sems("rows0_in"), sems("rows0_used")
        he_in, he_used = sems("he_in"), sems("he_used")
        chunk_step = sem("chunk_step")
        scan0_set, scan0_out = sems("scan0_set"), sems("scan0_out")
        hot_set, hot_used, hist_ps = sems("hot_set"), sems("hot_used"), sem("hist_ps")
        node_step, offset_ps, rows_ps = sem("node_step"), sem("offset_ps"), sem("rows_ps")
        carry_step = sem("carry_step")
        ends_ps, carry_ps, carry_set, fixed = sem("ends_ps"), sem("carry_ps"), sem("carry_set"), sem("fixed")
        gather_begun = sem("gather_begun")
        group0_set, sums0_in = sems("group0_set"), sems("sums0_in")
        ln_step = sem("ln_step")
        var_set, std_set, y_set = sem("var_set"), sem("std_set"), sem("y_set")
        state_set = sem("state_set")
        yT_ps, yT_sb, t1_ps, t1_sb, t1_out = sem("yT_ps"), sem("yT_sb"), sem("t1_ps"), sem("t1_sb"), sems("t1_out")
        idx1_set, rows1_in, cont_set = sems("idx1_set"), sems("rows1_in"), sem("cont_set")
        scan1_set, scan1_out = sems("scan1_set"), sems("scan1_out")
        group1_set, sums1_in = sems("group1_set"), sems("sums1_in")
        m_set, mT_ps, mT_sb = sem("m_set"), sem("mT_ps"), sem("mT_sb")
        gates_ps, gates_set, pre_set, cand_set = sem("gates_ps"), sem("gates_set"), sem("pre_set"), sem("cand_set")
        out_set, out_out = sems("out_set"), sems("out_out")

        block = ctx.enter_context(nc.Block())

        def col(n):
            return bass.ds(n * CHUNK, CHUNK)

        def tiles(g):
            return bass.ds(g * GROUP, GROUP)

        def edge_views(a):
            tail = " f" if len(a.shape) == 2 else ""
            body = a[0:(P - 1) * COLS].rearrange(f"(p c){tail} -> p c{tail}", c=COLS)
            last = a[(P - 1) * COLS:EDGES].rearrange(f"(p c){tail} -> p c{tail}", p=1)
            return body, last

        he_body, he_last = edge_views(edge_attr)
        scan0_v = scan0[0:ROWS, :].rearrange("(p c) f -> p c f", c=COLS)
        scan1_v = scan1[0:ROWS, :].rearrange("(p c) f -> p c f", c=COLS)
        table0_v = table0.rearrange("(t p r) f -> p t (r f)", p=P, r=RELS)
        table1_v = table1.rearrange("(t p r) f -> p t (r f)", p=P, r=TYPES)
        out_v = out[0:(TILES - 1) * P, :].rearrange("(t p) f -> p t f", p=P)
        type_cols = type_w[:, :, :].rearrange("h t m -> h (t m)")
        xT_bank = [ps_misc, ps_hist]
        score_ps = ps_table[1][:, 0, :]
        WEIGHTS_IN, X_IN, EDGES_IN, LATE_IN, HE_IN = 4 * 16, 2 * 16, 13 * 16, 11 * 16, 3 * 16
        ROWS_IN, SUMS_IN = 16 * CHUNK, 16 * GROUP

        @block.sync
        def _(sp):
            with nc.allow_non_contiguous_dma(reason="small weights, transposed once"):
                sp.wait_ge(pads_set, 1)
                sp.dma_start(wcT[:, :], w_comp.rearrange("r b -> b r")).then_inc(weights_in, 16)
                sp.dma_start(basis[:, :].rearrange("b (i o) -> b i o", o=D),
                             weight.rearrange("b i o -> (b i o)").rearrange("(i b o) -> b i o", i=D, b=BASES)
                             ).then_inc(weights_in, 16)
                sp.dma_start(Ws_sb[:, :], Ws).then_inc(weights_in, 16)
                sp.dma_start(WaT[:, :], Wa.rearrange("a (k o) -> o (a k)", o=D)).then_inc(weights_in, 16)
                sp.dma_start(x_sb[:, 0:TILES - 1, :],
                             x[0:(TILES - 1) * P, :].rearrange("(t p) f -> p t f", p=P)).then_inc(x_in, 16)
                sp.dma_start(x_sb[0:TAIL, TILES - 1, :], x[(TILES - 1) * P:NODES, :]).then_inc(x_in, 16)
                sp.wait_ge(mats_sb, 1)
                sp.dma_start(relation_dram.rearrange("(i r) o -> r i o", r=RELS),
                             mats[:, :].rearrange("r (i o) -> r i o", o=D)).then_inc(mats_out, 16)
                sp.wait_ge(mats_out, 16)
                sp.dma_start(rel_w[:, :, 0:D], relation_dram.rearrange("(r i) o -> i r o", i=D)).then_inc(rel_in, 16)
                for a, to, at in ((src, src_sb, 0), (type_90, t90_sb, 0), (dst, dst_sb, 1), (type_8, t8_sb, 0)):
                    body, last = edge_views(a)
                    sp.dma_start(to[0:REST, at:at + COLS], body[0:REST, :]).then_inc(edges_in, 16)
                    sp.dma_start(to[REST:P - 1, at:at + COLS], body[REST:P - 1, :]).then_inc(edges_in, 16)
                    sp.dma_start(to[P - 1:P, at:at + LAST], last).then_inc(edges_in, 16)
                sp.dma_start(dst_before[1:P, :], edge_views(dst)[0][:, COLS - 1:COLS]).then_inc(edges_in, 16)
                sp.dma_start(type_w[:, :, :], edge_emb.rearrange("t (m h) -> h t m", h=D)).then_inc(late_in, 16)
                for w, row, own in ((w_ih, 0, 2 * D), (w_hh, D, 3 * D)):
                    sp.dma_start(gate_w[row:row + D, 0:2 * D], w[0:2 * D, :].rearrange("g i -> i g")
                                 ).then_inc(late_in, 16)
                    sp.dma_start(gate_w[row:row + D, own:own + D], w[2 * D:3 * D, :].rearrange("g i -> i g")
                                 ).then_inc(late_in, 16)
                for b, row, own in ((b_ih, 2 * D, 2 * D), (b_hh, 2 * D + 1, 3 * D)):
                    b = b.rearrange("(a g) -> a g", a=1)
                    sp.dma_start(gate_w[row:row + 1, 0:2 * D], b[:, 0:2 * D]).then_inc(late_in, 16)
                    sp.dma_start(gate_w[row:row + 1, own:own + D], b[:, 2 * D:3 * D]).then_inc(late_in, 16)
                sp.dma_start(scan0[ROWS:ROWS + 1, :], zero_row[:, :]).then_inc(late_in, 16)
                sp.dma_start(scan1[ROWS:ROWS + 1, :], zero_row[:, 0:D]).then_inc(late_in, 16)

            with sp.Fori(0, TILES // 2) as i:
                for h in range(2):
                    sp.wait_ge(t0_dve[h], i + 1)
                    sp.wait_ge(t0_act[h], i + 1)
                    sp.dma_start(table0_v[:, bass.ds(i * 2 + h, 1), :], t0_buf[:, h:h + 1, :]).then_inc(t0_out[h], 16)

            def load_he(n, h):
                sp.dma_start(he[0:REST, h, :, :], he_body[0:REST, col(n), :]).then_inc(he_in[h], 16)
                sp.dma_start(he[REST:P - 1, h, :, :], he_body[REST:P - 1, col(n), :]).then_inc(he_in[h], 16)

            with sp.Fori(0, FULL // 2) as i:
                for h in range(2):
                    sp.wait_ge(he_used[h], i)
                    load_he(i * 2 + h, h)
                    sp.dma_start(he[P - 1:P, h, :, :], he_last[:, col(i * 2 + h), :]).then_inc(he_in[h], 16)
            for n in range(FULL, CHUNKS):
                h = n % 2
                sp.wait_ge(he_used[h], n // 2)
                load_he(n, h)
                left = min(CHUNK, max(LAST - n * CHUNK, 1))
                at = min(n * CHUNK, LAST - left)
                sp.dma_start(he[P - 1:P, h, 0:left, :], he_last[:, at:at + left, :]).then_inc(he_in[h], 16)

            with sp.Fori(0, GROUPS // 2) as i:
                for h in range(2):
                    sp.wait_ge(t1_sb, i * 2 + h + 1)
                    sp.dma_start(table1_v[:, tiles(i * 2 + h), :],
                                 t1_buf[:, h, :].rearrange("p (t f) -> p t f", t=GROUP)).then_inc(t1_out[h], 16)

            with sp.Fori(0, GROUPS // 2 - 1) as i:
                for h in range(2):
                    sp.wait_ge(out_set[h], i + 1)
                    sp.dma_start(out_v[:, tiles(i * 2 + h), :], out_buf[:, h, :, :]).then_inc(out_out[h], 16)
            sp.wait_ge(out_set[0], GROUPS // 2)
            sp.dma_start(out_v[:, tiles(GROUPS - 2), :], out_buf[:, 0, :, :]).then_inc(out_out[0], 16)
            sp.wait_ge(out_set[1], GROUPS // 2)
            sp.dma_start(out_v[:, TILES - GROUP:TILES - 1, :], out_buf[:, 1, 0:GROUP - 1, :]).then_inc(out_out[1], 16)
            sp.dma_start(out[(TILES - 1) * P:NODES, :], out_buf[0:TAIL, 1, GROUP - 1, :]).then_inc(out_out[1], 16)
            sp.wait_ge(out_out[0], 16 * (GROUPS // 2))
            sp.wait_ge(out_out[1], 16 * (GROUPS // 2 + 1))

        @block.gpsimd
        def _(pool):
            pool.memset(ident[:, :], 0.0)
            pool.memset(earlier[:, :], 1.0).then_inc(consts_set, 1)
            pool.wait_ge(consts_set, 1)
            pool.affine_select(out=ident[:, :], in_=ident[:, :], compare_op=ALU.not_equal, fill=1.0, base=0,
                               pattern=[[-1, P]], channel_multiplier=1)
            pool.affine_select(out=earlier[:, :], in_=earlier[:, :], compare_op=ALU.is_gt, fill=0.0, base=0,
                               pattern=[[1, P]], channel_multiplier=-1)
            pool.iota(run_start[:, :], pattern=[[1, 1]], base=-1, channel_multiplier=COLS)
            pool.iota(iota_i[:, :], pattern=[[1, P]], base=0, channel_multiplier=0).then_inc(consts_set, 1)

            pool.wait_ge(x_in, X_IN)
            for h in range(2):
                pool.tensor_copy(x_tile[:, h, :], x_sb[:, h, :]).then_inc(x_tile_set, 1)
            with pool.Fori(0, TILES // 2) as i:
                for h in range(2):
                    pool.wait_ge(xT_ps, i * 2 + h + 1)
                    pool.tensor_copy(x_tile[:, h, :], x_sb[:, bass.ds(i * 2 + h + 2, 1), :].rearrange(
                        "p t f -> p (t f)")).then_inc(x_tile_set, 1)

            def gather(rows, table, index, width, landed):
                pool.sem_inc(gather_begun, 1)
                for k in range(width):
                    pool.indirect_dma_start(out=rows[:, k, :], out_offset=None, in_=table,
                                            in_offset=bass.IndirectOffsetOnAxis(ap=index[:, k:k + 1], axis=0)
                                            ).then_inc(landed, 16)

            def add_carries(layer, scan, scan_out, width):
                for h in range(2):
                    pool.wait_ge(scan_out[h], 16 * PAIRS)
                pool.wait_ge(carry_set, layer + 1)
                pool.indirect_dma_start(out=scan, out_offset=bass.IndirectOffsetOnAxis(ap=fix_row[:, 0:1], axis=0),
                                        in_=carry[:, 0:width], in_offset=None, compute_op=ALU.add
                                        ).then_inc(fixed, 16)

            with pool.Fori(0, PAIRS) as i:
                for h in range(2):
                    pool.wait_ge(idx0_set[h], i + 1)
                    pool.wait_ge(rows0_used[h], i)
                    for half in range(2):
                        pool.wait_ge(t0_out[half], 16 * (TILES // 2))
                    gather(rows0[:, h, :, :], table0, idx[:, h, :], CHUNK, rows0_in[h])
            add_carries(0, scan0, scan0_out, 2 * D)
            pool.wait_ge(late_in, LATE_IN)
            with pool.Fori(0, GROUPS // 2) as i:
                for h in range(2):
                    pool.wait_ge(group0_set[h], i + 1)
                    pool.wait_ge(y_set, i * 2)
                    pool.wait_ge(fixed, 16)
                    gather(sums0[:, h, :, :], scan0, group_row[:, h, :], GROUP, sums0_in[h])

            with pool.Fori(0, PAIRS) as i:
                for h in range(2):
                    pool.wait_ge(idx1_set[h], i + 1)
                    pool.wait_ge(scan1_set[h], i)
                    for half in range(2):
                        pool.wait_ge(t1_out[half], 16 * (GROUPS // 2))
                    gather(rows1[:, h, :, :], table1, idx[:, h, :], CHUNK, rows1_in[h])
            add_carries(1, scan1, scan1_out, D)
            with pool.Fori(0, GROUPS // 2) as i:
                for h in range(2):
                    pool.wait_ge(group1_set[h], i + 1)
                    pool.wait_ge(m_set, i * 2)
                    pool.wait_ge(fixed, 32)
                    gather(sums1[:, h, :, :], scan1, group_row[:, h, :], GROUP, sums1_in[h])

        @block.tensor
        def _(pe):
            pe.wait_ge(weights_in, WEIGHTS_IN)
            pe.matmul(ps_misc[0:RELS, 0:D * D], wcT[:, :], basis[:, :], start=True, stop=True).then_inc(mats_ps, 1)
            pe.wait_ge(wab_set, 1)
            pe.matmul(score_ps[0:D, 0:1], Ws_sb[:, :], WaT[:, 0:1], start=True, stop=True)
            pe.matmul(score_ps[:, D:2 * D], WaB[:, 0, :], Ws_sb[:, :], start=True, stop=True)
            pe.matmul(score_ps[:, 2 * D:3 * D], WaB[:, 1, :], Ws_sb[:, :], start=True, stop=True).then_inc(scores_ps, 1)

            def transpose_x(t, h):
                pe.wait_ge(x_tile_set, t + 1)
                pe.transpose(xT_bank[h][0:D, 0:P], x_tile[:, h, :], ident[:, :]).then_inc(xT_ps, 1)

            pe.wait_ge(consts_set, 2)
            pe.wait_ge(mats_sb, 1)
            transpose_x(0, 0)
            pe.wait_ge(rel_in, 16)
            pe.wait_ge(rel_set, 1)
            rel_cols = rel_w[:, :, :].rearrange("i r f -> i (r f)")
            with pe.Fori(0, TILES // 2) as i:
                for h in range(2):
                    pe.wait_ge(xT_sb, i * 2 + h)
                    transpose_x(i * 2 + h + 1, 1 - h)
                    pe.wait_ge(xT_sb, i * 2 + h + 1)
                    pe.wait_ge(t0_dve[h], i)
                    pe.wait_ge(t0_act[h], i)
                    for b in range(BANKS):
                        last = pe.matmul(ps_table[h][:, b, 0:BW], xT[:, h, :], rel_cols[:, b * BW:(b + 1) * BW],
                                         start=True, stop=True)
                    last.then_inc(t0_ps, 1)

            pe.wait_ge(flags_set, 1)
            pe.wait_ge(xT_sb, TILES + 1)
            for k in range(2):
                last = pe.matmul(ps_misc[0:2 * D, k * P:(k + 1) * P], flag_cols[:, k, :], ident[:, :],
                                 start=True, stop=True)
            last.then_inc(flags_ps, 1)

            pe.matmul(ps_hist[0:TILES, 0:P], zeros_bf[:, 0:TILES], zeros_bf[:, :], start=True, stop=False)
            with pe.Fori(0, PAIRS) as i:
                for q in range(2 * HOTS):
                    pe.wait_ge(hot_set[q % 2], i * HOTS + q // 2 + 1)
                    for k in range(HOT):
                        last = pe.matmul(ps_hist[0:TILES, 0:P], hot_hi[:, q % 2, k, :], hot_lo[:, q % 2, k, :],
                                         start=False, stop=False)
                    last.then_inc(hot_used[q % 2], 1)
            pe.matmul(ps_hist[0:TILES, 0:P], zeros_bf[:, 0:TILES], zeros_bf[:, :], start=False, stop=True
                      ).then_inc(hist_ps, 1)

            def carries(layer, width):
                pe.wait_ge(carry_step, 1 + 3 * layer)
                pe.transpose(ps_misc[0:width, 0:P], last_state[:, 0:width], ident[:, :]).then_inc(ends_ps, 1)
                pe.wait_ge(carry_step, 3 + 3 * layer)
                pe.transpose(ps_misc[:, P:P + width], carryT[0:width, :], ident[0:width, 0:width]).then_inc(carry_ps, 1)

            carries(0, 2 * D)

            pe.wait_ge(node_step, 2)
            pe.matmul(ps_misc[0:TILES, 2 * P:2 * P + 1], earlier[0:TILES, 0:TILES], node_end[:, P - 1:P],
                      start=True, stop=True).then_inc(offset_ps, 1)
            pe.wait_ge(node_step, 6)
            pe.transpose(ps_misc[:, 3 * P:3 * P + TILES], node_end[:, :], ident[0:TILES, 0:TILES]).then_inc(rows_ps, 1)

            def turn(h, lo, hi):
                for k in range(GROUP):
                    bank = ps_misc if k < 4 else ps_hist
                    last = pe.transpose(bank[0:hi - lo, (k % 4) * P:(k % 4 + 1) * P],
                                        cat[:, h, k, lo:hi], ident[:, :])
                return last

            pe.wait_ge(late_in, LATE_IN)
            with pe.Fori(0, GROUPS // 2) as i:
                for h in range(2):
                    pe.wait_ge(y_set, i * 2 + h + 1)
                    turn(h, D, 2 * D).then_inc(yT_ps, 1)
                    pe.wait_ge(yT_sb, i * 2 + h + 1)
                    pe.wait_ge(t1_sb, i * 2 + h)
                    for k in range(GROUP):
                        last = pe.matmul(ps_table[h][:, k // 4, (k % 4) * P:(k % 4 + 1) * P],
                                         catT[0:D, k * P:(k + 1) * P], type_cols, start=True, stop=True)
                    last.then_inc(t1_ps, 1)

            carries(1, D)

            with pe.Fori(0, GROUPS // 2) as i:
                for h in range(2):
                    pe.wait_ge(m_set, i * 2 + h + 1)
                    turn(h, 0, 2 * D).then_inc(mT_ps, 1)
                    pe.wait_ge(mT_sb, i * 2 + h + 1)
                    pe.wait_ge(pre_set, i * 2 + h)
                    for k in range(GROUP):
                        last = pe.matmul(ps_table[h][:, 0, k * 4 * D:(k + 1) * 4 * D],
                                         catT[:, k * P:(k + 1) * P], gate_w[:, :], start=True, stop=True)
                    last.then_inc(gates_ps, 1)

        @block.scalar
        def _(act):
            act.wait_ge(xT_ps, 1)
            act.copy(xT[:, 0, :], xT_bank[0][0:D, 0:P]).then_inc(xT_sb, 1)
            with act.Fori(0, TILES // 2) as i:
                for h in range(2):
                    act.wait_ge(xT_ps, i * 2 + h + 2)
                    act.copy(xT[:, 1 - h, :], xT_bank[1 - h][0:D, 0:P]).then_inc(xT_sb, 1)
                    act.wait_ge(t0_ps, i * 2 + h + 1)
                    act.wait_ge(t0_out[h], i * 16)
                    act.copy(t0_buf[:, h, 2 * BW:RW], ps_table[h][:, 2, 0:BW]).then_inc(t0_act[h], 1)

            with act.Fori(0, PAIRS) as i:
                for h in range(2):
                    act.wait_ge(scan0_set[h], i + 1)
                    act.dma_start(scan0_v[:, col(i * 2 + h), :], scanned[:, h, :, :]).then_inc(scan0_out[h], 16)

            with act.Fori(0, GROUPS // 2) as i:
                for h in range(2):
                    act.wait_ge(var_set, i * 2 + h + 1)
                    act.activation(std[:, :], stat[:, 3, :], ACT.Sqrt).then_inc(std_set, 1)
                    act.wait_ge(y_set, i * 2 + h + 1)
                    act.copy(state[:, tiles(i * 2 + h), :], cat[:, h, :, D:2 * D]).then_inc(state_set, 1)
                    act.wait_ge(yT_ps, i * 2 + h + 1)
                    act.copy(catT[0:D, 0:4 * P], ps_misc[0:D, :])
                    act.copy(catT[0:D, 4 * P:GROUP * P], ps_hist[0:D, 0:(GROUP - 4) * P]).then_inc(yT_sb, 1)
                    act.wait_ge(t1_ps, i * 2 + h + 1)
                    act.wait_ge(t1_out[h], i * 16)
                    act.copy(t1_buf[:, h, 0:4 * P], ps_table[h][:, 0, :])
                    act.copy(t1_buf[:, h, 4 * P:GROUP * P], ps_table[h][:, 1, 0:(GROUP - 4) * P]).then_inc(t1_sb, 1)

            with act.Fori(0, PAIRS) as i:
                for h in range(2):
                    act.wait_ge(scan1_set[h], i + 1)
                    act.dma_start(scan1_v[:, col(i * 2 + h), :], scanned[:, h, :, 0:D]).then_inc(scan1_out[h], 16)

            with act.Fori(0, GROUPS // 2) as i:
                for h in range(2):
                    act.wait_ge(mT_ps, i * 2 + h + 1)
                    act.copy(catT[0:2 * D, 0:4 * P], ps_misc[0:2 * D, :])
                    act.copy(catT[0:2 * D, 4 * P:GROUP * P], ps_hist[0:2 * D, 0:(GROUP - 4) * P]).then_inc(mT_sb, 1)
                    act.wait_ge(gates_ps, i * 2 + h + 1)
                    act.activation(gates[:, :, :], gate_view(h)[:, :, 0:2 * D], ACT.Sigmoid).then_inc(gates_set, 1)
                    act.wait_ge(pre_set, i * 2 + h + 1)
                    act.activation(cand[:, :, :], tmp[:, :, :], ACT.Tanh).then_inc(cand_set, 1)
                    act.wait_ge(var_set, i * 2 + (GROUPS + h + 1))
                    act.activation(std[:, :], stat[:, 3, :], ACT.Sqrt).then_inc(std_set, 1)

        @block.vector
        def _(dve):
            prep_n = [0]

            def step(ins):
                prep_n[0] += 1
                ins.then_inc(prep, 1)
                dve.wait_ge(prep, prep_n[0])

            dve.memset(x_sb[:, TILES - 1:TILES + 2, :], 0.0)
            for a in (src_sb, t90_sb, t8_sb):
                dve.memset(a[96:P, LAST:COLS], 0)
                dve.memset(a[:, COLS:COLS + 2 * CHUNK], 0)
            dve.memset(dst_sb[96:P, 1 + LAST:1 + COLS], NODES)
            dve.memset(dst_sb[:, 0:1], -1)
            dve.memset(dst_before[:, :], -1)
            dve.memset(gate_w[:, :], 0.0)
            dve.memset(zero_row[:, :], 0.0)
            dve.memset(zeros_bf[:, :], 0.0)
            dve.memset(ones[:, :], 1.0)
            dve.memset(catT[2 * D:2 * D + 2, :], 1.0)
            dve.memset(scanned[:, 1, :, :], 0.0)
            dve.memset(node_row[:, TILES:TILES + 2 * GROUP], 0)
            dve.memset(pass_on[:, 0:1], 0.0)
            dve.memset(endsT[:, :], 0.0).then_inc(pads_set, 1)

            dve.wait_ge(weights_in, WEIGHTS_IN)
            for k in range(2):
                last = dve.tensor_copy(WaB[:, k, :], WaT[:, k + 1:k + 2].to_broadcast([D, P]))
            last.then_inc(wab_set, 1)
            dve.wait_ge(mats_ps, 1)
            dve.tensor_copy(mats[:, :], ps_misc[0:RELS, 0:D * D]).then_inc(mats_sb, 1)
            dve.wait_ge(scores_ps, 1)
            dve.tensor_copy(he_w[:, :], score_ps[:, D:2 * D])
            dve.tensor_copy(dst_w[:, :], score_ps[:, 2 * D:3 * D])
            dve.tensor_copy(rel_w[:, :, D:RD], score_ps[0:D, 0:1].unsqueeze(1).to_broadcast([D, RELS, 1])
                            ).then_inc(rel_set, 1)
            dve.wait_ge(consts_set, 2)
            step(dve.tensor_copy(iota_bf[:, :], iota_i[:, :]))

            with dve.Fori(0, TILES // 2) as i:
                for h in range(2):
                    dve.wait_ge(t0_ps, i * 2 + h + 1)
                    dve.wait_ge(t0_out[h], i * 16)
                    dve.tensor_copy(t0_buf[:, h, 0:2 * BW].rearrange("p (b c) -> p b c", b=2),
                                    ps_table[h][:, 0:2, 0:BW]).then_inc(t0_dve[h], 1)

            def index(n, h, types, count, done):
                dve.scalar_tensor_tensor(out=idx[:, h, :], in0=src_sb[:, col(n)], scalar=float(count),
                                         in1=types[:, col(n)], op0=ALU.mult, op1=ALU.add).then_inc(done[h], 1)

            dve.wait_ge(edges_in, EDGES_IN)
            for h in range(2):
                index(h, h, t90_sb, RELS, idx0_set)

            dve.wait_ge(x_in, X_IN)
            step(dve.tensor_tensor(state[:, :, :], x_sb[:, 0:TILES, :],
                                   dst_w[:, :].unsqueeze(1).to_broadcast([P, TILES, D]), ALU.mult))
            dve.tensor_reduce(dst_score[:, :], state[:, :, :], AX, ALU.add)

            step(dve.tensor_copy(first[:, 0:1], dst_sb[:, 1:2]))
            step(dve.tensor_scalar(whole[:, :], dst_sb[:, 1:1 + COLS], first[:, 0:1], None, ALU.is_equal))
            step(dve.tensor_reduce(first[:, 1:2], whole[:, :], AX, ALU.add))
            dve.tensor_tensor(fix_row[:, :], run_start[:, :], first[:, 1:2], ALU.add)
            dve.tensor_scalar(first[:, 2:3], first[:, 1:2], float(COLS), None, ALU.is_equal)
            step(dve.tensor_tensor(first[:, 3:4], dst_sb[:, 1:2], dst_before[:, :], ALU.is_equal))
            dve.tensor_copy(flag_cols[:, :, :], first[:, 2:4].unsqueeze(2).to_broadcast([P, 2, 2 * D])
                            ).then_inc(flags_set, 1)
            dve.wait_ge(flags_ps, 1)
            step(dve.tensor_copy(take_in[:, :], ps_misc[0:2 * D, P:2 * P]))
            step(dve.tensor_tensor(pass_on[:, 1:P], ps_misc[0:2 * D, 0:P - 1], take_in[:, 1:P], ALU.mult))

            def continues(n):
                return dve.tensor_tensor(cont[:, :], dst_sb[:, bass.ds(n * CHUNK + 1, CHUNK)], dst_sb[:, col(n)],
                                         ALU.is_equal)

            def scan(h, at, f, messages):
                return dve.tensor_tensor_scan(scanned[:, h, :, at + f], cont[:, :], messages[:, :, f],
                                              scanned[:, 1 - h, CHUNK - 1, at + f:at + f + 1], ALU.mult, ALU.add)

            STEPS = 5
            with dve.Fori(0, PAIRS) as i:
                for h in range(2):
                    n = i * 2 + h

                    def chunk_done(k):
                        dve.wait_ge(chunk_step, i * (2 * STEPS) + (h * STEPS + k))

                    continues(n)
                    dve.tensor_scalar(dst_lo_i[:, :], dst_sb[:, bass.ds(n * CHUNK + 1, CHUNK)], P - 1, None,
                                      ALU.bitwise_and)
                    dve.tensor_scalar(dst_hi_i[:, :], dst_sb[:, bass.ds(n * CHUNK + 1, CHUNK)], P.bit_length() - 1,
                                      None, ALU.logical_shift_right).then_inc(chunk_step, 1)
                    chunk_done(1)
                    dve.tensor_copy(dst_lo[:, :], dst_lo_i[:, :])
                    dve.tensor_copy(dst_hi[:, :], dst_hi_i[:, :]).then_inc(chunk_step, 1)
                    chunk_done(2)
                    dve.wait_ge(he_in[h], i * HE_IN + HE_IN)
                    dve.tensor_tensor(he_dot[:, :, :], he[:, h, :, :],
                                      he_w[:, :].unsqueeze(1).to_broadcast([P, CHUNK, D]), ALU.mult
                                      ).then_inc(chunk_step, 1)
                    chunk_done(3)
                    dve.tensor_reduce(score[:, :], he_dot[:, :, :], AX, ALU.add).then_inc(he_used[h], 1)
                    dve.wait_ge(he_used[h], i + 1)
                    dve.wait_ge(rows0_in[h], i * ROWS_IN + ROWS_IN)
                    index(n + 2, h, t90_sb, RELS, idx0_set)
                    dve.tensor_tensor(score[:, :], score[:, :], rows0[:, h, :, D], ALU.add).then_inc(chunk_step, 1)
                    chunk_done(4)
                    dve.tensor_tensor(weighted[:, :, :], rows0[:, h, :, 0:D],
                                      score[:, :].unsqueeze(2).to_broadcast([P, CHUNK, D]), ALU.mult
                                      ).then_inc(chunk_step, 1)
                    chunk_done(5)
                    dve.wait_ge(scan0_out[h], i * 16)
                    dve.wait_ge(scan0_set[1 - h], i + h)
                    for f in range(D):
                        last = scan(h, D, f, rows0[:, h, :, :])
                    last.then_inc(rows0_used[h], 1)
                    for f in range(D):
                        last = scan(h, 0, f, weighted)
                    last.then_inc(scan0_set[h], 1)
                    for q in range(HOTS):
                        b = (h * HOTS + q) % 2
                        dve.wait_ge(hot_used[b], i * HOTS + (h * HOTS + q) // 2)
                        edges = slice(q * HOT, (q + 1) * HOT)
                        for hot, part, width in ((hot_lo, dst_lo, P), (hot_hi, dst_hi, TILES)):
                            last = dve.tensor_tensor(hot[:, b, :, :],
                                                     part[:, edges].unsqueeze(2).to_broadcast([P, HOT, width]),
                                                     iota_bf[:, 0:width].unsqueeze(1).to_broadcast([P, HOT, width]),
                                                     ALU.is_equal)
                        last.then_inc(hot_set[b], 1)

            def carries(layer, width, all_scanned):
                dve.wait_ge(all_scanned, PAIRS)
                dve.tensor_copy(last_state[:, 0:width], scanned[:, 1, CHUNK - 1, 0:width]).then_inc(carry_step, 1)
                dve.wait_ge(ends_ps, layer + 1)
                dve.tensor_tensor(endsT[0:width, 1:P], ps_misc[0:width, 0:P - 1], take_in[0:width, 1:P], ALU.mult
                                  ).then_inc(carry_step, 1)
                dve.wait_ge(carry_step, 2 + 3 * layer)
                dve.tensor_tensor_scan(carryT[0:width, :], pass_on[0:width, :], endsT[0:width, :], 0.0,
                                       ALU.mult, ALU.add).then_inc(carry_step, 1)
                dve.wait_ge(carry_ps, layer + 1)
                dve.tensor_copy(carry[:, 0:width], ps_misc[:, P:P + width]).then_inc(carry_set, 1)

            carries(0, 2 * D, scan0_set[1])

            dve.wait_ge(hist_ps, 1)
            dve.tensor_copy(degree[:, :], ps_hist[0:TILES, 0:P]).then_inc(node_step, 1)
            dve.wait_ge(node_step, 1)
            dve.tensor_tensor_scan(node_end[:, :], ones[0:TILES, :], degree[:, :], 0.0, ALU.mult, ALU.add
                                   ).then_inc(node_step, 1)
            dve.wait_ge(node_step, 2)
            dve.tensor_scalar(degree[:, :], degree[:, :], 0.0, None, ALU.is_gt).then_inc(node_step, 1)
            dve.wait_ge(offset_ps, 1)
            dve.tensor_scalar(node_end[:, :], node_end[:, :], ps_misc[0:TILES, 2 * P:2 * P + 1], float(-1 - ROWS),
                              ALU.add, ALU.add).then_inc(node_step, 1)
            dve.wait_ge(node_step, 4)
            dve.tensor_tensor(node_end[:, :], node_end[:, :], degree[:, :], ALU.mult).then_inc(node_step, 1)
            dve.wait_ge(node_step, 5)
            dve.tensor_scalar(node_end[:, :], node_end[:, :], float(ROWS), None, ALU.add).then_inc(node_step, 1)
            dve.wait_ge(rows_ps, 1)
            dve.tensor_copy(node_row[:, 0:TILES], ps_misc[:, 3 * P:3 * P + TILES]).then_inc(node_step, 1)
            dve.wait_ge(node_step, 7)

            def group_rows(g, h, done):
                dve.tensor_copy(group_row[:, h, :], node_row[:, tiles(g)]).then_inc(done[h], 1)

            for h in range(2):
                group_rows(h, h, group0_set)

            LN_STEPS = 6

            def layernorm(done, group, result):
                def bc(s):
                    return s.unsqueeze(2).to_broadcast([P, GROUP, D])

                dve.tensor_reduce(stat[:, 0, :], val[:, :, :], AX, ALU.add).then_inc(ln_step, 1)
                done(1)
                dve.tensor_scalar(stat[:, 1, :], stat[:, 0, :], -1.0 / D, None, ALU.mult).then_inc(ln_step, 1)
                done(2)
                dve.tensor_tensor(tmp[:, :, :], val[:, :, :], bc(stat[:, 1, :]), ALU.add).then_inc(ln_step, 1)
                done(3)
                dve.tensor_tensor(val[:, :, :], tmp[:, :, :], tmp[:, :, :], ALU.mult).then_inc(ln_step, 1)
                done(4)
                dve.tensor_reduce(stat[:, 2, :], val[:, :, :], AX, ALU.add).then_inc(ln_step, 1)
                done(5)
                dve.tensor_scalar(stat[:, 3, :], stat[:, 2, :], 1.0 / D, EPS, ALU.mult, ALU.add).then_inc(var_set, 1)
                dve.wait_ge(std_set, group + 1)
                dve.reciprocal(stat[:, 0, :], std[:, :]).then_inc(ln_step, 1)
                done(6)
                return dve.tensor_tensor(result, tmp[:, :, :], bc(stat[:, 0, :]), ALU.mult)

            PER0 = 3 + LN_STEPS
            with dve.Fori(0, GROUPS // 2) as i:
                for h in range(2):
                    g = i * 2 + h

                    def done(k):
                        dve.wait_ge(ln_step, i * (2 * PER0) + (h * PER0 + k))

                    dve.wait_ge(sums0_in[h], i * SUMS_IN + SUMS_IN)
                    group_rows(g + 2, h, group0_set)
                    dve.wait_ge(y_set, g)
                    dve.tensor_tensor(tmp[:, :, :], sums0[:, h, :, D:2 * D],
                                      dst_score[:, tiles(g)].unsqueeze(2).to_broadcast([P, GROUP, D]), ALU.mult
                                      ).then_inc(ln_step, 1)
                    done(1)
                    dve.tensor_tensor(tmp[:, :, :], tmp[:, :, :], sums0[:, h, :, 0:D], ALU.add).then_inc(ln_step, 1)
                    done(2)
                    dve.tensor_tensor(val[:, :, :], tmp[:, :, :], x_sb[:, tiles(g), :], ALU.add).then_inc(ln_step, 1)
                    done(3)
                    layernorm(lambda k: done(3 + k), g, cat[:, h, :, D:2 * D]).then_inc(y_set, 1)

            for h in range(2):
                group_rows(h, h, group1_set)
                index(h, h, t8_sb, TYPES, idx1_set)
                dve.wait_ge(scan0_out[h], 16 * PAIRS)
            with dve.Fori(0, PAIRS) as i:
                for h in range(2):
                    n = i * 2 + h
                    dve.wait_ge(scan1_set[1 - h], i + h)
                    continues(n).then_inc(cont_set, 1)
                    dve.wait_ge(cont_set, n + 1)
                    dve.wait_ge(rows1_in[h], i * ROWS_IN + ROWS_IN)
                    index(n + 2, h, t8_sb, TYPES, idx1_set)
                    dve.wait_ge(scan1_out[h], i * 16)
                    for f in range(D):
                        last = scan(h, 0, f, rows1[:, h, :, :])
                    last.then_inc(scan1_set[h], 1)
            carries(1, D, scan1_set[1])

            PER1 = 5 + LN_STEPS
            dve.wait_ge(state_set, GROUPS)
            with dve.Fori(0, GROUPS // 2) as i:
                for h in range(2):
                    g = i * 2 + h
                    pre = gate_view(h)
                    old = cat[:, h, :, D:2 * D]

                    def done(k):
                        dve.wait_ge(ln_step, i * (2 * PER1) + (GROUPS * PER0 + h * PER1 + k))

                    dve.tensor_copy(old, state[:, tiles(g), :])
                    dve.wait_ge(sums1_in[h], i * SUMS_IN + SUMS_IN)
                    group_rows(g + 2, h, group1_set)
                    dve.tensor_copy(cat[:, h, :, 0:D], sums1[:, h, :, :]).then_inc(m_set, 1)
                    dve.wait_ge(out_set[1 - h], i + h)
                    dve.wait_ge(gates_set, g + 1)
                    dve.tensor_tensor(tmp[:, :, :], pre[:, :, 3 * D:4 * D], gates[:, :, 0:D], ALU.mult
                                      ).then_inc(ln_step, 1)
                    done(1)
                    dve.tensor_tensor(tmp[:, :, :], pre[:, :, 2 * D:3 * D], tmp[:, :, :], ALU.add).then_inc(pre_set, 1)
                    dve.wait_ge(cand_set, g + 1)
                    dve.tensor_tensor(val[:, :, :], old, cand[:, :, :], ALU.subtract).then_inc(ln_step, 1)
                    done(2)
                    dve.tensor_tensor(val[:, :, :], val[:, :, :], gates[:, :, D:2 * D], ALU.mult).then_inc(ln_step, 1)
                    done(3)
                    dve.tensor_tensor(val[:, :, :], val[:, :, :], cand[:, :, :], ALU.add).then_inc(ln_step, 1)
                    done(4)
                    dve.tensor_tensor(val[:, :, :], val[:, :, :], old, ALU.add).then_inc(ln_step, 1)
                    done(5)
                    dve.wait_ge(out_out[h], i * 16)
                    layernorm(lambda k: done(5 + k), g + GROUPS, out_buf[:, h, :, :]).then_inc(out_set[h], 1)


INPUTS = ["x", "src", "dst", "edge_attr_16", "edge_type_8", "edge_type_90", "L0_gnn_Ws", "L0_gnn_Wa",
          "L0_gnn_weight", "L0_gnn_w_comp", "L1_gnn_edge_emb", "L1_gnn_w_ih", "L1_gnn_w_hh", "L1_gnn_b_ih",
          "L1_gnn_b_hh"]


def kernel(**inputs):
    import numpy as np
    import concourse.bacc as bacc
    from concourse.bass_utils import run_bass_kernel_spmd

    nc = bacc.Bacc("TRN2", target_bir_lowering=False, num_devices=1)
    arrays, args = {}, []
    for name in INPUTS:
        a = np.ascontiguousarray(inputs[name])
        arrays[f"in_{name}"] = a
        args.append(nc.dram_tensor(f"in_{name}", a.shape, mybir.dt.from_np(a.dtype), kind="ExternalInput").ap())
    result = nc.dram_tensor("result", inputs["x"].shape, F32, kind="ExternalOutput").ap()
    build(nc, *args, result)
    return run_bass_kernel_spmd(nc, [arrays], core_ids=[0]).results[0]["result"]
```

```python
import concourse.bass as bass
from concourse import mybir
from contextlib import ExitStack

F32 = mybir.dt.float32
I32 = mybir.dt.int32
BF16 = mybir.dt.bfloat16
F16 = mybir.dt.float16
ALU = mybir.AluOpType
ACT = mybir.ActivationFunctionType
AX = mybir.AxisListType.X

P = 128
D = 16
EPS = 1e-5
CHUNK = 62
QUAD, DUO = 4, 2


class Layer:
    def __init__(self, n, quads, by_act, edge_types, kinds, strips, mats, outs, rows):
        self.n, self.by_act, self.edge_types, self.kinds, self.strips = n, by_act, edge_types, kinds, strips
        self.mats, self.outs, self.rows = mats, outs, rows
        self.quads, self.share, self.at = quads, quads * QUAD, CHUNK - quads * QUAD


def build(nc, x, src, dst, edge_attr, type_8, type_90, Ws, Wa, weight, w_comp,
          edge_emb, w_ih, w_hh, b_ih, b_hh, out):
    NODES, EDGES = x.shape[0], src.shape[0]
    RELS, BASES = w_comp.shape
    TYPES = edge_emb.shape[0]
    CHUNKS = -(-EDGES // (P * CHUNK))
    CHUNKS += CHUNKS % 2
    COLS = CHUNKS * CHUNK
    LAST = EDGES - (P - 1) * COLS
    FULL = LAST // CHUNK // 2 * 2
    ROWS = P * COLS
    TILES = -(-NODES // P)
    TAIL = NODES - (TILES - 1) * P
    GROUP = 7
    GROUPS = TILES // GROUP
    REST = 112
    RD = D + 1
    RW = RELS * RD
    BANKS = 3
    BW = RW // BANKS
    HOT = 14
    HOTS = -(-CHUNK // HOT)
    assert TILES % 4 == 2 and 2 * RW <= 2 * CHUNK * 2 * D
    assert TILES % GROUP == 0 and GROUPS % 2 == 0 and CHUNK % 2 == 0 and HOT % 2 == 0 and RW % BANKS == 0 and BW <= 512
    assert 0 < LAST <= COLS and TILES <= P
    PAIRS = CHUNKS // 2
    SUM_BANKS = 7
    SUM_TILES = TILES // SUM_BANKS
    assert TILES % SUM_BANKS == 0 and SUM_TILES * 2 * D <= 512 and TILES * 2 * D <= COLS
    BLOCKS = 8
    BLOCK_TILES = -(-TILES // BLOCKS)
    BLOCK_W = BLOCK_TILES * D
    QUADS = (4, 5)
    assert DUO * BLOCK_W <= 512
    STRIP = 32
    assert TYPES <= STRIP
    LEFT_PARTS = (0, 0, 0, 1, 1, 1, 2, 2)
    RIGHT_PARTS = (0, 1, 2, 0, 1, 2, 0, 1)
    assert len(LEFT_PARTS) * D == P

    ctx = ExitStack()
    with ctx:
        def sb(name, shape, dt=F32):
            return ctx.enter_context(nc.sbuf_tensor(name, shape, dt))

        def ps(name, shape, dt=F32):
            return ctx.enter_context(nc.psum_tensor(name, shape, dt))

        def sem(name):
            return ctx.enter_context(nc.semaphore(name))

        def sems(name):
            return [sem(f"{name}_{h}") for h in range(2)]

        relation_dram = nc.dram_tensor("relation_mats", (D * RELS, D), F32).ap()
        table0 = nc.dram_tensor("relation_table", (TILES * P * RELS, RD), F32).ap()
        table1 = nc.dram_tensor("type_table", (TILES * P * TYPES, D), F32).ap()
        scan0 = nc.dram_tensor("scanned_0", (ROWS + 1, 2 * D), F32).ap()
        scan1 = nc.dram_tensor("scanned_1", (ROWS + 1, D), F32).ap()

        x_sb = sb("x_sb", [P, TILES, D])
        node_parts = sb("node_parts", [P, 3, TILES + 2, D], BF16)
        x_tile = sb("x_tile", [P, 2, len(LEFT_PARTS), D], BF16)
        state = sb("state", [P, TILES, D])
        cat = sb("cat", [P, 2, GROUP, 2 * D])
        src_sb = sb("src_sb", [P, COLS + 2 * CHUNK], I32)
        t90_sb = sb("t90_sb", [P, COLS + 2 * CHUNK], I32)
        t8_sb = sb("t8_sb", [P, COLS + 2 * CHUNK], I32)
        dst_sb = sb("dst_sb", [P, COLS + 1], I32)
        dst_before = sb("dst_before", [P, 1], I32)
        whole = sb("whole", [P, COLS])
        ident = sb("ident", [P, P])
        ident_bf = sb("ident_bf", [P, P], BF16)
        ones = sb("ones", [P, P])
        earlier = sb("earlier", [P, P])
        iota_i = sb("iota_i", [P, P], I32)
        run_start = sb("run_start", [P, 1], I32)
        iota_bf = sb("iota_bf", [P, P, 2], BF16)
        zeros_bf = sb("zeros_bf", [P, P], BF16)
        zero_row = sb("zero_row", [1, 2 * D])
        wcT = sb("wcT", [BASES, RELS])
        basis = sb("basis", [BASES, D * D])
        mats = sb("mats", [RELS, D * D])
        Ws_sb = sb("Ws_sb", [D, D])
        WaT = sb("WaT", [D, 3])
        WaB = sb("WaB", [D, 3, P])
        rel_stack = sb("rel_stack", [P, RW], BF16)
        he_w = sb("he_w", [P, D])
        rel_rows = sb("rel_rows", [RELS, D, RD])
        rel_mats = sb("rel_mats", [RELS, 3, RD, D], BF16)
        emb_sb = sb("emb_sb", [3 * STRIP, D * D])
        type_mats = sb("type_mats", [3 * STRIP, D * D], BF16)
        ident_f16 = sb("ident_f16", [P, P], F16)
        less_key = sb("less_key", [P, BLOCKS])
        type_i = sb("type_i", [P, 1], I32)
        less_type = sb("less_type", [P, 2])
        match_i = sb("match_i", [P, 2, max(QUADS) * QUAD], I32)
        match_cols = sb("match_cols", [P, 2, max(QUADS) * QUAD], F16)
        hot_tile = sb("hot_tile", [P, 2, max(QUADS) * QUAD, BLOCK_TILES])
        hot_key = sb("hot_key", [P, 2, BLOCKS, QUAD * P], BF16)
        hot_type = sb("hot_type", [P, 2, QUAD * P], BF16)
        rel_parts = hot_key[0:D, :, :, :].rearrange("p h g e -> p (h g e)")[:, 0:3 * RW].rearrange(
            "p (k c) -> p k c", k=3)
        picked = sb("picked", [P, DUO, BLOCK_TILES, D])
        source = sb("source", [P, DUO, D])
        by_in = sb("by_in", [P, DUO, RD, D])
        dst_w = sb("dst_w", [P, D])
        dst_score = sb("dst_score", [P, TILES])
        type_w = sb("type_w", [D, TYPES, D])
        gate_w = sb("gate_w", [2 * D + 2, 4 * D])
        xT = sb("xT", [P, 2, P], BF16)
        t0_buf = sb("t0_buf", [P, 2, RW])
        idx = sb("idx", [P, 2, CHUNK], I32)
        he = sb("he", [P, 2, CHUNK, D])
        rows0 = sb("rows0", [P, 2, CHUNK, RD])
        rel_w = rows0[0:D, :, :, :].rearrange("p h c f -> p (h c f)")[:, 0:RW].rearrange("p (r f) -> p r f", f=RD)
        rows1 = rows0[:, :, :, 0:D]
        he_dot = sb("he_dot", [P, CHUNK, D])
        score = sb("score", [P, CHUNK])
        weighted = he_dot
        cont = sb("cont", [P, CHUNK])
        scanned = sb("scanned", [P, 2, CHUNK, 2 * D])
        t0_tiles = [t0_buf[:, 0, :], t0_buf[:, 1, :]] + [
            scanned[:, :, :, :].rearrange("p h c f -> p (h c f)")[:, k * RW:(k + 1) * RW] for k in range(2)]
        dst_lo_i = sb("dst_lo_i", [P, CHUNK], I32)
        dst_hi_i = sb("dst_hi_i", [P, CHUNK], I32)
        dst_lo = sb("dst_lo", [P, CHUNK], BF16)
        dst_hi = sb("dst_hi", [P, CHUNK], BF16)
        hot_lo = sb("hot_lo", [P, 2, HOT // 2, P, 2], BF16)
        hot_hi = sb("hot_hi", [P, 2, HOT // 2, TILES, 2], BF16)
        ordered = sb("ordered", [P, 4])
        disorder = sb("disorder", [1, 1], I32)
        edge_row = sb("edge_row", [P, 2 * D])
        edge_part_i = sb("edge_part_i", [P, 2], I32)
        edge_part = sb("edge_part", [P, 2])
        edge_lo = sb("edge_lo", [P, P])
        edge_hi = sb("edge_hi", [P, TILES])
        node_id = sb("node_id", [P, TILES], I32)
        first = sb("first", [P, 4])
        flag_cols = sb("flag_cols", [P, 2, 2 * D])
        fix_row = sb("fix_row", [P, 1], I32)
        pass_on = sb("pass_on", [2 * D, P])
        take_in = sb("take_in", [2 * D, P])
        endsT = sb("endsT", [2 * D, P])
        carryT = sb("carryT", [2 * D, P])
        carry = sb("carry", [P, 2 * D])
        last_state = sb("last_state", [P, 2 * D])
        degree = sb("degree", [TILES, P])
        node_end = sb("node_end", [TILES, P])
        node_row = sb("node_row", [P, TILES + 2 * GROUP], I32)
        group_row = sb("group_row", [P, 2, GROUP], I32)
        sums0 = sb("sums0", [P, 2, GROUP, 2 * D])
        sums1 = sb("sums1", [P, 2, GROUP, D])
        val = sb("val", [P, GROUP, D])
        tmp = sb("tmp", [P, GROUP, D])
        stat = sb("stat", [P, 4, GROUP])
        std = sb("std", [P, GROUP])
        catT = sb("catT", [2 * D + 2, GROUP * P])
        t1_buf = t0_buf[:, :, 0:GROUP * TYPES * D]
        gates = sb("gates", [P, GROUP, 2 * D])
        cand = sb("cand", [P, GROUP, D])
        out_buf = sb("out_buf", [P, 2, GROUP, D])

        ps_table = [ps(f"ps_table_{h}", [P, BANKS, 512]) for h in range(2)]
        ps_misc = ps("ps_misc", [P, 512])
        ps_hist = ps("ps_hist", [P, 512])

        def gate_view(h):
            return ps_table[h][:, 0, 0:GROUP * 4 * D].rearrange("p (t g) -> p t g", g=4 * D)

        pads_set = sem("pads_set")
        consts_set = sem("consts_set")
        weights_in, x_in, edges_in, late_in = sem("weights_in"), sem("x_in"), sem("edges_in"), sem("late_in")
        wab_set, mats_ps, mats_sb, mats_out = sem("wab_set"), sem("mats_ps"), sem("mats_sb"), sem("mats_out")
        rel_in, scores_ps = sem("rel_in"), sem("scores_ps")
        prep = sem("prep")
        flags_set, flags_ps = sem("flags_set"), sem("flags_ps")
        x_parts_set, x_tile_set, rel_parts_set = sem("x_parts_set"), sem("x_tile_set"), sem("rel_parts_set")
        stack_in = sem("stack_in")
        order_set, order_ps, order_flag = sem("order_set"), sem("order_ps"), sem("order_flag")
        xT_ps, xT_sb, t0_ps = sem("xT_ps"), sem("xT_sb"), sem("t0_ps")
        t0_sb = sem("t0_sb")
        t0_out = [sem(f"t0_out_{k}") for k in range(4)]
        idx0_set, rows0_in, rows0_used = sems("idx0_set"), sems("rows0_in"), sems("rows0_used")
        he_in, he_used = sems("he_in"), sems("he_used")
        chunk_step = sem("chunk_step")
        scan0_set, scan0_out = sems("scan0_set"), sems("scan0_out")
        hot_set, hot_used, hist_ps = sems("hot_set"), sems("hot_used"), sem("hist_ps")
        node_step, offset_ps, rows_ps = sem("node_step"), sem("offset_ps"), sem("rows_ps")
        carry_step = sem("carry_step")
        ends_ps, carry_ps, carry_set, fixed = sem("ends_ps"), sem("carry_ps"), sem("carry_set"), sem("fixed")
        gather_begun = sem("gather_begun")
        group0_set, sums0_in, sums0_used = sems("group0_set"), sems("sums0_in"), sem("sums0_used")
        ln_step = sem("ln_step")
        var_set, std_set, y_set = sem("var_set"), sem("std_set"), sem("y_set")
        state_set = sem("state_set")
        yT_ps, yT_sb, t1_ps, t1_sb, t1_out = sem("yT_ps"), sem("yT_sb"), sem("t1_ps"), sem("t1_sb"), sems("t1_out")
        idx1_set, rows1_in, cont_set = sems("idx1_set"), sems("rows1_in"), sem("cont_set")
        scan1_set, scan1_out = sems("scan1_set"), sems("scan1_out")
        group1_set, sums1_in = sems("group1_set"), sems("sums1_in")
        m_set, mT_ps, mT_sb = sem("m_set"), sem("mT_ps"), sem("mT_sb")
        gates_ps, gates_set, pre_set, cand_set = sem("gates_ps"), sem("gates_set"), sem("pre_set"), sem("cand_set")
        product_mats_set, node_parts_set = sems("product_mats_set"), sem("node_parts_set")
        match_step = sems("match_step")
        keys_set, match_ps, match_sb, match_set = sems("keys_set"), sems("match_ps"), sems("match_sb"), sems("match_set")
        match_rest = sem("match_rest")
        products_ps, products_used, rows_made = sems("products_ps"), sems("products_used"), sems("rows_made")
        edge_in, edge_step, spread_set = sem("edge_in"), sem("edge_step"), sem("spread_set")
        summed, sums_sb, sums_out = sem("summed"), sem("sums_sb"), sem("sums_out")
        out_set, out_out = sems("out_set"), sems("out_out")

        block = ctx.enter_context(nc.Block())

        def wait_past(eng, signal, value):
            if not (isinstance(value, int) and value <= 0):
                eng.wait_ge(signal, value)

        def col(n):
            return bass.ds(n * CHUNK, CHUNK)

        def tiles(g):
            return bass.ds(g * GROUP, GROUP)

        def edge_views(a):
            tail = " f" if len(a.shape) == 2 else ""
            body = a[0:(P - 1) * COLS].rearrange(f"(p c){tail} -> p c{tail}", c=COLS)
            last = a[(P - 1) * COLS:EDGES].rearrange(f"(p c){tail} -> p c{tail}", p=1)
            return body, last

        he_body, he_last = edge_views(edge_attr)
        scan0_v = scan0[0:ROWS, :].rearrange("(p c) f -> p c f", c=COLS)
        scan1_v = scan1[0:ROWS, :].rearrange("(p c) f -> p c f", c=COLS)
        table0_v = table0.rearrange("(t p r) f -> p t (r f)", p=P, r=RELS)
        table1_v = table1.rearrange("(t p r) f -> p t (r f)", p=P, r=TYPES)
        out_v = out[0:(TILES - 1) * P, :].rearrange("(t p) f -> p t f", p=P)
        type_cols = type_w[:, :, :].rearrange("h t m -> h (t m)")
        xT_bank = [b[:, 0:P // 2].bitcast(BF16) for b in (ps_misc, ps_hist)]
        score_ps = ps_table[1][:, 0, :]
        match_bank = ps_misc[:, :].bitcast(F16).rearrange("p (k e) -> p k e", k=2)
        sum_banks = [ps_table[h][:, b, :] for h in range(2) for b in range(BANKS)] + [ps_misc[:, :]]

        def out_of_order(eng):
            eng.wait_ge(order_flag, 1)
            return eng.If(eng.value_load(disorder[0:1, 0:1], min_val=0, max_val=1))

        COUNT_WITH = ((0,), (1,), (2,), (3, 4))
        assert sum(map(len, COUNT_WITH)) == HOTS and len(COUNT_WITH) == QUADS[0]
        WEIGHTS_IN, X_IN, EDGES_IN, LATE_IN, HE_IN = 4 * 16, 2 * 16, 13 * 16, 14 * 16, 3 * 16
        SUMS_IN = 16 * GROUP

        layers = [
            Layer(0, QUADS[0], BLOCKS, t90_sb, RELS, RELS,
                  [rel_mats[:, k, :, :].rearrange("r o i -> r (o i)") for k in range(3)], RD, rows0),
            Layer(1, QUADS[1], BLOCKS - 2, t8_sb, TYPES, 3 * STRIP, [type_mats[:, :]], D, rows1),
        ]

        @block.sync
        def _(sp):
            with nc.allow_non_contiguous_dma(reason="small weights, transposed once"):
                sp.dma_start(wcT[:, :], w_comp.rearrange("r b -> b r")).then_inc(weights_in, 16)
                sp.dma_start(basis[:, :].rearrange("b (i o) -> b i o", o=D),
                             weight.rearrange("b i o -> (b i o)").rearrange("(i b o) -> b i o", i=D, b=BASES)
                             ).then_inc(weights_in, 16)
                sp.dma_start(Ws_sb[:, :], Ws).then_inc(weights_in, 16)
                sp.dma_start(WaT[:, :], Wa.rearrange("a (k o) -> o (a k)", o=D)).then_inc(weights_in, 16)
                sp.dma_start(x_sb[:, 0:TILES - 1, :],
                             x[0:(TILES - 1) * P, :].rearrange("(t p) f -> p t f", p=P)).then_inc(x_in, 16)
                sp.wait_ge(pads_set, 1)
                sp.dma_start(x_sb[0:TAIL, TILES - 1, :], x[(TILES - 1) * P:NODES, :]).then_inc(x_in, 16)
                sp.wait_ge(mats_sb, 1)
                sp.dma_start(relation_dram.rearrange("(i r) o -> r i o", r=RELS),
                             mats[:, :].rearrange("r (i o) -> r i o", o=D)).then_inc(mats_out, 16)
                sp.wait_ge(mats_out, 16)
                sp.dma_start(rel_w[:, :, 0:D], relation_dram.rearrange("(r i) o -> i r o", i=D)).then_inc(rel_in, 16)
                sp.dma_start(rel_rows[:, :, 0:D], relation_dram.rearrange("(r i) o -> r i o", i=D)).then_inc(rel_in, 16)
                sp.wait_ge(rel_parts_set, 1)
                for k in range(0, len(RIGHT_PARTS), 2):
                    sp.dma_start(rel_stack[k * D:(k + 1) * D, :], rel_parts[:, RIGHT_PARTS[k], :]).then_inc(stack_in, 16)

            def store_tile(t, k):
                sp.wait_ge(t0_sb, t + 1)
                sp.dma_start(table0_v[:, bass.ds(t, 1), :], t0_tiles[k].unsqueeze(1)).then_inc(t0_out[k], 16)

            for k in range(2):
                store_tile(k, k + 2)
            with sp.Fori(0, TILES // 4) as i:
                for k in range(4):
                    store_tile(i * 4 + (k + 2), k)

            with nc.allow_non_contiguous_dma(reason="small weights, transposed once"):
                for k in range(3):
                    sp.dma_start(emb_sb[k * STRIP:k * STRIP + TYPES, :], edge_emb).then_inc(late_in, 16)
                sp.dma_start(type_w[:, :, :], edge_emb.rearrange("t (m h) -> h t m", h=D)).then_inc(late_in, 16)
                for w, row, own in ((w_ih, 0, 2 * D), (w_hh, D, 3 * D)):
                    sp.dma_start(gate_w[row:row + D, 0:2 * D], w[0:2 * D, :].rearrange("g i -> i g")
                                 ).then_inc(late_in, 16)
                    sp.dma_start(gate_w[row:row + D, own:own + D], w[2 * D:3 * D, :].rearrange("g i -> i g")
                                 ).then_inc(late_in, 16)
                for b, row, own in ((b_ih, 2 * D, 2 * D), (b_hh, 2 * D + 1, 3 * D)):
                    b = b.rearrange("(a g) -> a g", a=1)
                    sp.dma_start(gate_w[row:row + 1, 0:2 * D], b[:, 0:2 * D]).then_inc(late_in, 16)
                    sp.dma_start(gate_w[row:row + 1, own:own + D], b[:, 2 * D:3 * D]).then_inc(late_in, 16)
                sp.dma_start(scan0[ROWS:ROWS + 1, :], zero_row[:, :]).then_inc(late_in, 16)
                sp.dma_start(scan1[ROWS:ROWS + 1, :], zero_row[:, 0:D]).then_inc(late_in, 16)

            def load_he(n, h):
                sp.dma_start(he[0:REST, h, :, :], he_body[0:REST, col(n), :]).then_inc(he_in[h], 16)
                sp.dma_start(he[REST:P - 1, h, :, :], he_body[REST:P - 1, col(n), :]).then_inc(he_in[h], 16)

            def pair(i):
                for h in range(2):
                    wait_past(sp, he_used[h], i)
                    load_he(i * 2 + h, h)
                    sp.dma_start(he[P - 1:P, h, :, :], he_last[:, col(i * 2 + h), :]).then_inc(he_in[h], 16)

            pair(0)
            with sp.Fori(1, FULL // 2) as i:
                pair(i)
            for n in range(FULL, CHUNKS):
                h = n % 2
                sp.wait_ge(he_used[h], n // 2)
                load_he(n, h)
                left = min(CHUNK, max(LAST - n * CHUNK, 1))
                at = min(n * CHUNK, LAST - left)
                sp.dma_start(he[P - 1:P, h, 0:left, :], he_last[:, at:at + left, :]).then_inc(he_in[h], 16)

            def sum_edges(layer, scan, width):
                rows = scan[0:ROWS, :].rearrange("(p c) f -> p c f", c=COLS)

                def load(c):
                    wait_past(sp, spread_set, c + layer * COLS)
                    sp.dma_start(edge_row[:, 0:width].unsqueeze(1), rows[:, bass.ds(c, 1), :]).then_inc(edge_in, 16)

                with out_of_order(sp):
                    sp.wait_ge(fixed, 16 * (layer + 1))
                    load(0)
                    with sp.Fori(1, COLS) as c:
                        load(c)
                    sp.wait_ge(sums_sb, layer + 1)
                    sp.dma_start(scan[0:TILES * P, :].rearrange("(t p) f -> p t f", p=P),
                                 whole[:, 0:TILES * width].rearrange("p (t f) -> p t f", f=width)
                                 ).then_inc(sums_out, 16)

            sum_edges(0, scan0, 2 * D)

            def pair(i):
                for h in range(2):
                    sp.wait_ge(t1_sb, i * 2 + h + 1)
                    sp.dma_start(table1_v[:, tiles(i * 2 + h), :],
                                 t1_buf[:, h, :].rearrange("p (t f) -> p t f", t=GROUP)).then_inc(t1_out[h], 16)

            pair(0)
            with sp.Fori(1, GROUPS // 2) as i:
                pair(i)

            sum_edges(1, scan1, D)

            def pair(i):
                for h in range(2):
                    sp.wait_ge(out_set[h], i + 1)
                    sp.dma_start(out_v[:, tiles(i * 2 + h), :], out_buf[:, h, :, :]).then_inc(out_out[h], 16)

            pair(0)
            with sp.Fori(1, GROUPS // 2 - 1) as i:
                pair(i)
            sp.wait_ge(out_set[0], GROUPS // 2)
            sp.dma_start(out_v[:, tiles(GROUPS - 2), :], out_buf[:, 0, :, :]).then_inc(out_out[0], 16)
            sp.wait_ge(out_set[1], GROUPS // 2)
            sp.dma_start(out_v[:, TILES - GROUP:TILES - 1, :], out_buf[:, 1, 0:GROUP - 1, :]).then_inc(out_out[1], 16)
            sp.dma_start(out[(TILES - 1) * P:NODES, :], out_buf[0:TAIL, 1, GROUP - 1, :]).then_inc(out_out[1], 16)
            sp.wait_ge(out_out[0], 16 * (GROUPS // 2))
            sp.wait_ge(out_out[1], 16 * (GROUPS // 2 + 1))

        @block.gpsimd
        def _(pool):
            pool.memset(ident[:, :], 0.0)
            pool.memset(earlier[:, :], 1.0).then_inc(consts_set, 1)
            pool.wait_ge(consts_set, 1)
            pool.affine_select(out=ident[:, :], in_=ident[:, :], compare_op=ALU.not_equal, fill=1.0, base=0,
                               pattern=[[-1, P]], channel_multiplier=1)
            pool.affine_select(out=earlier[:, :], in_=earlier[:, :], compare_op=ALU.is_gt, fill=0.0, base=0,
                               pattern=[[1, P]], channel_multiplier=-1)
            pool.iota(less_key[:, :], pattern=[[-P, BLOCKS]], base=0, channel_multiplier=-1,
                      allow_small_or_imprecise_dtypes=True)
            pool.iota(node_id[:, :], pattern=[[P, TILES]], base=0, channel_multiplier=1)
            pool.iota(run_start[:, :], pattern=[[1, 1]], base=-1, channel_multiplier=COLS)
            pool.iota(iota_i[:, :], pattern=[[1, P]], base=0, channel_multiplier=0).then_inc(consts_set, 1)

            def stack_tile(t, h):
                for part in range(3):
                    at, count = LEFT_PARTS.index(part), LEFT_PARTS.count(part)
                    last = pool.tensor_copy(x_tile[:, h, at:at + count, :],
                                            node_parts[:, part, bass.ds(t, 1), :].to_broadcast([P, count, D]))
                last.then_inc(x_tile_set, 1)

            pool.wait_ge(x_parts_set, 1)
            for h in range(2):
                stack_tile(h, h)

            def pair(i):
                for h in range(2):
                    pool.wait_ge(xT_ps, i * 2 + h + 1)
                    stack_tile(i * 2 + h + 2, h)

            pair(0)
            with pool.Fori(1, TILES // 2) as i:
                pair(i)

            def gather(rows, table, index, width, landed):
                pool.sem_inc(gather_begun, 1)
                for k in range(width):
                    pool.indirect_dma_start(out=rows[:, k, :], out_offset=None, in_=table,
                                            in_offset=bass.IndirectOffsetOnAxis(ap=index[:, k:k + 1], axis=0)
                                            ).then_inc(landed, 16)

            def add_carries(layer, scan, scan_out, width):
                for h in range(2):
                    pool.wait_ge(scan_out[h], 16 * PAIRS)
                pool.wait_ge(carry_set, layer + 1)
                pool.indirect_dma_start(out=scan, out_offset=bass.IndirectOffsetOnAxis(ap=fix_row[:, 0:1], axis=0),
                                        in_=carry[:, 0:width], in_offset=None, compute_op=ALU.add
                                        ).then_inc(fixed, 16)
                with out_of_order(pool):
                    pool.wait_ge(sums_out, 16 * (layer + 1))

            def pair(i):
                for h in range(2):
                    pool.wait_ge(idx0_set[h], i + 1)
                    wait_past(pool, rows0_used[h], i)
                    for k in range(4):
                        pool.wait_ge(t0_out[k], 16 * (TILES // 4 + (k >= 2)))
                    gather(rows0[:, h, :, :], table0, idx[:, h, :], layers[0].at, rows0_in[h])

            pair(0)
            with pool.Fori(1, PAIRS) as i:
                pair(i)
            add_carries(0, scan0, scan0_out, 2 * D)
            pool.wait_ge(late_in, LATE_IN)
            def pair(i):
                for h in range(2):
                    pool.wait_ge(group0_set[h], i + 1)
                    wait_past(pool, sums0_used, i * 2 + (h - 1))
                    pool.wait_ge(fixed, 16)
                    gather(sums0[:, h, :, :], scan0, group_row[:, h, :], GROUP, sums0_in[h])

            pair(0)
            with pool.Fori(1, GROUPS // 2) as i:
                pair(i)

            def pair(i):
                for h in range(2):
                    pool.wait_ge(idx1_set[h], i + 1)
                    wait_past(pool, scan1_set[h], i)
                    for half in range(2):
                        pool.wait_ge(t1_out[half], 16 * (GROUPS // 2))
                    gather(rows1[:, h, :, :], table1, idx[:, h, :], layers[1].at, rows1_in[h])

            pair(0)
            with pool.Fori(1, PAIRS) as i:
                pair(i)
            add_carries(1, scan1, scan1_out, D)
            def pair(i):
                for h in range(2):
                    pool.wait_ge(group1_set[h], i + 1)
                    wait_past(pool, m_set, i * 2 + (h - 1))
                    pool.wait_ge(fixed, 32)
                    gather(sums1[:, h, :, :], scan1, group_row[:, h, :], GROUP, sums1_in[h])

            pair(0)
            with pool.Fori(1, GROUPS // 2) as i:
                pair(i)

        @block.tensor
        def _(pe):
            pe.wait_ge(weights_in, WEIGHTS_IN)
            pe.matmul(ps_misc[0:RELS, 0:D * D], wcT[:, :], basis[:, :], start=True, stop=True).then_inc(mats_ps, 1)
            pe.wait_ge(wab_set, 1)
            pe.matmul(score_ps[0:D, 0:1], Ws_sb[:, :], WaT[:, 0:1], start=True, stop=True)
            for k in range(3):
                last = pe.matmul(score_ps[:, (k + 1) * D:(k + 2) * D], WaB[:, k, :], Ws_sb[:, :], start=True, stop=True)
            last.then_inc(scores_ps, 1)

            def transpose_x(t, h):
                pe.wait_ge(x_tile_set, t + 1)
                pe.transpose(xT_bank[h], x_tile[:, h, :, :].rearrange("p k f -> p (k f)"), ident_bf[:, :]
                             ).then_inc(xT_ps, 1)

            pe.wait_ge(x_parts_set, 1)
            pe.wait_ge(mats_sb, 1)
            transpose_x(0, 0)
            pe.wait_ge(stack_in, 16 * len(RIGHT_PARTS))
            def pair(i):
                for h in range(2):
                    wait_past(pe, xT_sb, i * 2 + h)
                    transpose_x(i * 2 + h + 1, 1 - h)
                    pe.wait_ge(xT_sb, i * 2 + h + 1)
                    wait_past(pe, t0_sb, i * 2 + (h - 1))
                    for b in range(BANKS):
                        last = pe.matmul(ps_table[h][:, b, 0:BW], xT[:, h, :], rel_stack[:, b * BW:(b + 1) * BW],
                                         start=True, stop=True)
                    last.then_inc(t0_ps, 1)

            pair(0)
            with pe.Fori(1, TILES // 2) as i:
                pair(i)

            pe.wait_ge(order_set, 1)
            pe.wait_ge(xT_sb, TILES + 1)
            pe.matmul(ps_misc[:, 3 * P:3 * P + 1], ones[:, :], ordered[:, 0:1], start=True, stop=True
                      ).then_inc(order_ps, 1)
            pe.wait_ge(flags_set, 1)
            for k in range(2):
                last = pe.matmul(ps_misc[0:2 * D, k * P:(k + 1) * P], flag_cols[:, k, :], ident[:, :],
                                 start=True, stop=True)
            last.then_inc(flags_ps, 1)

            pe.matmul(ps_hist[0:TILES, 0:P], zeros_bf[:, 0:TILES], zeros_bf[:, :], start=True, stop=False)

            def count_edges(i, q):
                pe.wait_ge(hot_set[q % 2], i * HOTS + q // 2 + 1)
                for k in range(min(HOT, CHUNK - q % HOTS * HOT)):
                    last = pe.matmul(ps_hist[0:TILES, 0:P], hot_hi[:, q % 2, k // 2, :, k % 2],
                                     hot_lo[:, q % 2, k // 2, :, k % 2],
                                     start=False, stop=False)
                last.then_inc(hot_used[q % 2], 1)

            def spread_quad(lay, m, quad, q):
                pe.wait_ge(keys_set[lay.n], m + 1)
                wait_past(pe, match_sb[lay.n], quad)
                for k in range(2):
                    for c in range(QUAD):
                        at = q * QUAD + c
                        last = pe.transpose(match_bank[:, k, c * P:(c + 1) * P],
                                            match_cols[:, k, at:at + 1].to_broadcast([P, P]), ident_f16[:, :])
                last.then_inc(match_ps[lay.n], 1)

            def products(lay, quad, b, duo):
                pe.wait_ge(match_set[lay.n], quad + 1)
                if lay.by_act < BLOCKS:
                    pe.wait_ge(match_rest, quad + 1)
                wait_past(pe, products_used[lay.n], quad * 2 + (duo - 1))
                if isinstance(quad, int) and quad == 0:
                    pe.wait_ge(product_mats_set[lay.n], 1)
                for t in range(DUO):
                    edges = slice((duo * DUO + t) * P, (duo * DUO + t + 1) * P)
                    for g in range(BLOCKS):
                        width = len(range(g, TILES, BLOCKS)) * D
                        for part in range(3):
                            pe.matmul(ps_table[duo][:, 0, t * BLOCK_W:t * BLOCK_W + width], hot_key[:, b, g, edges],
                                      node_parts[:, part, g:TILES:BLOCKS, :],
                                      start=(g == 0 and part == 0), stop=(g == BLOCKS - 1 and part == 2))
                    for k, mats_part in enumerate(lay.mats):
                        last = pe.matmul(ps_table[duo][:, 1 + t, 0:lay.outs * D], hot_type[0:lay.strips, b, edges],
                                         mats_part, start=(k == 0), stop=(k == len(lay.mats) - 1))
                last.then_inc(products_ps[lay.n], 1)

            def chunk_by_products(lay, m, parity, last, between=lambda q: None):
                for q in range(lay.quads):
                    quad = m * lay.quads + q
                    if q + 1 < lay.quads:
                        spread_quad(lay, m, quad + 1, q + 1)
                    elif not last:
                        spread_quad(lay, m + 1, quad + 1, 0)
                    for duo in range(QUAD // DUO):
                        products(lay, quad, (parity * lay.quads + q) % 2, duo)
                    between(q)

            spread_quad(layers[0], 0, 0, 0)
            chunk_by_products(layers[0], 0, 0, False)

            def pair(i, last=False):
                for h in range(2):
                    def counts(q):
                        for k in COUNT_WITH[q]:
                            count_edges(i, h * HOTS + k)

                    if last and h == 1:
                        for k in range(HOTS):
                            count_edges(i, h * HOTS + k)
                    else:
                        chunk_by_products(layers[0], i * 2 + (h + 1), (h + 1) % 2, last, counts)

            pair(0)
            with pe.Fori(1, PAIRS - 1) as i:
                pair(i)
            pair(PAIRS - 1, True)
            pe.matmul(ps_hist[0:TILES, 0:P], zeros_bf[:, 0:TILES], zeros_bf[:, :], start=False, stop=True
                      ).then_inc(hist_ps, 1)

            def carries(layer, width):
                pe.wait_ge(carry_step, 1 + 3 * layer)
                pe.transpose(ps_misc[0:width, 0:P], last_state[:, 0:width], ident[:, :]).then_inc(ends_ps, 1)
                pe.wait_ge(carry_step, 3 + 3 * layer)
                pe.transpose(ps_misc[:, P:P + width], carryT[0:width, :], ident[0:width, 0:width]).then_inc(carry_ps, 1)

            carries(0, 2 * D)

            pe.wait_ge(node_step, 2)
            pe.matmul(ps_misc[0:TILES, 2 * P:2 * P + 1], earlier[0:TILES, 0:TILES], node_end[:, P - 1:P],
                      start=True, stop=True).then_inc(offset_ps, 1)
            pe.wait_ge(node_step, 6)
            pe.transpose(ps_misc[:, 3 * P:3 * P + TILES], node_end[:, :], ident[0:TILES, 0:TILES]).then_inc(rows_ps, 1)

            def sum_edges(layer, width):
                def add(c):
                    pe.wait_ge(spread_set, c + (layer * COLS + 1))
                    for b, bank in enumerate(sum_banks):
                        cols = SUM_TILES * width
                        last = pe.matmul(bank[:, 0:cols], edge_lo[:, :], whole[:, b * cols:(b + 1) * cols],
                                         start=isinstance(c, int) and c == 0, stop=isinstance(c, int) and c == COLS - 1)
                    last.then_inc(summed, 1)

                with out_of_order(pe):
                    add(0)
                    with pe.Fori(1, COLS - 1) as c:
                        add(c)
                    add(COLS - 1)

            sum_edges(0, 2 * D)

            def turn(h, lo, hi):
                for k in range(GROUP):
                    bank = ps_misc if k < 4 else ps_hist
                    last = pe.transpose(bank[0:hi - lo, (k % 4) * P:(k % 4 + 1) * P],
                                        cat[:, h, k, lo:hi], ident[:, :])
                return last

            pe.wait_ge(late_in, LATE_IN)
            def pair(i):
                for h in range(2):
                    pe.wait_ge(y_set, i * 2 + h + 1)
                    turn(h, D, 2 * D).then_inc(yT_ps, 1)
                    pe.wait_ge(yT_sb, i * 2 + h + 1)
                    wait_past(pe, t1_sb, i * 2 + h)
                    for k in range(GROUP):
                        last = pe.matmul(ps_table[h][:, k // 4, (k % 4) * P:(k % 4 + 1) * P],
                                         catT[0:D, k * P:(k + 1) * P], type_cols, start=True, stop=True)
                    last.then_inc(t1_ps, 1)

            pair(0)
            with pe.Fori(1, GROUPS // 2) as i:
                pair(i)

            spread_quad(layers[1], 0, 0, 0)
            chunk_by_products(layers[1], 0, 0, False)

            def pair(i, last=False):
                for h in range(2):
                    if not (last and h == 1):
                        chunk_by_products(layers[1], i * 2 + (h + 1), (h + 1) % 2, last)

            pair(0)
            with pe.Fori(1, PAIRS - 1) as i:
                pair(i)
            pair(PAIRS - 1, True)

            carries(1, D)
            sum_edges(1, D)

            def pair(i):
                for h in range(2):
                    pe.wait_ge(m_set, i * 2 + h + 1)
                    turn(h, 0, 2 * D).then_inc(mT_ps, 1)
                    pe.wait_ge(mT_sb, i * 2 + h + 1)
                    wait_past(pe, pre_set, i * 2 + h)
                    for k in range(GROUP):
                        last = pe.matmul(ps_table[h][:, 0, k * 4 * D:(k + 1) * 4 * D],
                                         catT[:, k * P:(k + 1) * P], gate_w[:, :], start=True, stop=True)
                    last.then_inc(gates_ps, 1)

            pair(0)
            with pe.Fori(1, GROUPS // 2) as i:
                pair(i)

        @block.scalar
        def _(act):
            with nc.allow_non_contiguous_dma(reason="one column"):
                act.wait_ge(pads_set, 1)
                act.wait_ge(rel_in, 32)
                for a, to, at in ((src, src_sb, 0), (type_90, t90_sb, 0), (dst, dst_sb, 1), (type_8, t8_sb, 0)):
                    body, last = edge_views(a)
                    act.dma_start(to[0:REST, at:at + COLS], body[0:REST, :]).then_inc(edges_in, 16)
                    act.dma_start(to[REST:P - 1, at:at + COLS], body[REST:P - 1, :]).then_inc(edges_in, 16)
                    act.dma_start(to[P - 1:P, at:at + LAST], last).then_inc(edges_in, 16)
                act.dma_start(dst_before[1:P, :], edge_views(dst)[0][:, COLS - 1:COLS]).then_inc(edges_in, 16)

            act.wait_ge(rel_parts_set, 1)
            for k in range(1, len(RIGHT_PARTS), 2):
                act.dma_start(rel_stack[k * D:(k + 1) * D, :], rel_parts[:, RIGHT_PARTS[k], :]).then_inc(stack_in, 16)

            act.wait_ge(xT_ps, 1)
            act.copy(xT[:, 0, :], xT_bank[0]).then_inc(xT_sb, 1)

            def table_tile(t, h, k, stored):
                act.wait_ge(xT_ps, t + 2)
                act.copy(xT[:, 1 - h, :], xT_bank[1 - h]).then_inc(xT_sb, 1)
                act.wait_ge(t0_ps, t + 1)
                wait_past(act, t0_out[k], stored * 16)
                act.copy(t0_tiles[k].rearrange("p (b c) -> p b c", b=BANKS), ps_table[h][:, :, 0:BW]).then_inc(t0_sb, 1)

            def four(i):
                for k in range(4):
                    table_tile(i * 4 + (k + 2), k % 2, k, i + (k >= 2))

            for k in range(2):
                table_tile(k, k, k + 2, 0)
            four(0)
            with act.Fori(1, TILES // 4) as i:
                four(i)

            def one_hot(lay, quad, b):
                act.wait_ge(match_ps[lay.n], quad + 1)
                wait_past(act, products_ps[lay.n], quad * 2 - 2)
                for g in range(BLOCKS):
                    act.activation(hot_key[:, b, g, :], match_bank[:, 0, :], ACT.Abs, bias=less_key[:, g:g + 1])
                own = slice(0, lay.strips)
                act.activation(hot_type[own, b, :], match_bank[own, 1, :], ACT.Abs, bias=less_type[own, lay.n:lay.n + 1]
                               ).then_inc(match_sb[lay.n], 1)
                act.wait_ge(match_sb[lay.n], quad + 1)
                mine = slice(0, lay.by_act)
                last = act.activation(hot_key[:, b, mine, :], hot_key[:, b, mine, :], ACT.Relu, bias=ones[:, 0:1],
                                      scale=-1.0)
                if lay.by_act == BLOCKS:
                    last = act.activation(hot_type[own, b, :], hot_type[own, b, :], ACT.Relu, bias=ones[own, 0:1],
                                          scale=-1.0)
                last.then_inc(match_set[lay.n], 1)

            def chunks_out(lay, stored, scan_set, scan_out):
                for q in range(lay.quads + 1):
                    one_hot(lay, q, q % 2)

                def pair(i, last=False):
                    for h in range(2):
                        m = i * 2 + (h + 1)
                        if not (last and h == 1):
                            for q in range(1, lay.quads):
                                one_hot(lay, m * lay.quads + q, ((h + 1) * lay.quads + q) % 2)
                        act.wait_ge(scan_set[h], i + 1)
                        act.dma_start(stored[:, col(i * 2 + h), :], scanned[:, h, :, 0:stored.shape[2]]
                                      ).then_inc(scan_out[h], 16)
                        if not last:
                            one_hot(lay, (m + 1) * lay.quads, h * lay.quads % 2)

                pair(0)
                with act.Fori(1, PAIRS - 1) as i:
                    pair(i)
                pair(PAIRS - 1, True)

            chunks_out(layers[0], scan0_v, scan0_set, scan0_out)

            def pair(i):
                for h in range(2):
                    act.wait_ge(var_set, i * 2 + h + 1)
                    act.activation(std[:, :], stat[:, 3, :], ACT.Sqrt).then_inc(std_set, 1)
                    act.wait_ge(y_set, i * 2 + h + 1)
                    act.copy(state[:, tiles(i * 2 + h), :], cat[:, h, :, D:2 * D]).then_inc(state_set, 1)
                    act.wait_ge(yT_ps, i * 2 + h + 1)
                    act.copy(catT[0:D, 0:4 * P], ps_misc[0:D, :])
                    act.copy(catT[0:D, 4 * P:GROUP * P], ps_hist[0:D, 0:(GROUP - 4) * P]).then_inc(yT_sb, 1)
                    act.wait_ge(t1_ps, i * 2 + h + 1)
                    wait_past(act, t1_out[h], i * 16)
                    act.copy(t1_buf[:, h, 0:4 * P], ps_table[h][:, 0, :])
                    act.copy(t1_buf[:, h, 4 * P:GROUP * P], ps_table[h][:, 1, 0:(GROUP - 4) * P]).then_inc(t1_sb, 1)

            pair(0)
            with act.Fori(1, GROUPS // 2) as i:
                pair(i)

            chunks_out(layers[1], scan1_v, scan1_set, scan1_out)

            def pair(i):
                for h in range(2):
                    act.wait_ge(mT_ps, i * 2 + h + 1)
                    act.copy(catT[0:2 * D, 0:4 * P], ps_misc[0:2 * D, :])
                    act.copy(catT[0:2 * D, 4 * P:GROUP * P], ps_hist[0:2 * D, 0:(GROUP - 4) * P]).then_inc(mT_sb, 1)
                    act.wait_ge(gates_ps, i * 2 + h + 1)
                    act.activation(gates[:, :, :], gate_view(h)[:, :, 0:2 * D], ACT.Sigmoid).then_inc(gates_set, 1)
                    act.wait_ge(pre_set, i * 2 + h + 1)
                    act.activation(cand[:, :, :], tmp[:, :, :], ACT.Tanh).then_inc(cand_set, 1)
                    act.wait_ge(var_set, i * 2 + (GROUPS + h + 1))
                    act.activation(std[:, :], stat[:, 3, :], ACT.Sqrt).then_inc(std_set, 1)

            pair(0)
            with act.Fori(1, GROUPS // 2) as i:
                pair(i)

        @block.vector
        def _(dve):
            prep_n = [0]

            def step(ins):
                prep_n[0] += 1
                ins.then_inc(prep, 1)
                dve.wait_ge(prep, prep_n[0])

            dve.memset(x_sb[:, TILES - 1, :], 0.0)
            dve.memset(node_parts[:, :, TILES:TILES + 2, :], 0.0)
            dve.memset(emb_sb[:, :], 0.0)
            for a in (src_sb, t90_sb, t8_sb):
                dve.memset(a[96:P, LAST:COLS], 0)
                dve.memset(a[:, COLS:COLS + 2 * CHUNK], 0)
            dve.memset(dst_sb[96:P, 1 + LAST:1 + COLS], NODES)
            dve.memset(dst_sb[:, 0:1], -1)
            dve.memset(dst_before[:, :], -1)
            dve.memset(gate_w[:, :], 0.0)
            dve.memset(zero_row[:, :], 0.0)
            dve.memset(zeros_bf[:, :], 0.0)
            dve.memset(ones[:, :], 1.0)
            dve.memset(catT[2 * D:2 * D + 2, :], 1.0)
            dve.memset(node_row[:, TILES:TILES + 2 * GROUP], 0)
            dve.memset(pass_on[:, 0:1], 0.0)
            dve.memset(endsT[:, :], 0.0).then_inc(pads_set, 1)

            def split(value, rest, parts):
                step(dve.tensor_copy(parts[0], value))
                step(dve.tensor_tensor(rest, value, parts[0], ALU.subtract))
                step(dve.tensor_copy(parts[1], rest))
                return dve.tensor_tensor(parts[2], rest, parts[1], ALU.subtract)

            def split_nodes(nodes):
                return split(nodes, whole[:, 0:TILES * D].rearrange("p (t f) -> p t f", f=D),
                             [node_parts[:, k, 0:TILES, :] for k in range(3)])

            dve.wait_ge(weights_in, WEIGHTS_IN)
            for k in range(3):
                last = dve.tensor_copy(WaB[:, k, :], WaT[:, k:k + 1].to_broadcast([D, P]))
            last.then_inc(wab_set, 1)
            dve.wait_ge(mats_ps, 1)
            dve.tensor_copy(mats[:, :], ps_misc[0:RELS, 0:D * D]).then_inc(mats_sb, 1)
            dve.wait_ge(consts_set, 2)
            dve.tensor_copy(iota_bf[:, :, :], iota_i[:, :].unsqueeze(2).to_broadcast([P, P, 2]))
            dve.tensor_copy(ident_bf[:, :], ident[:, :])
            dve.tensor_copy(ident_f16[:, :], ident[:, :])
            dve.tensor_copy(less_type[:, 0:1], less_key[:, 0:1])
            step(dve.tensor_scalar(type_i[:, :], node_id[:, 0:1], STRIP - 1, None, ALU.bitwise_and))
            dve.tensor_scalar(less_type[:, 1:2], type_i[:, :], -1.0, None, ALU.mult)
            dve.wait_ge(x_in, X_IN)
            split_nodes(x_sb[:, :, :]).then_inc(x_parts_set, 1)
            dve.wait_ge(scores_ps, 1)
            dve.tensor_copy(he_w[:, :], score_ps[:, 2 * D:3 * D])
            dve.tensor_copy(dst_w[:, :], score_ps[:, 3 * D:4 * D])
            dve.tensor_copy(rel_rows[:, :, D:RD], score_ps[0:RELS, D:2 * D].unsqueeze(2))
            step(dve.tensor_copy(rel_w[:, :, D:RD], score_ps[0:D, 0:1].unsqueeze(1).to_broadcast([D, RELS, 1])))
            dve.wait_ge(rel_in, 32)
            dve.wait_ge(x_parts_set, 1)
            split(rel_w[:, :, :].rearrange("i r f -> i (r f)"), whole[0:D, 0:RW],
                  [rel_parts[:, k, :] for k in range(3)]).then_inc(rel_parts_set, 1)

            def index(lay, n, h, done):
                edges = bass.ds(n * CHUNK, lay.at)
                dve.scalar_tensor_tensor(out=idx[:, h, 0:lay.at], in0=src_sb[:, edges], scalar=float(lay.kinds),
                                         in1=lay.edge_types[:, edges], op0=ALU.mult, op1=ALU.add).then_inc(done[h], 1)

            dve.wait_ge(edges_in, EDGES_IN)
            for h in range(2):
                index(layers[0], h, h, idx0_set)

            dve.wait_ge(rel_parts_set, 1)
            split(rel_rows[:, :, :].rearrange("r i o -> r o i"),
                  whole[0:RELS, 0:RD * D].rearrange("r (o i) -> r o i", i=D),
                  [rel_mats[:, k, :, :] for k in range(3)]).then_inc(product_mats_set[0], 1)
            dve.wait_ge(product_mats_set[0], 1)

            step(dve.tensor_tensor(state[:, :, :], x_sb[:, 0:TILES, :],
                                   dst_w[:, :].unsqueeze(1).to_broadcast([P, TILES, D]), ALU.mult))
            dve.tensor_reduce(dst_score[:, :], state[:, :, :], AX, ALU.add)

            step(dve.tensor_tensor(whole[:, 0:COLS - 1], dst_sb[:, 2:1 + COLS], dst_sb[:, 1:COLS], ALU.is_ge))
            step(dve.tensor_reduce(ordered[:, 1:2], whole[:, 0:COLS - 1], AX, ALU.add))
            dve.tensor_scalar(ordered[:, 2:3], ordered[:, 1:2], float(COLS - 1), None, ALU.is_equal)
            step(dve.tensor_tensor(ordered[:, 3:4], dst_sb[:, 1:2], dst_before[:, :], ALU.is_ge))
            dve.tensor_tensor(ordered[:, 0:1], ordered[:, 2:3], ordered[:, 3:4], ALU.mult).then_inc(order_set, 1)
            for k in range(4):
                dve.wait_ge(t0_out[k], 16 * (TILES // 4 + (k >= 2)))
            step(dve.memset(scanned[:, 1, :, :], 0.0))
            dve.wait_ge(order_ps, 1)
            step(dve.tensor_scalar(ordered[:, 1:2], ps_misc[:, 3 * P:3 * P + 1], float(P), None, ALU.is_lt))
            dve.tensor_copy(disorder[:, :], ordered[0:1, 1:2]).then_inc(order_flag, 1)
            step(dve.tensor_scalar(ordered[:, 2:3], ordered[:, 1:2], 0.5, None, ALU.mult))

            step(dve.tensor_copy(first[:, 0:1], dst_sb[:, 1:2]))
            step(dve.tensor_scalar(whole[:, :], dst_sb[:, 1:1 + COLS], first[:, 0:1], None, ALU.is_equal))
            step(dve.tensor_reduce(first[:, 1:2], whole[:, :], AX, ALU.add))
            dve.tensor_tensor(fix_row[:, :], run_start[:, :], first[:, 1:2], ALU.add)
            dve.tensor_scalar(first[:, 2:3], first[:, 1:2], float(COLS), None, ALU.is_equal)
            step(dve.scalar_tensor_tensor(out=first[:, 3:4], in0=dst_sb[:, 1:2], scalar=ordered[:, 2:3],
                                          in1=dst_before[:, :], op0=ALU.add, op1=ALU.is_equal))
            dve.tensor_copy(flag_cols[:, :, :], first[:, 2:4].unsqueeze(2).to_broadcast([P, 2, 2 * D])
                            ).then_inc(flags_set, 1)
            dve.wait_ge(flags_ps, 1)
            step(dve.tensor_copy(take_in[:, :], ps_misc[0:2 * D, P:2 * P]))
            step(dve.tensor_tensor(pass_on[:, 1:P], ps_misc[0:2 * D, 0:P - 1], take_in[:, 1:P], ALU.mult))

            def continues(n):
                return dve.scalar_tensor_tensor(out=cont[:, :], in0=dst_sb[:, bass.ds(n * CHUNK + 1, CHUNK)],
                                                scalar=ordered[:, 2:3], in1=dst_sb[:, col(n)],
                                                op0=ALU.add, op1=ALU.is_equal)

            def scan(h, at, f, messages):
                return dve.tensor_tensor_scan(scanned[:, h, :, at + f], cont[:, :], messages[:, :, f],
                                              scanned[:, 1 - h, CHUNK - 1, at + f:at + f + 1], ALU.mult, ALU.add)

            ROW_STEPS = 2 * QUAD // DUO
            DUOS = QUAD // DUO

            def keys(lay, m, parity, base):
                edges = bass.ds(m * CHUNK + lay.at, lay.share)
                own = slice(0, lay.share)
                dve.tensor_scalar(match_i[:, 0, own], src_sb[:, edges], BLOCKS * P - 1, None, ALU.bitwise_and)
                dve.tensor_scalar(match_i[:, 1, own], src_sb[:, edges], (BLOCKS * P).bit_length() - 1, None,
                                  ALU.logical_shift_right).then_inc(match_step[lay.n], 1)
                dve.wait_ge(match_step[lay.n], base + 1)
                wait_past(dve, match_ps[lay.n], m * lay.quads)
                dve.tensor_copy(match_cols[:, 0, own], match_i[:, 0, own])
                dve.tensor_copy(match_cols[:, 1, own], lay.edge_types[:, edges])
                dve.tensor_tensor(hot_tile[:, parity, own, :],
                                  match_i[:, 1, own].unsqueeze(2).to_broadcast([P, lay.share, BLOCK_TILES]),
                                  iota_i[:, 0:BLOCK_TILES].unsqueeze(1).to_broadcast([P, lay.share, BLOCK_TILES]),
                                  ALU.is_equal).then_inc(keys_set[lay.n], 1)

            def make_rows(lay, quad, half, q, base):
                for duo in range(QUAD // DUO):
                    own = q * QUAD + duo * DUO

                    def done(k):
                        dve.wait_ge(match_step[lay.n], base + (2 * duo + k))

                    dve.wait_ge(products_ps[lay.n], quad * 2 + (duo + 1))
                    dve.tensor_tensor(picked[:, :, :, :],
                                      ps_table[duo][:, 0, 0:DUO * BLOCK_W].rearrange("p (t j f) -> p t j f", t=DUO, f=D),
                                      hot_tile[:, half, own:own + DUO, :].unsqueeze(3).to_broadcast(
                                          [P, DUO, BLOCK_TILES, D]), ALU.mult).then_inc(match_step[lay.n], 1)
                    done(1)
                    dve.tensor_reduce(source[:, :, :], picked[:, :, :, :].rearrange("p t j f -> p t f j"), AX, ALU.add
                                      ).then_inc(match_step[lay.n], 1)
                    done(2)
                    wait_past(dve, rows_made[lay.n], quad * 2 + duo)
                    dve.tensor_tensor(by_in[:, :, 0:lay.outs, :],
                                      ps_table[duo][:, 1:1 + DUO, 0:lay.outs * D].rearrange("p t (o i) -> p t o i", i=D),
                                      source[:, :, :].unsqueeze(2).to_broadcast([P, DUO, lay.outs, D]), ALU.mult
                                      ).then_inc(products_used[lay.n], 1)
                    dve.wait_ge(products_used[lay.n], quad * 2 + (duo + 1))
                    dve.tensor_reduce(lay.rows[:, half, lay.at + own:lay.at + own + DUO, 0:lay.outs],
                                      by_in[:, :, 0:lay.outs, :], AX, ALU.add).then_inc(rows_made[lay.n], 1)

            def rest_one_hot(lay, quad, b):
                if lay.by_act < BLOCKS:
                    dve.wait_ge(match_sb[lay.n], quad + 1)
                    rest, own = slice(lay.by_act, BLOCKS), slice(0, lay.strips)
                    dve.tensor_scalar(hot_key[:, b, rest, :], hot_key[:, b, rest, :], 0.0, None, ALU.is_equal)
                    dve.tensor_scalar(hot_type[own, b, :], hot_type[own, b, :], 0.0, None, ALU.is_equal
                                      ).then_inc(match_rest, 1)

            def chunk_rows(lay, m, parity, last, between=lambda q: None):
                steps = m * (lay.quads * ROW_STEPS + 1) + 1
                for q in range(lay.quads):
                    ahead = q >= lay.quads - 2 and not last
                    if ahead and q == lay.quads - 2:
                        keys(lay, m + 1, 1 - parity, steps + q * ROW_STEPS)
                    between(q)
                    if q + 1 < lay.quads or not last:
                        rest_one_hot(lay, m * lay.quads + (q + 1), (parity * lay.quads + q + 1) % 2)
                    make_rows(lay, m * lay.quads + q, parity, q, steps + (q * ROW_STEPS + ahead))

            def first_rows(lay):
                keys(lay, 0, 0, 0)
                rest_one_hot(lay, 0, 0)
                chunk_rows(lay, 0, 0, False)

            STEPS = 5

            def chunk_done(i, h, k):
                dve.wait_ge(chunk_step, i * (2 * STEPS) + (h * STEPS + k))

            def target_parts(i, h):
                targets = dst_sb[:, bass.ds((i * 2 + h) * CHUNK + 1, CHUNK)]
                dve.tensor_scalar(dst_lo_i[:, :], targets, P - 1, None, ALU.bitwise_and)
                dve.tensor_scalar(dst_hi_i[:, :], targets, P.bit_length() - 1, None, ALU.logical_shift_right
                                  ).then_inc(chunk_step, 1)
                chunk_done(i, h, 1)
                dve.tensor_copy(dst_lo[:, :], dst_lo_i[:, :])
                dve.tensor_copy(dst_hi[:, :], dst_hi_i[:, :]).then_inc(chunk_step, 1)
                chunk_done(i, h, 2)

            def target_hots(i, h, q):
                b = (h * HOTS + q) % 2
                wait_past(dve, hot_used[b], i * HOTS + (h * HOTS + q) // 2)
                edges = slice(q * HOT, min((q + 1) * HOT, CHUNK))
                twos = (edges.stop - edges.start) // 2
                for hot, part, width in ((hot_lo, dst_lo, P), (hot_hi, dst_hi, TILES)):
                    all_of = [P, twos, width, 2]
                    last = dve.tensor_tensor(hot[:, b, 0:twos, :, :],
                                             part[:, edges].rearrange("p (c e) -> p c e", e=2).unsqueeze(2).to_broadcast(all_of),
                                             iota_bf[:, 0:width, :].unsqueeze(1).to_broadcast(all_of), ALU.is_equal)
                last.then_inc(hot_set[b], 1)

            def edge_scores(i, h):
                continues(i * 2 + h)
                dve.wait_ge(he_in[h], i * HE_IN + HE_IN)
                dve.tensor_tensor(he_dot[:, :, :], he[:, h, :, :],
                                  he_w[:, :].unsqueeze(1).to_broadcast([P, CHUNK, D]), ALU.mult).then_inc(chunk_step, 1)
                chunk_done(i, h, 3)
                dve.tensor_reduce(score[:, :], he_dot[:, :, :], AX, ALU.add).then_inc(he_used[h], 1)

            def scan_messages(i, h):
                n = i * 2 + h
                dve.wait_ge(he_used[h], i + 1)
                dve.wait_ge(rows_made[0], n * (QUADS[0] * DUOS) + QUADS[0] * DUOS)
                dve.wait_ge(rows0_in[h], i * (16 * layers[0].at) + 16 * layers[0].at)
                index(layers[0], n + 2, h, idx0_set)
                dve.tensor_tensor(score[:, :], score[:, :], rows0[:, h, :, D], ALU.add).then_inc(chunk_step, 1)
                chunk_done(i, h, 4)
                dve.tensor_tensor(weighted[:, :, :], rows0[:, h, :, 0:D],
                                  score[:, :].unsqueeze(2).to_broadcast([P, CHUNK, D]), ALU.mult
                                  ).then_inc(chunk_step, 1)
                wait_past(dve, scan0_out[h], i * 16)
                for f in range(D):
                    last = scan(h, D, f, rows0[:, h, :, :])
                last.then_inc(rows0_used[h], 1)

            def scan_weighted(i, h):
                chunk_done(i, h, 5)
                for f in range(D):
                    last = scan(h, 0, f, weighted)
                last.then_inc(scan0_set[h], 1)

            def pair(i, last=False):
                for h in range(2):
                    before = (HOTS if h == 0 else 2 * HOTS) - 1 - HOTS

                    def with_quad(q):
                        if q == 0:
                            wait_past(dve, scan0_set[1 - h], i + h)
                            wait_past(dve, hot_set[before % 2], i * HOTS + before // 2 + 1)
                            target_parts(i, h)
                            edge_scores(i, h)
                        if q == 1:
                            scan_messages(i, h)
                        if q == 2:
                            scan_weighted(i, h)
                        if not (last and h == 1):
                            for k in COUNT_WITH[q]:
                                target_hots(i, h, k)

                    if last and h == 1:
                        with_quad(0)
                        for k in range(HOTS):
                            target_hots(i, h, k)
                        with_quad(1)
                        with_quad(2)
                    else:
                        chunk_rows(layers[0], i * 2 + (h + 1), 1 - h, last, with_quad)

            first_rows(layers[0])
            pair(0)
            with dve.Fori(1, PAIRS - 1) as i:
                pair(i)
            pair(PAIRS - 1, True)

            def carries(layer, width, all_scanned):
                dve.wait_ge(all_scanned, PAIRS)
                dve.tensor_copy(last_state[:, 0:width], scanned[:, 1, CHUNK - 1, 0:width]).then_inc(carry_step, 1)
                dve.wait_ge(ends_ps, layer + 1)
                dve.tensor_tensor(endsT[0:width, 1:P], ps_misc[0:width, 0:P - 1], take_in[0:width, 1:P], ALU.mult
                                  ).then_inc(carry_step, 1)
                dve.wait_ge(carry_step, 2 + 3 * layer)
                dve.tensor_tensor_scan(carryT[0:width, :], pass_on[0:width, :], endsT[0:width, :], 0.0,
                                       ALU.mult, ALU.add).then_inc(carry_step, 1)
                dve.wait_ge(carry_ps, layer + 1)
                dve.tensor_copy(carry[:, 0:width], ps_misc[:, P:P + width]).then_inc(carry_set, 1)

            carries(0, 2 * D, scan0_set[1])

            dve.wait_ge(hist_ps, 1)
            dve.tensor_copy(degree[:, :], ps_hist[0:TILES, 0:P]).then_inc(node_step, 1)
            dve.wait_ge(node_step, 1)
            dve.tensor_tensor_scan(node_end[:, :], ones[0:TILES, :], degree[:, :], 0.0, ALU.mult, ALU.add
                                   ).then_inc(node_step, 1)
            dve.wait_ge(node_step, 2)
            dve.tensor_scalar(degree[:, :], degree[:, :], 0.0, None, ALU.is_gt).then_inc(node_step, 1)
            dve.wait_ge(offset_ps, 1)
            dve.tensor_scalar(node_end[:, :], node_end[:, :], ps_misc[0:TILES, 2 * P:2 * P + 1], float(-1 - ROWS),
                              ALU.add, ALU.add).then_inc(node_step, 1)
            dve.wait_ge(node_step, 4)
            dve.tensor_tensor(node_end[:, :], node_end[:, :], degree[:, :], ALU.mult).then_inc(node_step, 1)
            dve.wait_ge(node_step, 5)
            dve.tensor_scalar(node_end[:, :], node_end[:, :], float(ROWS), None, ALU.add).then_inc(node_step, 1)
            dve.wait_ge(rows_ps, 1)
            dve.tensor_copy(node_row[:, 0:TILES], ps_misc[:, 3 * P:3 * P + TILES]).then_inc(node_step, 1)
            dve.wait_ge(node_step, 7)

            def sum_edges(layer, width):
                EDGE_STEPS = 3

                def spread(c):
                    def done(k):
                        dve.wait_ge(edge_step, c * EDGE_STEPS + (layer * COLS * EDGE_STEPS + k))

                    target = dst_sb[:, bass.ds(c + 1, 1)]
                    wait_past(dve, summed, c + layer * COLS)
                    dve.tensor_scalar(edge_part_i[:, 0:1], target, P - 1, None, ALU.bitwise_and)
                    dve.tensor_scalar(edge_part_i[:, 1:2], target, P.bit_length() - 1, None,
                                      ALU.logical_shift_right).then_inc(edge_step, 1)
                    done(1)
                    dve.tensor_copy(edge_part[:, :], edge_part_i[:, :]).then_inc(edge_step, 1)
                    done(2)
                    dve.tensor_scalar(edge_lo[:, :], iota_i[:, :], edge_part[:, 0:1], None, ALU.is_equal)
                    dve.tensor_scalar(edge_hi[:, :], iota_i[:, 0:TILES], edge_part[:, 1:2], None, ALU.is_equal
                                      ).then_inc(edge_step, 1)
                    done(3)
                    dve.wait_ge(edge_in, c * 16 + 16 * (layer * COLS + 1))
                    dve.tensor_tensor(whole[:, 0:TILES * width].rearrange("p (t f) -> p t f", f=width),
                                      edge_hi[:, :].unsqueeze(2).to_broadcast([P, TILES, width]),
                                      edge_row[:, 0:width].unsqueeze(1).to_broadcast([P, TILES, width]), ALU.mult
                                      ).then_inc(spread_set, 1)

                with out_of_order(dve):
                    spread(0)
                    with dve.Fori(1, COLS) as c:
                        spread(c)
                    dve.wait_ge(summed, (layer + 1) * COLS)
                    cols = SUM_TILES * width
                    for b, bank in enumerate(sum_banks):
                        last = dve.tensor_copy(whole[:, b * cols:(b + 1) * cols], bank[:, 0:cols])
                    last.then_inc(sums_sb, 1)
                    dve.tensor_copy(node_row[:, 0:TILES], node_id[:, :]).then_inc(node_step, 1)
                    dve.wait_ge(node_step, 8 + layer)

            sum_edges(0, 2 * D)

            def group_rows(g, h, done):
                dve.tensor_copy(group_row[:, h, :], node_row[:, tiles(g)]).then_inc(done[h], 1)

            for h in range(2):
                group_rows(h, h, group0_set)

            LN_STEPS = 6

            def layernorm(done, group, result):
                def bc(s):
                    return s.unsqueeze(2).to_broadcast([P, GROUP, D])

                dve.tensor_reduce(stat[:, 0, :], val[:, :, :], AX, ALU.add).then_inc(ln_step, 1)
                done(1)
                dve.tensor_scalar(stat[:, 1, :], stat[:, 0, :], -1.0 / D, None, ALU.mult).then_inc(ln_step, 1)
                done(2)
                dve.tensor_tensor(tmp[:, :, :], val[:, :, :], bc(stat[:, 1, :]), ALU.add).then_inc(ln_step, 1)
                done(3)
                dve.tensor_tensor(val[:, :, :], tmp[:, :, :], tmp[:, :, :], ALU.mult).then_inc(ln_step, 1)
                done(4)
                dve.tensor_reduce(stat[:, 2, :], val[:, :, :], AX, ALU.add).then_inc(ln_step, 1)
                done(5)
                dve.tensor_scalar(stat[:, 3, :], stat[:, 2, :], 1.0 / D, EPS, ALU.mult, ALU.add).then_inc(var_set, 1)
                dve.wait_ge(std_set, group + 1)
                dve.reciprocal(stat[:, 0, :], std[:, :]).then_inc(ln_step, 1)
                done(6)
                return dve.tensor_tensor(result, tmp[:, :, :], bc(stat[:, 0, :]), ALU.mult)

            PER0 = 2 + LN_STEPS
            def pair(i):
                for h in range(2):
                    g = i * 2 + h

                    def done(k):
                        dve.wait_ge(ln_step, i * (2 * PER0) + (h * PER0 + k))

                    dve.wait_ge(sums0_in[h], i * SUMS_IN + SUMS_IN)
                    group_rows(g + 2, h, group0_set)
                    wait_past(dve, y_set, g)
                    dve.tensor_tensor(tmp[:, :, :], sums0[:, h, :, D:2 * D],
                                      dst_score[:, tiles(g)].unsqueeze(2).to_broadcast([P, GROUP, D]), ALU.mult
                                      ).then_inc(ln_step, 1)
                    done(1)
                    dve.tensor_tensor(tmp[:, :, :], tmp[:, :, :], sums0[:, h, :, 0:D], ALU.add).then_inc(sums0_used, 1)
                    dve.wait_ge(sums0_used, g + 1)
                    dve.tensor_tensor(val[:, :, :], tmp[:, :, :], x_sb[:, tiles(g), :], ALU.add).then_inc(ln_step, 1)
                    done(2)
                    layernorm(lambda k: done(2 + k), g, cat[:, h, :, D:2 * D]).then_inc(y_set, 1)

            pair(0)
            with dve.Fori(1, GROUPS // 2) as i:
                pair(i)

            for h in range(2):
                group_rows(h, h, group1_set)
                index(layers[1], h, h, idx1_set)
                dve.wait_ge(scan0_out[h], 16 * PAIRS)
            dve.wait_ge(late_in, LATE_IN)
            dve.wait_ge(state_set, GROUPS)
            split_nodes(state[:, :, :]).then_inc(node_parts_set, 1)
            dve.wait_ge(node_parts_set, 1)
            type_parts = [hot_key[0:3 * STRIP, 0, k, 0:D * D] for k in range(3)]
            step(split(emb_sb[:, :], whole[0:3 * STRIP, 0:D * D], type_parts))
            for k in range(3):
                own = slice(k * STRIP, (k + 1) * STRIP)
                last = dve.tensor_copy(type_mats[own, :], hot_key[own, 0, k, 0:D * D])
            last.then_inc(product_mats_set[1], 1)
            dve.wait_ge(product_mats_set[1], 1)

            def pair(i, last=False):
                for h in range(2):
                    n = i * 2 + h

                    def with_quad(q):
                        if q == 0:
                            wait_past(dve, scan1_set[1 - h], i + h)
                            continues(n).then_inc(cont_set, 1)
                        if q == 1:
                            dve.wait_ge(cont_set, n + 1)
                            dve.wait_ge(rows_made[1], n * (QUADS[1] * DUOS) + QUADS[1] * DUOS)
                            dve.wait_ge(rows1_in[h], i * (16 * layers[1].at) + 16 * layers[1].at)
                            index(layers[1], n + 2, h, idx1_set)
                            wait_past(dve, scan1_out[h], i * 16)
                        if q in (1, 2):
                            for f in range((q - 1) * D // 2, q * D // 2):
                                last_scan = scan(h, 0, f, rows1[:, h, :, :])
                        if q == 2:
                            last_scan.then_inc(scan1_set[h], 1)

                    if last and h == 1:
                        for q in range(QUADS[1]):
                            with_quad(q)
                    else:
                        chunk_rows(layers[1], n + 1, 1 - h, last, with_quad)

            first_rows(layers[1])
            pair(0)
            with dve.Fori(1, PAIRS - 1) as i:
                pair(i)
            pair(PAIRS - 1, True)
            carries(1, D, scan1_set[1])
            sum_edges(1, D)

            PER1 = 5 + LN_STEPS

            def take_in_sums(i, h, ahead):
                g, half = i * 2 + (h + ahead), (h + ahead) % 2
                dve.tensor_copy(cat[:, half, :, D:2 * D], state[:, tiles(g), :])
                dve.wait_ge(sums1_in[half], (i + (h + ahead) // 2) * SUMS_IN + SUMS_IN)
                group_rows(g + 2, half, group1_set)
                dve.tensor_copy(cat[:, half, :, 0:D], sums1[:, half, :, :]).then_inc(m_set, 1)

            def pair(i, last=False):
                for h in range(2):
                    g = i * 2 + h
                    pre = gate_view(h)
                    old = cat[:, h, :, D:2 * D]

                    def done(k):
                        dve.wait_ge(ln_step, i * (2 * PER1) + (GROUPS * PER0 + h * PER1 + k))

                    wait_past(dve, out_set[1 - h], i + h)
                    dve.wait_ge(gates_set, g + 1)
                    dve.tensor_tensor(tmp[:, :, :], pre[:, :, 3 * D:4 * D], gates[:, :, 0:D], ALU.mult
                                      ).then_inc(ln_step, 1)
                    done(1)
                    dve.tensor_tensor(tmp[:, :, :], pre[:, :, 2 * D:3 * D], tmp[:, :, :], ALU.add).then_inc(pre_set, 1)
                    dve.wait_ge(cand_set, g + 1)
                    dve.tensor_tensor(val[:, :, :], old, cand[:, :, :], ALU.subtract).then_inc(ln_step, 1)
                    done(2)
                    dve.tensor_tensor(val[:, :, :], val[:, :, :], gates[:, :, D:2 * D], ALU.mult).then_inc(ln_step, 1)
                    done(3)
                    dve.tensor_tensor(val[:, :, :], val[:, :, :], cand[:, :, :], ALU.add).then_inc(ln_step, 1)
                    done(4)
                    if not (last and h == 1):
                        take_in_sums(i, h, 1)
                    dve.tensor_tensor(val[:, :, :], val[:, :, :], old, ALU.add).then_inc(ln_step, 1)
                    done(5)
                    wait_past(dve, out_out[h], i * 16)
                    layernorm(lambda k: done(5 + k), g + GROUPS, out_buf[:, h, :, :]).then_inc(out_set[h], 1)

            take_in_sums(0, 0, 0)
            pair(0)
            with dve.Fori(1, GROUPS // 2 - 1) as i:
                pair(i)
            pair(GROUPS // 2 - 1, True)


INPUTS = ["x", "src", "dst", "edge_attr_16", "edge_type_8", "edge_type_90", "L0_gnn_Ws", "L0_gnn_Wa",
          "L0_gnn_weight", "L0_gnn_w_comp", "L1_gnn_edge_emb", "L1_gnn_w_ih", "L1_gnn_w_hh", "L1_gnn_b_ih",
          "L1_gnn_b_hh"]


def kernel(**inputs):
    import numpy as np
    import concourse.bacc as bacc
    from concourse.bass_utils import run_bass_kernel_spmd

    nc = bacc.Bacc("TRN2", target_bir_lowering=False, num_devices=1)
    arrays, args = {}, []
    for name in INPUTS:
        a = np.ascontiguousarray(inputs[name])
        arrays[f"in_{name}"] = a
        args.append(nc.dram_tensor(f"in_{name}", a.shape, mybir.dt.from_np(a.dtype), kind="ExternalInput").ap())
    result = nc.dram_tensor("result", inputs["x"].shape, F32, kind="ExternalOutput").ap()
    build(nc, *args, result)
    return run_bass_kernel_spmd(nc, [arrays], core_ids=[0]).results[0]["result"]
```

```python
import concourse.bass as bass
from concourse import mybir
from contextlib import ExitStack

F32 = mybir.dt.float32
I32 = mybir.dt.int32
BF16 = mybir.dt.bfloat16
F16 = mybir.dt.float16
ALU = mybir.AluOpType
ACT = mybir.ActivationFunctionType
AX = mybir.AxisListType.X

P = 128
D = 16
EPS = 1e-5
CHUNK = 62
QUAD, DUO = 4, 2
QUADS = 5


class Layer:
    def __init__(self, n, by_act, known, edge_types, kinds, strips, mats, outs, rows):
        self.n, self.by_act, self.known, self.edge_types, self.kinds = n, by_act, known, edge_types, kinds
        self.strips, self.mats, self.outs, self.rows = strips, mats, outs, rows
        self.widths = [DUO] * known + [QUAD] * (QUADS - known)
        self.share = sum(self.widths)
        self.own = CHUNK - self.share
        self.starts = [sum(self.widths[:q]) for q in range(QUADS)]
        self.duos = self.share // DUO

    def half(self, parity, q):
        return (parity * (QUADS - self.known) + q - self.known) % 2

    def done(self, m, q, duo):
        return m * self.duos + (self.starts[q] // DUO + duo + 1)


def build(nc, x, src, dst, edge_attr, type_8, type_90, Ws, Wa, weight, w_comp,
          edge_emb, w_ih, w_hh, b_ih, b_hh, out):
    NODES, EDGES = x.shape[0], src.shape[0]
    RELS, BASES = w_comp.shape
    TYPES = edge_emb.shape[0]
    CHUNKS = -(-EDGES // (P * CHUNK))
    CHUNKS += CHUNKS % 2
    COLS = CHUNKS * CHUNK
    LAST = EDGES - (P - 1) * COLS
    FULL = LAST // CHUNK // 2 * 2
    ROWS = P * COLS
    TILES = -(-NODES // P)
    TAIL = NODES - (TILES - 1) * P
    GROUP = 7
    GROUPS = TILES // GROUP
    REST = 112
    RD = D + 1
    RW = RELS * RD
    BANKS = 3
    BW = RW // BANKS
    HOT = 16
    HOTS = -(-CHUNK // HOT)
    assert TILES % 4 == 2 and 2 * RW <= 2 * CHUNK * 2 * D
    assert TILES % GROUP == 0 and GROUPS % 2 == 0 and CHUNK % 2 == 0 and HOT % 2 == 0 and RW % BANKS == 0 and BW <= 512
    assert 0 < LAST <= COLS and TILES <= P
    PAIRS = CHUNKS // 2
    SUM_BANKS = 7
    SUM_TILES = TILES // SUM_BANKS
    assert TILES % SUM_BANKS == 0 and SUM_TILES * 2 * D <= 512 and TILES * 2 * D <= COLS
    BLOCKS = 8
    BLOCK_TILES = -(-TILES // BLOCKS)
    BLOCK_W = BLOCK_TILES * D
    assert DUO * BLOCK_W <= 512
    KNOWN = (1, 0)
    STRIP = 32
    assert TYPES <= STRIP
    LEFT_PARTS = (0, 0, 0, 1, 1, 1, 2, 2)
    RIGHT_PARTS = (0, 1, 2, 0, 1, 2, 0, 1)
    assert len(LEFT_PARTS) * D == P

    ctx = ExitStack()
    with ctx:
        def sb(name, shape, dt=F32):
            return ctx.enter_context(nc.sbuf_tensor(name, shape, dt))

        def ps(name, shape, dt=F32):
            return ctx.enter_context(nc.psum_tensor(name, shape, dt))

        def sem(name):
            return ctx.enter_context(nc.semaphore(name))

        def sems(name):
            return [sem(f"{name}_{h}") for h in range(2)]

        relation_dram = nc.dram_tensor("relation_mats", (D * RELS, D), F32).ap()
        table0 = nc.dram_tensor("relation_table", (TILES * P * RELS, RD), F32).ap()
        table1 = nc.dram_tensor("type_table", (TILES * P * TYPES, D), F32).ap()
        scan0 = nc.dram_tensor("scanned_0", (ROWS + 1, 2 * D), F32).ap()
        scan1 = nc.dram_tensor("scanned_1", (ROWS + 1, D), F32).ap()

        x_sb = sb("x_sb", [P, TILES, D])
        node_parts = sb("node_parts", [P, 3, TILES + 2, D], BF16)
        x_tile = sb("x_tile", [P, 2, len(LEFT_PARTS), D], BF16)
        state = sb("state", [P, TILES, D])
        cat = sb("cat", [P, 2, GROUP, 2 * D])
        src_sb = sb("src_sb", [P, COLS + 2 * CHUNK], I32)
        t90_sb = sb("t90_sb", [P, COLS + 2 * CHUNK], I32)
        t8_sb = sb("t8_sb", [P, COLS + 2 * CHUNK], I32)
        known = t8_sb[:, 0:CHUNKS * DUO * D].bitcast(F32).rearrange("p (c f) -> p c f", f=D)
        dst_sb = sb("dst_sb", [P, COLS + 1], I32)
        dst_before = sb("dst_before", [P, 1], I32)
        whole = sb("whole", [P, COLS])
        ident = sb("ident", [P, P])
        ident_bf = sb("ident_bf", [P, P], BF16)
        ones = sb("ones", [P, P])
        earlier = sb("earlier", [P, P])
        iota_i = sb("iota_i", [P, P], I32)
        run_start = sb("run_start", [P, 1], I32)
        iota_bf = sb("iota_bf", [P, P, 2], BF16)
        zeros_bf = sb("zeros_bf", [P, P], BF16)
        zero_row = sb("zero_row", [1, 2 * D])
        wcT = sb("wcT", [BASES, RELS])
        basis = sb("basis", [BASES, D * D])
        mats = sb("mats", [RELS, D * D])
        Ws_sb = sb("Ws_sb", [D, D])
        WaT = sb("WaT", [D, 3])
        WaB = sb("WaB", [D, 3, P])
        rel_stack = sb("rel_stack", [P, RW], BF16)
        he_w = sb("he_w", [P, D])
        rel_rows = sb("rel_rows", [RELS, D, RD])
        rel_mats = sb("rel_mats", [RELS, 3, RD, D], BF16)
        emb_sb = sb("emb_sb", [3 * STRIP, D * D])
        type_mats = sb("type_mats", [3 * STRIP, D * D], BF16)
        ident_f16 = sb("ident_f16", [P, P], F16)
        less_key = sb("less_key", [P, BLOCKS])
        type_i = sb("type_i", [P, 1], I32)
        less_type = sb("less_type", [P, 2])
        match_i = sb("match_i", [P, 2, QUADS * QUAD], I32)
        match_cols = sb("match_cols", [P, 2, 2, QUADS * QUAD], F16)
        hot_tile = sb("hot_tile", [P, 2, QUADS * QUAD, BLOCK_TILES])
        hot_key = sb("hot_key", [P, 2, BLOCKS, QUAD * P], BF16)
        hot_known = sb("hot_known", [RELS, DUO * P], BF16)
        hot_type = sb("hot_type", [P, 2, QUAD * P], BF16)
        rel_parts = hot_key[0:D, :, :, :].rearrange("p h g e -> p (h g e)")[:, 0:3 * RW].rearrange(
            "p (k c) -> p k c", k=3)
        picked = sb("picked", [P, DUO, BLOCK_TILES, D])
        source = sb("source", [P, DUO, D])
        by_in = sb("by_in", [P, DUO, RD, D])
        dst_w = sb("dst_w", [P, D])
        dst_score = sb("dst_score", [P, TILES])
        type_w = sb("type_w", [D, TYPES, D])
        gate_w = sb("gate_w", [2 * D + 2, 4 * D])
        xT = sb("xT", [P, 2, P], BF16)
        t0_buf = sb("t0_buf", [P, 2, RW])
        idx = sb("idx", [P, 2, CHUNK], I32)
        he = sb("he", [P, 2, CHUNK, D])
        rows0 = sb("rows0", [P, 2, CHUNK, RD])
        rel_w = rows0[0:D, :, :, :].rearrange("p h c f -> p (h c f)")[:, 0:RW].rearrange("p (r f) -> p r f", f=RD)
        rows1 = rows0[:, :, :, 0:D]
        he_dot = sb("he_dot", [P, CHUNK, D])
        score = sb("score", [P, CHUNK])
        weighted = he_dot
        cont = sb("cont", [P, CHUNK])
        scanned = sb("scanned", [P, 2, CHUNK, 2 * D])
        t0_tiles = [t0_buf[:, 0, :], t0_buf[:, 1, :]] + [
            scanned[:, :, :, :].rearrange("p h c f -> p (h c f)")[:, k * RW:(k + 1) * RW] for k in range(2)]
        dst_lo_i = sb("dst_lo_i", [P, CHUNK], I32)
        dst_hi_i = sb("dst_hi_i", [P, CHUNK], I32)
        dst_lo = sb("dst_lo", [P, CHUNK], BF16)
        dst_hi = sb("dst_hi", [P, CHUNK], BF16)
        hot_lo = sb("hot_lo", [P, 2, HOT // 2, P, 2], BF16)
        hot_hi = sb("hot_hi", [P, 2, HOT // 2, TILES, 2], BF16)
        ordered = sb("ordered", [P, 4])
        disorder = sb("disorder", [1, 1], I32)
        edge_row = sb("edge_row", [P, 2 * D])
        edge_part_i = sb("edge_part_i", [P, 2], I32)
        edge_part = sb("edge_part", [P, 2])
        edge_lo = sb("edge_lo", [P, P])
        edge_hi = sb("edge_hi", [P, TILES])
        node_id = sb("node_id", [P, TILES], I32)
        first = sb("first", [P, 4])
        flag_cols = sb("flag_cols", [P, 2, 2 * D])
        fix_row = sb("fix_row", [P, 1], I32)
        pass_on = sb("pass_on", [2 * D, P])
        take_in = sb("take_in", [2 * D, P])
        endsT = sb("endsT", [2 * D, P])
        carryT = sb("carryT", [2 * D, P])
        carry = sb("carry", [P, 2 * D])
        last_state = sb("last_state", [P, 2 * D])
        degree = sb("degree", [TILES, P])
        node_end = sb("node_end", [TILES, P])
        node_row = sb("node_row", [P, TILES + 2 * GROUP], I32)
        group_row = sb("group_row", [P, 2, GROUP], I32)
        sums0 = sb("sums0", [P, 2, GROUP, 2 * D])
        sums1 = sb("sums1", [P, 2, GROUP, D])
        val = sb("val", [P, GROUP, D])
        tmp = sb("tmp", [P, GROUP, D])
        stat = sb("stat", [P, 4, GROUP])
        std = sb("std", [P, GROUP])
        catT = sb("catT", [2 * D + 2, GROUP * P])
        t1_buf = t0_buf[:, :, 0:GROUP * TYPES * D]
        gates = sb("gates", [P, GROUP, 2 * D])
        cand = sb("cand", [P, GROUP, D])
        out_buf = sb("out_buf", [P, 2, GROUP, D])

        ps_table = [ps(f"ps_table_{h}", [P, BANKS, 512]) for h in range(2)]
        ps_misc = ps("ps_misc", [P, 512])
        ps_hist = ps("ps_hist", [P, 512])

        def gate_view(h):
            return ps_table[h][:, 0, 0:GROUP * 4 * D].rearrange("p (t g) -> p t g", g=4 * D)

        pads_set = sem("pads_set")
        consts_set = sem("consts_set")
        weights_in, x_in, edges_in, late_in = sem("weights_in"), sem("x_in"), sem("edges_in"), sem("late_in")
        wab_set, mats_ps, mats_sb, mats_out = sem("wab_set"), sem("mats_ps"), sem("mats_sb"), sem("mats_out")
        rel_in, scores_ps = sem("rel_in"), sem("scores_ps")
        prep = sem("prep")
        flags_set, flags_ps = sem("flags_set"), sem("flags_ps")
        x_parts_set, x_tile_set, rel_parts_set = sem("x_parts_set"), sem("x_tile_set"), sem("rel_parts_set")
        stack_in = sem("stack_in")
        order_set, order_ps, order_flag = sem("order_set"), sem("order_ps"), sem("order_flag")
        xT_ps, xT_sb, t0_ps = sem("xT_ps"), sem("xT_sb"), sem("t0_ps")
        t0_sb = sem("t0_sb")
        t0_out = [sem(f"t0_out_{k}") for k in range(4)]
        idx0_set, rows0_in, rows0_used = sems("idx0_set"), sems("rows0_in"), sems("rows0_used")
        he_in, he_used = sems("he_in"), sems("he_used")
        chunk_step = sem("chunk_step")
        scan0_set, scan0_out = sems("scan0_set"), sems("scan0_out")
        hot_set, hot_used, hist_ps = sems("hot_set"), sems("hot_used"), sem("hist_ps")
        node_step, offset_ps, rows_ps = sem("node_step"), sem("offset_ps"), sem("rows_ps")
        carry_step = sem("carry_step")
        ends_ps, carry_ps, carry_set, fixed = sem("ends_ps"), sem("carry_ps"), sem("carry_set"), sem("fixed")
        gather_begun = sem("gather_begun")
        group0_set, sums0_in, sums0_used = sems("group0_set"), sems("sums0_in"), sem("sums0_used")
        ln_step = sem("ln_step")
        var_set, std_set, y_set = sem("var_set"), sem("std_set"), sem("y_set")
        state_set = sem("state_set")
        yT_ps, yT_sb, t1_ps, t1_sb, t1_out = sem("yT_ps"), sem("yT_sb"), sem("t1_ps"), sem("t1_sb"), sems("t1_out")
        idx1_set, rows1_in, cont_set = sems("idx1_set"), sems("rows1_in"), sem("cont_set")
        scan1_set, scan1_out = sems("scan1_set"), sems("scan1_out")
        group1_set, sums1_in = sems("group1_set"), sems("sums1_in")
        m_set, mT_ps, mT_sb = sem("m_set"), sem("mT_ps"), sem("mT_sb")
        gates_ps, gates_set, pre_set, cand_set = sem("gates_ps"), sem("gates_set"), sem("pre_set"), sem("cand_set")
        gates_used = sem("gates_used")
        product_mats_set, node_parts_set = sems("product_mats_set"), sem("node_parts_set")
        match_step = sems("match_step")
        keys_set, match_ps, match_sb, match_set = sems("keys_set"), sems("match_ps"), sems("match_sb"), sems("match_set")
        known_in, types_pad_set, types_in = sem("known_in"), sem("types_pad_set"), sem("types_in")
        match_rest = sem("match_rest")
        products_ps, products_used, rows_made = sems("products_ps"), sems("products_used"), sems("rows_made")
        edge_in, edge_step, spread_set = sem("edge_in"), sem("edge_step"), sem("spread_set")
        summed, sums_sb, sums_out = sem("summed"), sem("sums_sb"), sem("sums_out")
        out_set, out_out = sems("out_set"), sems("out_out")

        block = ctx.enter_context(nc.Block())

        def wait_past(eng, signal, value):
            if not (isinstance(value, int) and value <= 0):
                eng.wait_ge(signal, value)

        def col(n):
            return bass.ds(n * CHUNK, CHUNK)

        def tiles(g):
            return bass.ds(g * GROUP, GROUP)

        def edge_views(a):
            tail = " f" if len(a.shape) == 2 else ""
            body = a[0:(P - 1) * COLS].rearrange(f"(p c){tail} -> p c{tail}", c=COLS)
            last = a[(P - 1) * COLS:EDGES].rearrange(f"(p c){tail} -> p c{tail}", p=1)
            return body, last

        he_body, he_last = edge_views(edge_attr)
        scan0_v = scan0[0:ROWS, :].rearrange("(p c) f -> p c f", c=COLS)
        scan1_v = scan1[0:ROWS, :].rearrange("(p c) f -> p c f", c=COLS)
        table0_v = table0.rearrange("(t p r) f -> p t (r f)", p=P, r=RELS)
        table1_v = table1.rearrange("(t p r) f -> p t (r f)", p=P, r=TYPES)
        out_v = out[0:(TILES - 1) * P, :].rearrange("(t p) f -> p t f", p=P)
        type_cols = type_w[:, :, :].rearrange("h t m -> h (t m)")
        xT_bank = [b[:, 0:P // 2].bitcast(BF16) for b in (ps_misc, ps_hist)]
        score_ps = ps_table[1][:, 0, :]
        match_bank = ps_misc[:, :].bitcast(F16).rearrange("p (k e) -> p k e", k=2)
        sum_banks = [ps_table[h][:, b, :] for h in range(2) for b in range(BANKS)] + [ps_misc[:, :]]

        def out_of_order(eng):
            eng.wait_ge(order_flag, 1)
            return eng.If(eng.value_load(disorder[0:1, 0:1], min_val=0, max_val=1))

        HOT_WITH, COUNT_WITH = ((), (0,), (1,), (2,), (3,)), ((), (), (0,), (1,), (2, 3))
        assert sum(map(len, COUNT_WITH)) == HOTS and len(COUNT_WITH) == QUADS
        WEIGHTS_IN, X_IN, EDGES_IN, LATE_IN, HE_IN = 4 * 16, 2 * 16, 10 * 16, 14 * 16, 3 * 16
        SUMS_IN = 16 * GROUP

        layers = [
            Layer(0, BLOCKS, KNOWN[0], t90_sb, RELS, RELS,
                  [rel_mats[:, k, :, :].rearrange("r o i -> r (o i)") for k in range(3)], RD, rows0),
            Layer(1, BLOCKS - 2, KNOWN[1], t8_sb, TYPES, 3 * STRIP, [type_mats[:, :]], D, rows1),
        ]

        @block.sync
        def _(sp):
            with nc.allow_non_contiguous_dma(reason="small weights, transposed once"):
                sp.dma_start(wcT[:, :], w_comp.rearrange("r b -> b r")).then_inc(weights_in, 16)
                sp.dma_start(basis[:, :].rearrange("b (i o) -> b i o", o=D),
                             weight.rearrange("b i o -> (b i o)").rearrange("(i b o) -> b i o", i=D, b=BASES)
                             ).then_inc(weights_in, 16)
                sp.dma_start(Ws_sb[:, :], Ws).then_inc(weights_in, 16)
                sp.dma_start(WaT[:, :], Wa.rearrange("a (k o) -> o (a k)", o=D)).then_inc(weights_in, 16)
                sp.dma_start(x_sb[:, 0:TILES - 1, :],
                             x[0:(TILES - 1) * P, :].rearrange("(t p) f -> p t f", p=P)).then_inc(x_in, 16)
                sp.wait_ge(pads_set, 1)
                sp.dma_start(x_sb[0:TAIL, TILES - 1, :], x[(TILES - 1) * P:NODES, :]).then_inc(x_in, 16)
                sp.wait_ge(mats_sb, 1)
                sp.dma_start(relation_dram.rearrange("(i r) o -> r i o", r=RELS),
                             mats[:, :].rearrange("r (i o) -> r i o", o=D)).then_inc(mats_out, 16)
                sp.wait_ge(mats_out, 16)
                sp.dma_start(rel_w[:, :, 0:D], relation_dram.rearrange("(r i) o -> i r o", i=D)).then_inc(rel_in, 16)
                sp.dma_start(rel_rows[:, :, 0:D], relation_dram.rearrange("(r i) o -> r i o", i=D)).then_inc(rel_in, 16)
                sp.wait_ge(rel_parts_set, 1)
                for k in range(0, len(RIGHT_PARTS), 2):
                    sp.dma_start(rel_stack[k * D:(k + 1) * D, :], rel_parts[:, RIGHT_PARTS[k], :]).then_inc(stack_in, 16)

            def store_tile(t, k):
                sp.wait_ge(t0_sb, t + 1)
                sp.dma_start(table0_v[:, bass.ds(t, 1), :], t0_tiles[k].unsqueeze(1)).then_inc(t0_out[k], 16)

            for k in range(2):
                store_tile(k, k + 2)
            with sp.Fori(0, TILES // 4) as i:
                for k in range(4):
                    store_tile(i * 4 + (k + 2), k)

            with nc.allow_non_contiguous_dma(reason="small weights, transposed once"):
                for k in range(3):
                    sp.dma_start(emb_sb[k * STRIP:k * STRIP + TYPES, :], edge_emb).then_inc(late_in, 16)
                sp.dma_start(type_w[:, :, :], edge_emb.rearrange("t (m h) -> h t m", h=D)).then_inc(late_in, 16)
                for w, row, own in ((w_ih, 0, 2 * D), (w_hh, D, 3 * D)):
                    sp.dma_start(gate_w[row:row + D, 0:2 * D], w[0:2 * D, :].rearrange("g i -> i g")
                                 ).then_inc(late_in, 16)
                    sp.dma_start(gate_w[row:row + D, own:own + D], w[2 * D:3 * D, :].rearrange("g i -> i g")
                                 ).then_inc(late_in, 16)
                for b, row, own in ((b_ih, 2 * D, 2 * D), (b_hh, 2 * D + 1, 3 * D)):
                    b = b.rearrange("(a g) -> a g", a=1)
                    sp.dma_start(gate_w[row:row + 1, 0:2 * D], b[:, 0:2 * D]).then_inc(late_in, 16)
                    sp.dma_start(gate_w[row:row + 1, own:own + D], b[:, 2 * D:3 * D]).then_inc(late_in, 16)
                sp.dma_start(scan0[ROWS:ROWS + 1, :], zero_row[:, :]).then_inc(late_in, 16)
                sp.dma_start(scan1[ROWS:ROWS + 1, :], zero_row[:, 0:D]).then_inc(late_in, 16)

            def load_he(n, h):
                sp.dma_start(he[0:REST, h, :, :], he_body[0:REST, col(n), :]).then_inc(he_in[h], 16)
                sp.dma_start(he[REST:P - 1, h, :, :], he_body[REST:P - 1, col(n), :]).then_inc(he_in[h], 16)

            def pair(i):
                for h in range(2):
                    wait_past(sp, he_used[h], i)
                    load_he(i * 2 + h, h)
                    sp.dma_start(he[P - 1:P, h, :, :], he_last[:, col(i * 2 + h), :]).then_inc(he_in[h], 16)

            pair(0)
            with sp.Fori(1, FULL // 2) as i:
                pair(i)
            for n in range(FULL, CHUNKS):
                h = n % 2
                sp.wait_ge(he_used[h], n // 2)
                load_he(n, h)
                left = min(CHUNK, max(LAST - n * CHUNK, 1))
                at = min(n * CHUNK, LAST - left)
                sp.dma_start(he[P - 1:P, h, 0:left, :], he_last[:, at:at + left, :]).then_inc(he_in[h], 16)

            def sum_edges(layer, scan, width):
                rows = scan[0:ROWS, :].rearrange("(p c) f -> p c f", c=COLS)

                def load(c):
                    wait_past(sp, spread_set, c + layer * COLS)
                    sp.dma_start(edge_row[:, 0:width].unsqueeze(1), rows[:, bass.ds(c, 1), :]).then_inc(edge_in, 16)

                with out_of_order(sp):
                    sp.wait_ge(fixed, 16 * (layer + 1))
                    load(0)
                    with sp.Fori(1, COLS) as c:
                        load(c)
                    sp.wait_ge(sums_sb, layer + 1)
                    sp.dma_start(scan[0:TILES * P, :].rearrange("(t p) f -> p t f", p=P),
                                 whole[:, 0:TILES * width].rearrange("p (t f) -> p t f", f=width)
                                 ).then_inc(sums_out, 16)

            sp.wait_ge(types_pad_set, 1)
            body, last = edge_views(type_8)
            sp.dma_start(t8_sb[0:REST, 0:COLS], body[0:REST, :]).then_inc(types_in, 16)
            sp.dma_start(t8_sb[REST:P - 1, 0:COLS], body[REST:P - 1, :]).then_inc(types_in, 16)
            sp.dma_start(t8_sb[P - 1:P, 0:LAST], last).then_inc(types_in, 16)

            sum_edges(0, scan0, 2 * D)

            def pair(i):
                for h in range(2):
                    sp.wait_ge(t1_sb, i * 2 + h + 1)
                    sp.dma_start(table1_v[:, tiles(i * 2 + h), :],
                                 t1_buf[:, h, :].rearrange("p (t f) -> p t f", t=GROUP)).then_inc(t1_out[h], 16)

            pair(0)
            with sp.Fori(1, GROUPS // 2) as i:
                pair(i)

            sum_edges(1, scan1, D)

            def pair(i):
                for h in range(2):
                    sp.wait_ge(out_set[h], i + 1)
                    sp.dma_start(out_v[:, tiles(i * 2 + h), :], out_buf[:, h, :, :]).then_inc(out_out[h], 16)

            pair(0)
            with sp.Fori(1, GROUPS // 2 - 1) as i:
                pair(i)
            sp.wait_ge(out_set[0], GROUPS // 2)
            sp.dma_start(out_v[:, tiles(GROUPS - 2), :], out_buf[:, 0, :, :]).then_inc(out_out[0], 16)
            sp.wait_ge(out_set[1], GROUPS // 2)
            sp.dma_start(out_v[:, TILES - GROUP:TILES - 1, :], out_buf[:, 1, 0:GROUP - 1, :]).then_inc(out_out[1], 16)
            sp.dma_start(out[(TILES - 1) * P:NODES, :], out_buf[0:TAIL, 1, GROUP - 1, :]).then_inc(out_out[1], 16)
            sp.wait_ge(out_out[0], 16 * (GROUPS // 2))
            sp.wait_ge(out_out[1], 16 * (GROUPS // 2 + 1))

        @block.gpsimd
        def _(pool):
            pool.memset(ident[:, :], 0.0)
            pool.memset(earlier[:, :], 1.0).then_inc(consts_set, 1)
            pool.wait_ge(consts_set, 1)
            pool.affine_select(out=ident[:, :], in_=ident[:, :], compare_op=ALU.not_equal, fill=1.0, base=0,
                               pattern=[[-1, P]], channel_multiplier=1)
            pool.affine_select(out=earlier[:, :], in_=earlier[:, :], compare_op=ALU.is_gt, fill=0.0, base=0,
                               pattern=[[1, P]], channel_multiplier=-1)
            pool.iota(less_key[:, :], pattern=[[-P, BLOCKS]], base=0, channel_multiplier=-1,
                      allow_small_or_imprecise_dtypes=True)
            pool.iota(node_id[:, :], pattern=[[P, TILES]], base=0, channel_multiplier=1)
            pool.iota(run_start[:, :], pattern=[[1, 1]], base=-1, channel_multiplier=COLS)
            pool.iota(iota_i[:, :], pattern=[[1, P]], base=0, channel_multiplier=0).then_inc(consts_set, 1)

            def gather(rows, table, index, width, landed):
                pool.sem_inc(gather_begun, 1)
                for k in range(width):
                    pool.indirect_dma_start(out=rows[:, k, :], out_offset=None, in_=table,
                                            in_offset=bass.IndirectOffsetOnAxis(ap=index[:, k:k + 1], axis=0)
                                            ).then_inc(landed, 16)

            pool.wait_ge(edges_in, EDGES_IN)
            pool.sem_inc(gather_begun, 1)
            for n in range(CHUNKS):
                for k in range(DUO):
                    at = n * CHUNK + layers[0].own + k
                    pool.indirect_dma_start(out=known[:, n * DUO + k, :], out_offset=None, in_=x,
                                            in_offset=bass.IndirectOffsetOnAxis(ap=src_sb[:, at:at + 1], axis=0)
                                            ).then_inc(known_in, 16)

            def add_carries(layer, scan, scan_out, width):
                for h in range(2):
                    pool.wait_ge(scan_out[h], 16 * PAIRS)
                pool.wait_ge(carry_set, layer + 1)
                pool.indirect_dma_start(out=scan, out_offset=bass.IndirectOffsetOnAxis(ap=fix_row[:, 0:1], axis=0),
                                        in_=carry[:, 0:width], in_offset=None, compute_op=ALU.add
                                        ).then_inc(fixed, 16)
                with out_of_order(pool):
                    pool.wait_ge(sums_out, 16 * (layer + 1))

            def pair(i):
                for h in range(2):
                    pool.wait_ge(idx0_set[h], i + 1)
                    wait_past(pool, rows0_used[h], i)
                    for k in range(4):
                        pool.wait_ge(t0_out[k], 16 * (TILES // 4 + (k >= 2)))
                    gather(rows0[:, h, :, :], table0, idx[:, h, :], layers[0].own, rows0_in[h])

            pair(0)
            with pool.Fori(1, PAIRS) as i:
                pair(i)
            add_carries(0, scan0, scan0_out, 2 * D)
            pool.wait_ge(late_in, LATE_IN)
            def pair(i):
                for h in range(2):
                    pool.wait_ge(group0_set[h], i + 1)
                    wait_past(pool, sums0_used, i * 2 + (h - 1))
                    pool.wait_ge(fixed, 16)
                    gather(sums0[:, h, :, :], scan0, group_row[:, h, :], GROUP, sums0_in[h])

            pair(0)
            with pool.Fori(1, GROUPS // 2) as i:
                pair(i)

            def pair(i):
                for h in range(2):
                    pool.wait_ge(idx1_set[h], i + 1)
                    wait_past(pool, scan1_set[h], i)
                    for half in range(2):
                        pool.wait_ge(t1_out[half], 16 * (GROUPS // 2))
                    gather(rows1[:, h, :, :], table1, idx[:, h, :], layers[1].own, rows1_in[h])

            pair(0)
            with pool.Fori(1, PAIRS) as i:
                pair(i)
            add_carries(1, scan1, scan1_out, D)
            def pair(i):
                for h in range(2):
                    pool.wait_ge(group1_set[h], i + 1)
                    wait_past(pool, m_set, i * 2 + (h - 1))
                    pool.wait_ge(fixed, 32)
                    gather(sums1[:, h, :, :], scan1, group_row[:, h, :], GROUP, sums1_in[h])

            pair(0)
            with pool.Fori(1, GROUPS // 2) as i:
                pair(i)

        @block.tensor
        def _(pe):
            pe.wait_ge(weights_in, WEIGHTS_IN)
            pe.matmul(ps_misc[0:RELS, 0:D * D], wcT[:, :], basis[:, :], start=True, stop=True).then_inc(mats_ps, 1)
            pe.wait_ge(wab_set, 1)
            pe.matmul(score_ps[0:D, 0:1], Ws_sb[:, :], WaT[:, 0:1], start=True, stop=True)
            for k in range(3):
                last = pe.matmul(score_ps[:, (k + 1) * D:(k + 2) * D], WaB[:, k, :], Ws_sb[:, :], start=True, stop=True)
            last.then_inc(scores_ps, 1)

            def transpose_x(t, h):
                pe.wait_ge(x_tile_set, t + 1)
                pe.transpose(xT_bank[h], x_tile[:, h, :, :].rearrange("p k f -> p (k f)"), ident_bf[:, :]
                             ).then_inc(xT_ps, 1)

            pe.wait_ge(x_parts_set, 1)
            pe.wait_ge(mats_sb, 1)
            transpose_x(0, 0)
            pe.wait_ge(stack_in, 16 * len(RIGHT_PARTS))
            def pair(i):
                for h in range(2):
                    wait_past(pe, xT_sb, i * 2 + h)
                    transpose_x(i * 2 + h + 1, 1 - h)
                    pe.wait_ge(xT_sb, i * 2 + h + 1)
                    wait_past(pe, t0_sb, i * 2 + (h - 1))
                    for b in range(BANKS):
                        last = pe.matmul(ps_table[h][:, b, 0:BW], xT[:, h, :], rel_stack[:, b * BW:(b + 1) * BW],
                                         start=True, stop=True)
                    last.then_inc(t0_ps, 1)

            pair(0)
            with pe.Fori(1, TILES // 2) as i:
                pair(i)

            pe.wait_ge(order_set, 1)
            pe.wait_ge(xT_sb, TILES + 1)
            pe.matmul(ps_misc[:, 3 * P:3 * P + 1], ones[:, :], ordered[:, 0:1], start=True, stop=True
                      ).then_inc(order_ps, 1)
            pe.wait_ge(flags_set, 1)
            for k in range(2):
                last = pe.matmul(ps_misc[0:2 * D, k * P:(k + 1) * P], flag_cols[:, k, :], ident[:, :],
                                 start=True, stop=True)
            last.then_inc(flags_ps, 1)

            pe.matmul(ps_hist[0:TILES, 0:P], zeros_bf[:, 0:TILES], zeros_bf[:, :], start=True, stop=False)

            def count_edges(i, q):
                pe.wait_ge(hot_set[q % 2], i * HOTS + q // 2 + 1)
                for k in range(min(HOT, CHUNK - q % HOTS * HOT)):
                    last = pe.matmul(ps_hist[0:TILES, 0:P], hot_hi[:, q % 2, k // 2, :, k % 2],
                                     hot_lo[:, q % 2, k // 2, :, k % 2],
                                     start=False, stop=False)
                last.then_inc(hot_used[q % 2], 1)

            def spread_quad(lay, m, parity, q):
                pe.wait_ge(keys_set[lay.n], m + 1)
                wait_past(pe, match_sb[lay.n], m * QUADS + q)
                for k in range(int(q < lay.known), 2):
                    for c in range(lay.widths[q]):
                        at = lay.starts[q] + c
                        last = pe.transpose(match_bank[:, k, c * P:(c + 1) * P],
                                            match_cols[:, parity, k, at:at + 1].to_broadcast([P, P]), ident_f16[:, :])
                last.then_inc(match_ps[lay.n], 1)

            def products(lay, m, parity, q, duo):
                quad = m * QUADS + q
                pe.wait_ge(match_set[lay.n], quad + 1)
                if lay.by_act < BLOCKS:
                    pe.wait_ge(match_rest, quad + 1)
                if isinstance(m, int) and m == 0 and q == 0:
                    pe.wait_ge(product_mats_set[lay.n], 1)
                    if lay.n == 1:
                        pe.wait_ge(node_parts_set, 1)
                        pe.wait_ge(t1_sb, GROUPS)
                columns = [(t, slice((duo * DUO + t) * P, (duo * DUO + t + 1) * P)) for t in range(DUO)]
                if q >= lay.known:
                    before = (m, q - 1) if q > lay.known else (m - 1, QUADS - 1)
                    wait_past(pe, products_used[lay.n], lay.done(*before, duo))
                    b = lay.half(parity, q)
                    for t, edges in columns:
                        for g in range(BLOCKS):
                            width = len(range(g, TILES, BLOCKS)) * D
                            for part in range(3):
                                pe.matmul(ps_table[duo][:, 0, t * BLOCK_W:t * BLOCK_W + width], hot_key[:, b, g, edges],
                                          node_parts[:, part, g:TILES:BLOCKS, :],
                                          start=(g == 0 and part == 0), stop=(g == BLOCKS - 1 and part == 2))
                    hot = hot_type[0:lay.strips, b, :]
                else:
                    hot = hot_known[:, :]
                before = (m, q - 1) if q > 0 and duo * DUO < lay.widths[q - 1] else (m - 1, QUADS - 1)
                wait_past(pe, products_used[lay.n], lay.done(*before, duo))
                for t, edges in columns:
                    for k, mats_part in enumerate(lay.mats):
                        last = pe.matmul(ps_table[duo][:, 1 + t, 0:lay.outs * D], hot[:, edges],
                                         mats_part, start=(k == 0), stop=(k == len(lay.mats) - 1))
                last.then_inc(products_ps[lay.n], 1)

            def chunk_by_products(lay, m, parity, last, between=lambda q: None):
                for q in range(QUADS):
                    if lay.known <= q < QUADS - 1:
                        spread_quad(lay, m, parity, q + 1)
                    if q == QUADS - 1 and not last:
                        spread_quad(lay, m + 1, 1 - parity, lay.known)
                    for duo in range(lay.widths[q] // DUO):
                        if lay.known and (q, duo) == (QUADS - 2, 1) and not last:
                            spread_quad(lay, m + 1, 1 - parity, 0)
                        products(lay, m, parity, q, duo)
                    between(q)

            for q in range(layers[0].known + 1):
                spread_quad(layers[0], 0, 0, q)
            chunk_by_products(layers[0], 0, 0, False)

            def pair(i, last=False):
                for h in range(2):
                    def counts(q):
                        for k in COUNT_WITH[q]:
                            count_edges(i, h * HOTS + k)

                    if last and h == 1:
                        for k in range(HOTS):
                            count_edges(i, h * HOTS + k)
                    else:
                        chunk_by_products(layers[0], i * 2 + (h + 1), (h + 1) % 2, last, counts)

            pair(0)
            with pe.Fori(1, PAIRS - 1) as i:
                pair(i)
            pair(PAIRS - 1, True)
            pe.matmul(ps_hist[0:TILES, 0:P], zeros_bf[:, 0:TILES], zeros_bf[:, :], start=False, stop=True
                      ).then_inc(hist_ps, 1)

            def carries(layer, width):
                pe.wait_ge(carry_step, 1 + 3 * layer)
                pe.transpose(ps_misc[0:width, 0:P], last_state[:, 0:width], ident[:, :]).then_inc(ends_ps, 1)
                pe.wait_ge(carry_step, 3 + 3 * layer)
                pe.transpose(ps_misc[:, P:P + width], carryT[0:width, :], ident[0:width, 0:width]).then_inc(carry_ps, 1)

            carries(0, 2 * D)

            pe.wait_ge(node_step, 2)
            pe.matmul(ps_misc[0:TILES, 2 * P:2 * P + 1], earlier[0:TILES, 0:TILES], node_end[:, P - 1:P],
                      start=True, stop=True).then_inc(offset_ps, 1)
            pe.wait_ge(node_step, 6)
            pe.transpose(ps_misc[:, 3 * P:3 * P + TILES], node_end[:, :], ident[0:TILES, 0:TILES]).then_inc(rows_ps, 1)

            def sum_edges(layer, width):
                def add(c):
                    pe.wait_ge(spread_set, c + (layer * COLS + 1))
                    for b, bank in enumerate(sum_banks):
                        cols = SUM_TILES * width
                        last = pe.matmul(bank[:, 0:cols], edge_lo[:, :], whole[:, b * cols:(b + 1) * cols],
                                         start=isinstance(c, int) and c == 0, stop=isinstance(c, int) and c == COLS - 1)
                    last.then_inc(summed, 1)

                with out_of_order(pe):
                    add(0)
                    with pe.Fori(1, COLS - 1) as c:
                        add(c)
                    add(COLS - 1)

            sum_edges(0, 2 * D)

            for q in range(layers[1].known + 1):
                spread_quad(layers[1], 0, 0, q)

            def turn(h, lo, hi):
                for k in range(GROUP):
                    bank = ps_misc if k < 4 else ps_hist
                    last = pe.transpose(bank[0:hi - lo, (k % 4) * P:(k % 4 + 1) * P],
                                        cat[:, h, k, lo:hi], ident[:, :])
                return last

            pe.wait_ge(late_in, LATE_IN)
            def pair(i):
                for h in range(2):
                    pe.wait_ge(y_set, i * 2 + h + 1)
                    turn(h, D, 2 * D).then_inc(yT_ps, 1)
                    pe.wait_ge(yT_sb, i * 2 + h + 1)
                    wait_past(pe, t1_sb, i * 2 + h)
                    for k in range(GROUP):
                        last = pe.matmul(ps_table[h][:, k // 4, (k % 4) * P:(k % 4 + 1) * P],
                                         catT[0:D, k * P:(k + 1) * P], type_cols, start=True, stop=True)
                    last.then_inc(t1_ps, 1)

            pair(0)
            with pe.Fori(1, GROUPS // 2) as i:
                pair(i)

            chunk_by_products(layers[1], 0, 0, False)

            def pair(i, last=False):
                for h in range(2):
                    if not (last and h == 1):
                        chunk_by_products(layers[1], i * 2 + (h + 1), (h + 1) % 2, last)

            pair(0)
            with pe.Fori(1, PAIRS - 1) as i:
                pair(i)
            pair(PAIRS - 1, True)

            carries(1, D)
            sum_edges(1, D)

            def pair(i):
                for h in range(2):
                    pe.wait_ge(m_set, i * 2 + h + 1)
                    turn(h, 0, 2 * D).then_inc(mT_ps, 1)
                    pe.wait_ge(mT_sb, i * 2 + h + 1)
                    wait_past(pe, pre_set, i * 2 + h)
                    for k in range(GROUP):
                        last = pe.matmul(ps_table[h][:, 0, k * 4 * D:(k + 1) * 4 * D],
                                         catT[:, k * P:(k + 1) * P], gate_w[:, :], start=True, stop=True)
                    last.then_inc(gates_ps, 1)

            pair(0)
            with pe.Fori(1, GROUPS // 2) as i:
                pair(i)

        @block.scalar
        def _(act):
            with nc.allow_non_contiguous_dma(reason="one column"):
                act.wait_ge(pads_set, 1)
                act.wait_ge(rel_in, 32)
                for a, to, at in ((src, src_sb, 0), (type_90, t90_sb, 0), (dst, dst_sb, 1)):
                    body, last = edge_views(a)
                    act.dma_start(to[0:REST, at:at + COLS], body[0:REST, :]).then_inc(edges_in, 16)
                    act.dma_start(to[REST:P - 1, at:at + COLS], body[REST:P - 1, :]).then_inc(edges_in, 16)
                    act.dma_start(to[P - 1:P, at:at + LAST], last).then_inc(edges_in, 16)
                act.dma_start(dst_before[1:P, :], edge_views(dst)[0][:, COLS - 1:COLS]).then_inc(edges_in, 16)

            act.wait_ge(rel_parts_set, 1)
            for k in range(1, len(RIGHT_PARTS), 2):
                act.dma_start(rel_stack[k * D:(k + 1) * D, :], rel_parts[:, RIGHT_PARTS[k], :]).then_inc(stack_in, 16)

            act.wait_ge(xT_ps, 1)
            act.copy(xT[:, 0, :], xT_bank[0]).then_inc(xT_sb, 1)

            def table_tile(t, h, k, stored):
                act.wait_ge(xT_ps, t + 2)
                act.copy(xT[:, 1 - h, :], xT_bank[1 - h]).then_inc(xT_sb, 1)
                act.wait_ge(t0_ps, t + 1)
                wait_past(act, t0_out[k], stored * 16)
                act.copy(t0_tiles[k].rearrange("p (b c) -> p b c", b=BANKS), ps_table[h][:, :, 0:BW]).then_inc(t0_sb, 1)

            def four(i):
                for k in range(4):
                    table_tile(i * 4 + (k + 2), k % 2, k, i + (k >= 2))

            for k in range(2):
                table_tile(k, k, k + 2, 0)
            four(0)
            with act.Fori(1, TILES // 4) as i:
                four(i)

            def one_hot(lay, m, parity, q):
                quad = m * QUADS + q
                own = slice(0, lay.strips)
                act.wait_ge(match_ps[lay.n], quad + 1)
                if q < lay.known:
                    wait_past(act, products_ps[lay.n], lay.done(m - 1, q, 0))
                    types, last_block = hot_known[:, :], 0
                else:
                    before = (m, q - 2) if q - 2 >= lay.known else (m - 1, q - 2 + QUADS - lay.known)
                    wait_past(act, products_ps[lay.n], lay.done(*before, 1))
                    b = lay.half(parity, q)
                    types, last_block = hot_type[own, b, :], lay.by_act
                    for g in range(BLOCKS):
                        act.activation(hot_key[:, b, g, :], match_bank[:, 0, :], ACT.Abs, bias=less_key[:, g:g + 1])
                act.activation(types, match_bank[own, 1, 0:lay.widths[q] * P], ACT.Abs, bias=less_type[own, lay.n:lay.n + 1]
                               ).then_inc(match_sb[lay.n], 1)
                act.wait_ge(match_sb[lay.n], quad + 1)
                if last_block:
                    last = act.activation(hot_key[:, b, 0:last_block, :], hot_key[:, b, 0:last_block, :], ACT.Relu,
                                          bias=ones[:, 0:1], scale=-1.0)
                if lay.by_act == BLOCKS:
                    last = act.activation(types, types, ACT.Relu, bias=ones[own, 0:1], scale=-1.0)
                last.then_inc(match_set[lay.n], 1)

            def chunks_out(lay, stored, scan_set, scan_out):
                ahead = lay.known + 1
                for q in range(1 - lay.known, QUADS):
                    one_hot(lay, 0, 0, q)
                for q in range(ahead):
                    one_hot(lay, 1, 1, q)

                def pair(i, last=False):
                    for h in range(2):
                        m = i * 2 + (h + 1)
                        if not (last and h == 1):
                            for q in range(ahead, QUADS):
                                one_hot(lay, m, 1 - h, q)
                        if not last:
                            for q in range(ahead):
                                one_hot(lay, m + 1, h, q)
                        act.wait_ge(scan_set[h], i + 1)
                        act.dma_start(stored[:, col(i * 2 + h), :], scanned[:, h, :, 0:stored.shape[2]]
                                      ).then_inc(scan_out[h], 16)

                pair(0)
                with act.Fori(1, PAIRS - 1) as i:
                    pair(i)
                pair(PAIRS - 1, True)

            chunks_out(layers[0], scan0_v, scan0_set, scan0_out)

            one_hot(layers[1], 0, 0, 0)

            def pair(i):
                for h in range(2):
                    act.wait_ge(var_set, i * 2 + h + 1)
                    act.activation(std[:, :], stat[:, 3, :], ACT.Sqrt).then_inc(std_set, 1)
                    act.wait_ge(y_set, i * 2 + h + 1)
                    act.copy(state[:, tiles(i * 2 + h), :], cat[:, h, :, D:2 * D]).then_inc(state_set, 1)
                    act.wait_ge(yT_ps, i * 2 + h + 1)
                    act.copy(catT[0:D, 0:4 * P], ps_misc[0:D, :])
                    act.copy(catT[0:D, 4 * P:GROUP * P], ps_hist[0:D, 0:(GROUP - 4) * P]).then_inc(yT_sb, 1)
                    act.wait_ge(t1_ps, i * 2 + h + 1)
                    wait_past(act, t1_out[h], i * 16)
                    act.copy(t1_buf[:, h, 0:4 * P], ps_table[h][:, 0, :])
                    act.copy(t1_buf[:, h, 4 * P:GROUP * P], ps_table[h][:, 1, 0:(GROUP - 4) * P]).then_inc(t1_sb, 1)

            pair(0)
            with act.Fori(1, GROUPS // 2) as i:
                pair(i)

            chunks_out(layers[1], scan1_v, scan1_set, scan1_out)

            def rows_out(g):
                act.wait_ge(mT_ps, g + 1)
                act.copy(catT[0:2 * D, 0:4 * P], ps_misc[0:2 * D, :])
                act.copy(catT[0:2 * D, 4 * P:GROUP * P], ps_hist[0:2 * D, 0:(GROUP - 4) * P]).then_inc(mT_sb, 1)

            def pair(i, last=False):
                for h in range(2):
                    g = i * 2 + h
                    act.wait_ge(gates_ps, g + 1)
                    wait_past(act, gates_used, g)
                    act.activation(gates[:, :, :], gate_view(h)[:, :, 0:2 * D], ACT.Sigmoid).then_inc(gates_set, 1)
                    act.wait_ge(pre_set, g + 1)
                    act.activation(cand[:, :, :], tmp[:, :, :], ACT.Tanh).then_inc(cand_set, 1)
                    if not (last and h == 1):
                        rows_out(g + 1)
                    act.wait_ge(var_set, g + (GROUPS + 1))
                    act.activation(std[:, :], stat[:, 3, :], ACT.Sqrt).then_inc(std_set, 1)

            rows_out(0)
            pair(0)
            with act.Fori(1, GROUPS // 2 - 1) as i:
                pair(i)
            pair(GROUPS // 2 - 1, True)

        @block.vector
        def _(dve):
            prep_n = [0]

            def step(ins):
                prep_n[0] += 1
                ins.then_inc(prep, 1)
                dve.wait_ge(prep, prep_n[0])

            dve.memset(x_sb[:, TILES - 1, :], 0.0)
            dve.memset(node_parts[:, :, TILES:TILES + 2, :], 0.0)
            dve.memset(emb_sb[:, :], 0.0)
            def pad_edges(a):
                dve.memset(a[96:P, LAST:COLS], 0)
                return dve.memset(a[:, COLS:COLS + 2 * CHUNK], 0)

            for a in (src_sb, t90_sb):
                pad_edges(a)
            dve.memset(dst_sb[96:P, 1 + LAST:1 + COLS], NODES)
            dve.memset(dst_sb[:, 0:1], -1)
            dve.memset(dst_before[:, :], -1)
            dve.memset(gate_w[:, :], 0.0)
            dve.memset(zero_row[:, :], 0.0)
            dve.memset(zeros_bf[:, :], 0.0)
            dve.memset(ones[:, :], 1.0)
            dve.memset(catT[2 * D:2 * D + 2, :], 1.0)
            dve.memset(node_row[:, TILES:TILES + 2 * GROUP], 0)
            dve.memset(pass_on[:, 0:1], 0.0)
            dve.memset(endsT[:, :], 0.0).then_inc(pads_set, 1)

            def split(value, rest, parts):
                step(dve.tensor_copy(parts[0], value))
                step(dve.tensor_tensor(rest, value, parts[0], ALU.subtract))
                step(dve.tensor_copy(parts[1], rest))
                return dve.tensor_tensor(parts[2], rest, parts[1], ALU.subtract)

            def split_nodes(nodes):
                return split(nodes, whole[:, 0:TILES * D].rearrange("p (t f) -> p t f", f=D),
                             [node_parts[:, k, 0:TILES, :] for k in range(3)])

            dve.wait_ge(weights_in, WEIGHTS_IN)
            for k in range(3):
                last = dve.tensor_copy(WaB[:, k, :], WaT[:, k:k + 1].to_broadcast([D, P]))
            last.then_inc(wab_set, 1)
            dve.wait_ge(mats_ps, 1)
            dve.tensor_copy(mats[:, :], ps_misc[0:RELS, 0:D * D]).then_inc(mats_sb, 1)
            dve.wait_ge(consts_set, 2)
            dve.tensor_copy(iota_bf[:, :, :], iota_i[:, :].unsqueeze(2).to_broadcast([P, P, 2]))
            dve.tensor_copy(ident_bf[:, :], ident[:, :])
            dve.tensor_copy(ident_f16[:, :], ident[:, :])
            dve.tensor_copy(less_type[:, 0:1], less_key[:, 0:1])
            step(dve.tensor_scalar(type_i[:, :], node_id[:, 0:1], STRIP - 1, None, ALU.bitwise_and))
            dve.tensor_scalar(less_type[:, 1:2], type_i[:, :], -1.0, None, ALU.mult)
            dve.wait_ge(x_in, X_IN)
            split_nodes(x_sb[:, :, :]).then_inc(x_parts_set, 1)
            def stack_tile(t, h):
                for part in range(3):
                    at, count = LEFT_PARTS.index(part), LEFT_PARTS.count(part)
                    last = dve.tensor_copy(x_tile[:, h, at:at + count, :],
                                            node_parts[:, part, bass.ds(t, 1), :].to_broadcast([P, count, D]))
                last.then_inc(x_tile_set, 1)

            dve.wait_ge(x_parts_set, 1)
            for h in range(2):
                stack_tile(h, h)

            dve.wait_ge(scores_ps, 1)
            dve.tensor_copy(he_w[:, :], score_ps[:, 2 * D:3 * D])
            dve.tensor_copy(dst_w[:, :], score_ps[:, 3 * D:4 * D])
            dve.tensor_copy(rel_rows[:, :, D:RD], score_ps[0:RELS, D:2 * D].unsqueeze(2))
            step(dve.tensor_copy(rel_w[:, :, D:RD], score_ps[0:D, 0:1].unsqueeze(1).to_broadcast([D, RELS, 1])))
            dve.wait_ge(rel_in, 32)
            dve.wait_ge(x_parts_set, 1)
            split(rel_w[:, :, :].rearrange("i r f -> i (r f)"), whole[0:D, 0:RW],
                  [rel_parts[:, k, :] for k in range(3)]).then_inc(rel_parts_set, 1)

            def index(lay, n, h, done):
                edges = bass.ds(n * CHUNK, lay.own)
                dve.scalar_tensor_tensor(out=idx[:, h, 0:lay.own], in0=src_sb[:, edges], scalar=float(lay.kinds),
                                         in1=lay.edge_types[:, edges], op0=ALU.mult, op1=ALU.add).then_inc(done[h], 1)

            dve.wait_ge(edges_in, EDGES_IN)
            for h in range(2):
                index(layers[0], h, h, idx0_set)

            def pair(i):
                for h in range(2):
                    dve.wait_ge(xT_ps, i * 2 + h + 1)
                    stack_tile(i * 2 + h + 2, h)

            pair(0)
            with dve.Fori(1, TILES // 2) as i:
                pair(i)

            dve.wait_ge(rel_parts_set, 1)
            split(rel_rows[:, :, :].rearrange("r i o -> r o i"),
                  whole[0:RELS, 0:RD * D].rearrange("r (o i) -> r o i", i=D),
                  [rel_mats[:, k, :, :] for k in range(3)]).then_inc(product_mats_set[0], 1)
            dve.wait_ge(product_mats_set[0], 1)

            step(dve.tensor_tensor(state[:, :, :], x_sb[:, 0:TILES, :],
                                   dst_w[:, :].unsqueeze(1).to_broadcast([P, TILES, D]), ALU.mult))
            dve.tensor_reduce(dst_score[:, :], state[:, :, :], AX, ALU.add)

            step(dve.tensor_tensor(whole[:, 0:COLS - 1], dst_sb[:, 2:1 + COLS], dst_sb[:, 1:COLS], ALU.is_ge))
            step(dve.tensor_reduce(ordered[:, 1:2], whole[:, 0:COLS - 1], AX, ALU.add))
            dve.tensor_scalar(ordered[:, 2:3], ordered[:, 1:2], float(COLS - 1), None, ALU.is_equal)
            step(dve.tensor_tensor(ordered[:, 3:4], dst_sb[:, 1:2], dst_before[:, :], ALU.is_ge))
            dve.tensor_tensor(ordered[:, 0:1], ordered[:, 2:3], ordered[:, 3:4], ALU.mult).then_inc(order_set, 1)
            for k in range(4):
                dve.wait_ge(t0_out[k], 16 * (TILES // 4 + (k >= 2)))
            step(dve.memset(scanned[:, 1, :, :], 0.0))
            dve.wait_ge(order_ps, 1)
            step(dve.tensor_scalar(ordered[:, 1:2], ps_misc[:, 3 * P:3 * P + 1], float(P), None, ALU.is_lt))
            dve.tensor_copy(disorder[:, :], ordered[0:1, 1:2]).then_inc(order_flag, 1)
            step(dve.tensor_scalar(ordered[:, 2:3], ordered[:, 1:2], 0.5, None, ALU.mult))

            step(dve.tensor_copy(first[:, 0:1], dst_sb[:, 1:2]))
            step(dve.tensor_scalar(whole[:, :], dst_sb[:, 1:1 + COLS], first[:, 0:1], None, ALU.is_equal))
            step(dve.tensor_reduce(first[:, 1:2], whole[:, :], AX, ALU.add))
            dve.tensor_tensor(fix_row[:, :], run_start[:, :], first[:, 1:2], ALU.add)
            dve.tensor_scalar(first[:, 2:3], first[:, 1:2], float(COLS), None, ALU.is_equal)
            step(dve.scalar_tensor_tensor(out=first[:, 3:4], in0=dst_sb[:, 1:2], scalar=ordered[:, 2:3],
                                          in1=dst_before[:, :], op0=ALU.add, op1=ALU.is_equal))
            dve.tensor_copy(flag_cols[:, :, :], first[:, 2:4].unsqueeze(2).to_broadcast([P, 2, 2 * D])
                            ).then_inc(flags_set, 1)
            dve.wait_ge(flags_ps, 1)
            step(dve.tensor_copy(take_in[:, :], ps_misc[0:2 * D, P:2 * P]))
            step(dve.tensor_tensor(pass_on[:, 1:P], ps_misc[0:2 * D, 0:P - 1], take_in[:, 1:P], ALU.mult))

            def continues(n):
                return dve.scalar_tensor_tensor(out=cont[:, :], in0=dst_sb[:, bass.ds(n * CHUNK + 1, CHUNK)],
                                                scalar=ordered[:, 2:3], in1=dst_sb[:, col(n)],
                                                op0=ALU.add, op1=ALU.is_equal)

            def scan(h, at, f, messages):
                return dve.tensor_tensor_scan(scanned[:, h, :, at + f], cont[:, :], messages[:, :, f],
                                              scanned[:, 1 - h, CHUNK - 1, at + f:at + f + 1], ALU.mult, ALU.add)

            ROW_STEPS = 2 * QUAD // DUO

            def keys(lay, m, parity, base):
                edges = bass.ds(m * CHUNK + lay.own, lay.share)
                own = slice(0, lay.share)
                dve.tensor_scalar(match_i[:, 0, own], src_sb[:, edges], BLOCKS * P - 1, None, ALU.bitwise_and)
                dve.tensor_scalar(match_i[:, 1, own], src_sb[:, edges], (BLOCKS * P).bit_length() - 1, None,
                                  ALU.logical_shift_right).then_inc(match_step[lay.n], 1)
                dve.wait_ge(match_step[lay.n], base + 1)
                wait_past(dve, match_ps[lay.n], (m - 1) * QUADS)
                dve.tensor_copy(match_cols[:, parity, 0, own], match_i[:, 0, own])
                dve.tensor_copy(match_cols[:, parity, 1, own], lay.edge_types[:, edges])
                dve.tensor_tensor(hot_tile[:, parity, own, :],
                                  match_i[:, 1, own].unsqueeze(2).to_broadcast([P, lay.share, BLOCK_TILES]),
                                  iota_i[:, 0:BLOCK_TILES].unsqueeze(1).to_broadcast([P, lay.share, BLOCK_TILES]),
                                  ALU.is_equal).then_inc(keys_set[lay.n], 1)

            def make_rows(lay, m, half, q, base, between):
                for duo in range(lay.widths[q] // DUO):
                    own = lay.starts[q] + duo * DUO
                    if duo == 1:
                        between(q)

                    def done(k):
                        dve.wait_ge(match_step[lay.n], base + (2 * duo + k))

                    dve.wait_ge(products_ps[lay.n], lay.done(m, q, duo))
                    if q < lay.known:
                        sources = known[:, bass.ds(m * DUO, DUO), :]
                    else:
                        sources = source[:, :, :]
                        dve.tensor_tensor(picked[:, :, :, :],
                                          ps_table[duo][:, 0, 0:DUO * BLOCK_W].rearrange("p (t j f) -> p t j f", t=DUO, f=D),
                                          hot_tile[:, half, own:own + DUO, :].unsqueeze(3).to_broadcast(
                                              [P, DUO, BLOCK_TILES, D]), ALU.mult).then_inc(match_step[lay.n], 1)
                        done(1)
                        dve.tensor_reduce(source[:, :, :], picked[:, :, :, :].rearrange("p t j f -> p t f j"), AX, ALU.add
                                          ).then_inc(match_step[lay.n], 1)
                        done(2)
                    wait_past(dve, rows_made[lay.n], m * lay.duos + own // DUO)
                    dve.tensor_tensor(by_in[:, :, 0:lay.outs, :],
                                      ps_table[duo][:, 1:1 + DUO, 0:lay.outs * D].rearrange("p t (o i) -> p t o i", i=D),
                                      sources.unsqueeze(2).to_broadcast([P, DUO, lay.outs, D]), ALU.mult
                                      ).then_inc(products_used[lay.n], 1)
                    dve.wait_ge(products_used[lay.n], lay.done(m, q, duo))
                    dve.tensor_reduce(lay.rows[:, half, lay.own + own:lay.own + own + DUO, 0:lay.outs],
                                      by_in[:, :, 0:lay.outs, :], AX, ALU.add).then_inc(rows_made[lay.n], 1)

            def rest_one_hot(lay, quad, b):
                if lay.by_act < BLOCKS:
                    dve.wait_ge(match_sb[lay.n], quad + 1)
                    rest, own = slice(lay.by_act, BLOCKS), slice(0, lay.strips)
                    dve.tensor_scalar(hot_key[:, b, rest, :], hot_key[:, b, rest, :], 0.0, None, ALU.is_equal)
                    dve.tensor_scalar(hot_type[own, b, :], hot_type[own, b, :], 0.0, None, ALU.is_equal
                                      ).then_inc(match_rest, 1)

            def chunk_rows(lay, m, parity, last, between=lambda q: None):
                steps = m * ((QUADS - lay.known) * ROW_STEPS + 1) + 1
                for q in range(QUADS):
                    base = steps + (q - lay.known) * ROW_STEPS
                    if q == QUADS - 3 and not last:
                        keys(lay, m + 1, 1 - parity, base)
                    if q >= QUADS - 3 and not last:
                        base = base + 1
                    if q + 1 < QUADS or not last:
                        rest_one_hot(lay, m * QUADS + (q + 1), lay.half(parity, q + 1))
                    make_rows(lay, m, parity, q, base, between)
                    if q < lay.known:
                        between(q)

            STEPS = 5

            def chunk_done(i, h, k):
                dve.wait_ge(chunk_step, i * (2 * STEPS) + (h * STEPS + k))

            def target_parts(i, h):
                targets = dst_sb[:, bass.ds((i * 2 + h) * CHUNK + 1, CHUNK)]
                dve.tensor_scalar(dst_lo_i[:, :], targets, P - 1, None, ALU.bitwise_and)
                dve.tensor_scalar(dst_hi_i[:, :], targets, P.bit_length() - 1, None, ALU.logical_shift_right
                                  ).then_inc(chunk_step, 1)
                chunk_done(i, h, 1)
                dve.tensor_copy(dst_lo[:, :], dst_lo_i[:, :])
                dve.tensor_copy(dst_hi[:, :], dst_hi_i[:, :]).then_inc(chunk_step, 1)
                chunk_done(i, h, 2)

            def target_hots(i, h, q):
                b = (h * HOTS + q) % 2
                wait_past(dve, hot_used[b], i * HOTS + (h * HOTS + q) // 2)
                edges = slice(q * HOT, min((q + 1) * HOT, CHUNK))
                twos = (edges.stop - edges.start) // 2
                for hot, part, width in ((hot_lo, dst_lo, P), (hot_hi, dst_hi, TILES)):
                    all_of = [P, twos, width, 2]
                    last = dve.tensor_tensor(hot[:, b, 0:twos, :, :],
                                             part[:, edges].rearrange("p (c e) -> p c e", e=2).unsqueeze(2).to_broadcast(all_of),
                                             iota_bf[:, 0:width, :].unsqueeze(1).to_broadcast(all_of), ALU.is_equal)
                last.then_inc(hot_set[b], 1)

            def edge_scores(i, h):
                continues(i * 2 + h)
                dve.wait_ge(he_in[h], i * HE_IN + HE_IN)
                dve.tensor_tensor(he_dot[:, :, :], he[:, h, :, :],
                                  he_w[:, :].unsqueeze(1).to_broadcast([P, CHUNK, D]), ALU.mult).then_inc(chunk_step, 1)
                chunk_done(i, h, 3)
                dve.tensor_reduce(score[:, :], he_dot[:, :, :], AX, ALU.add).then_inc(he_used[h], 1)

            def weigh_messages(i, h):
                n = i * 2 + h
                dve.wait_ge(he_used[h], i + 1)
                dve.wait_ge(rows_made[0], n * layers[0].duos + layers[0].duos)
                dve.wait_ge(rows0_in[h], i * (16 * layers[0].own) + 16 * layers[0].own)
                index(layers[0], n + 2, h, idx0_set)
                dve.tensor_tensor(score[:, :], score[:, :], rows0[:, h, :, D], ALU.add).then_inc(chunk_step, 1)
                chunk_done(i, h, 4)
                dve.tensor_tensor(weighted[:, :, :], rows0[:, h, :, 0:D],
                                  score[:, :].unsqueeze(2).to_broadcast([P, CHUNK, D]), ALU.mult
                                  ).then_inc(chunk_step, 1)
                wait_past(dve, scan0_out[h], i * 16)
                chunk_done(i, h, 5)

            def scan_some(h, some):
                for k in some:
                    last = scan(h, D, k, rows0[:, h, :, :]) if k < D else scan(h, 0, k - D, weighted)
                    if k == D - 1:
                        last.then_inc(rows0_used[h], 1)
                    if k == 2 * D - 1:
                        last.then_inc(scan0_set[h], 1)

            SCAN_WITH = (range(0), range(4), range(4, 12), range(12, 24), range(24, 2 * D))

            def pair(i, last=False):
                for h in range(2):
                    before = (HOTS if h == 0 else 2 * HOTS) - 1 - HOTS

                    def with_quad(q):
                        if q == 0:
                            wait_past(dve, scan0_set[1 - h], i + h)
                            wait_past(dve, hot_set[before % 2], i * HOTS + before // 2 + 1)
                            target_parts(i, h)
                            edge_scores(i, h)
                        if q == 1:
                            weigh_messages(i, h)
                        scan_some(h, SCAN_WITH[q])
                        if not (last and h == 1):
                            for k in HOT_WITH[q]:
                                target_hots(i, h, k)

                    if last and h == 1:
                        with_quad(0)
                        for k in range(HOTS):
                            target_hots(i, h, k)
                        for q in range(1, QUADS):
                            with_quad(q)
                    else:
                        chunk_rows(layers[0], i * 2 + (h + 1), 1 - h, last, with_quad)

            dve.wait_ge(known_in, 16 * CHUNKS * DUO)
            keys(layers[0], 0, 0, 0)
            rest_one_hot(layers[0], 0, 0)
            chunk_rows(layers[0], 0, 0, False)
            pair(0)
            with dve.Fori(1, PAIRS - 1) as i:
                pair(i)
            pair(PAIRS - 1, True)

            pad_edges(t8_sb).then_inc(types_pad_set, 1)

            def carries(layer, width, all_scanned):
                dve.wait_ge(all_scanned, PAIRS)
                dve.tensor_copy(last_state[:, 0:width], scanned[:, 1, CHUNK - 1, 0:width]).then_inc(carry_step, 1)
                dve.wait_ge(ends_ps, layer + 1)
                dve.tensor_tensor(endsT[0:width, 1:P], ps_misc[0:width, 0:P - 1], take_in[0:width, 1:P], ALU.mult
                                  ).then_inc(carry_step, 1)
                dve.wait_ge(carry_step, 2 + 3 * layer)
                dve.tensor_tensor_scan(carryT[0:width, :], pass_on[0:width, :], endsT[0:width, :], 0.0,
                                       ALU.mult, ALU.add).then_inc(carry_step, 1)
                dve.wait_ge(carry_ps, layer + 1)
                dve.tensor_copy(carry[:, 0:width], ps_misc[:, P:P + width]).then_inc(carry_set, 1)

            carries(0, 2 * D, scan0_set[1])

            dve.wait_ge(hist_ps, 1)
            dve.tensor_copy(degree[:, :], ps_hist[0:TILES, 0:P]).then_inc(node_step, 1)
            dve.wait_ge(node_step, 1)
            dve.tensor_tensor_scan(node_end[:, :], ones[0:TILES, :], degree[:, :], 0.0, ALU.mult, ALU.add
                                   ).then_inc(node_step, 1)
            dve.wait_ge(node_step, 2)
            dve.tensor_scalar(degree[:, :], degree[:, :], 0.0, None, ALU.is_gt).then_inc(node_step, 1)
            dve.wait_ge(offset_ps, 1)
            dve.tensor_scalar(node_end[:, :], node_end[:, :], ps_misc[0:TILES, 2 * P:2 * P + 1], float(-1 - ROWS),
                              ALU.add, ALU.add).then_inc(node_step, 1)
            dve.wait_ge(node_step, 4)
            dve.tensor_tensor(node_end[:, :], node_end[:, :], degree[:, :], ALU.mult).then_inc(node_step, 1)
            dve.wait_ge(node_step, 5)
            dve.tensor_scalar(node_end[:, :], node_end[:, :], float(ROWS), None, ALU.add).then_inc(node_step, 1)
            dve.wait_ge(rows_ps, 1)
            dve.tensor_copy(node_row[:, 0:TILES], ps_misc[:, 3 * P:3 * P + TILES]).then_inc(node_step, 1)
            dve.wait_ge(node_step, 7)

            def sum_edges(layer, width):
                EDGE_STEPS = 3

                def spread(c):
                    def done(k):
                        dve.wait_ge(edge_step, c * EDGE_STEPS + (layer * COLS * EDGE_STEPS + k))

                    target = dst_sb[:, bass.ds(c + 1, 1)]
                    wait_past(dve, summed, c + layer * COLS)
                    dve.tensor_scalar(edge_part_i[:, 0:1], target, P - 1, None, ALU.bitwise_and)
                    dve.tensor_scalar(edge_part_i[:, 1:2], target, P.bit_length() - 1, None,
                                      ALU.logical_shift_right).then_inc(edge_step, 1)
                    done(1)
                    dve.tensor_copy(edge_part[:, :], edge_part_i[:, :]).then_inc(edge_step, 1)
                    done(2)
                    dve.tensor_scalar(edge_lo[:, :], iota_i[:, :], edge_part[:, 0:1], None, ALU.is_equal)
                    dve.tensor_scalar(edge_hi[:, :], iota_i[:, 0:TILES], edge_part[:, 1:2], None, ALU.is_equal
                                      ).then_inc(edge_step, 1)
                    done(3)
                    dve.wait_ge(edge_in, c * 16 + 16 * (layer * COLS + 1))
                    dve.tensor_tensor(whole[:, 0:TILES * width].rearrange("p (t f) -> p t f", f=width),
                                      edge_hi[:, :].unsqueeze(2).to_broadcast([P, TILES, width]),
                                      edge_row[:, 0:width].unsqueeze(1).to_broadcast([P, TILES, width]), ALU.mult
                                      ).then_inc(spread_set, 1)

                with out_of_order(dve):
                    spread(0)
                    with dve.Fori(1, COLS) as c:
                        spread(c)
                    dve.wait_ge(summed, (layer + 1) * COLS)
                    cols = SUM_TILES * width
                    for b, bank in enumerate(sum_banks):
                        last = dve.tensor_copy(whole[:, b * cols:(b + 1) * cols], bank[:, 0:cols])
                    last.then_inc(sums_sb, 1)
                    dve.tensor_copy(node_row[:, 0:TILES], node_id[:, :]).then_inc(node_step, 1)
                    dve.wait_ge(node_step, 8 + layer)

            sum_edges(0, 2 * D)

            def group_rows(g, h, done):
                dve.tensor_copy(group_row[:, h, :], node_row[:, tiles(g)]).then_inc(done[h], 1)

            for h in range(2):
                group_rows(h, h, group0_set)

            dve.wait_ge(late_in, LATE_IN)
            type_parts = [hot_key[0:3 * STRIP, 0, k, 0:D * D] for k in range(3)]
            step(split(emb_sb[:, :], by_in[0:3 * STRIP, 0, 0:D, :].rearrange("p o i -> p (o i)"), type_parts))
            for k in range(3):
                own = slice(k * STRIP, (k + 1) * STRIP)
                last = dve.tensor_copy(type_mats[own, :], hot_key[own, 0, k, 0:D * D])
            last.then_inc(product_mats_set[1], 1)
            dve.wait_ge(product_mats_set[1], 1)
            dve.wait_ge(types_in, 48)
            for h in range(2):
                index(layers[1], h, h, idx1_set)
            keys(layers[1], 0, 0, 0)
            rest_one_hot(layers[1], 0, 0)

            LN_STEPS = 6

            def layernorm(done, group, result):
                def bc(s):
                    return s.unsqueeze(2).to_broadcast([P, GROUP, D])

                dve.tensor_reduce(stat[:, 0, :], val[:, :, :], AX, ALU.add).then_inc(ln_step, 1)
                done(1)
                dve.tensor_scalar(stat[:, 1, :], stat[:, 0, :], -1.0 / D, None, ALU.mult).then_inc(ln_step, 1)
                done(2)
                dve.tensor_tensor(tmp[:, :, :], val[:, :, :], bc(stat[:, 1, :]), ALU.add).then_inc(ln_step, 1)
                done(3)
                dve.tensor_tensor(val[:, :, :], tmp[:, :, :], tmp[:, :, :], ALU.mult).then_inc(ln_step, 1)
                done(4)
                dve.tensor_reduce(stat[:, 2, :], val[:, :, :], AX, ALU.add).then_inc(ln_step, 1)
                done(5)
                dve.tensor_scalar(stat[:, 3, :], stat[:, 2, :], 1.0 / D, EPS, ALU.mult, ALU.add).then_inc(var_set, 1)
                dve.wait_ge(std_set, group + 1)
                dve.reciprocal(stat[:, 0, :], std[:, :]).then_inc(ln_step, 1)
                done(6)
                return dve.tensor_tensor(result, tmp[:, :, :], bc(stat[:, 0, :]), ALU.mult)

            PER0 = 2 + LN_STEPS
            def pair(i):
                for h in range(2):
                    g = i * 2 + h

                    def done(k):
                        dve.wait_ge(ln_step, i * (2 * PER0) + (h * PER0 + k))

                    dve.wait_ge(sums0_in[h], i * SUMS_IN + SUMS_IN)
                    group_rows(g + 2, h, group0_set)
                    wait_past(dve, y_set, g)
                    dve.tensor_tensor(tmp[:, :, :], sums0[:, h, :, D:2 * D],
                                      dst_score[:, tiles(g)].unsqueeze(2).to_broadcast([P, GROUP, D]), ALU.mult
                                      ).then_inc(ln_step, 1)
                    done(1)
                    dve.tensor_tensor(tmp[:, :, :], tmp[:, :, :], sums0[:, h, :, 0:D], ALU.add).then_inc(sums0_used, 1)
                    dve.wait_ge(sums0_used, g + 1)
                    dve.tensor_tensor(val[:, :, :], tmp[:, :, :], x_sb[:, tiles(g), :], ALU.add).then_inc(ln_step, 1)
                    done(2)
                    layernorm(lambda k: done(2 + k), g, cat[:, h, :, D:2 * D]).then_inc(y_set, 1)

            pair(0)
            with dve.Fori(1, GROUPS // 2) as i:
                pair(i)

            for h in range(2):
                group_rows(h, h, group1_set)
                dve.wait_ge(scan0_out[h], 16 * PAIRS)
            dve.wait_ge(state_set, GROUPS)
            split_nodes(state[:, :, :]).then_inc(node_parts_set, 1)
            dve.wait_ge(node_parts_set, 1)

            def pair(i, last=False):
                for h in range(2):
                    n = i * 2 + h

                    def with_quad(q):
                        if q == 0:
                            wait_past(dve, scan1_set[1 - h], i + h)
                            continues(n).then_inc(cont_set, 1)
                        if q == 1:
                            dve.wait_ge(cont_set, n + 1)
                            dve.wait_ge(rows_made[1], n * layers[1].duos + layers[1].duos)
                            dve.wait_ge(rows1_in[h], i * (16 * layers[1].own) + 16 * layers[1].own)
                            index(layers[1], n + 2, h, idx1_set)
                            wait_past(dve, scan1_out[h], i * 16)
                        if q in (1, 2):
                            for f in range((q - 1) * D // 2, q * D // 2):
                                last_scan = scan(h, 0, f, rows1[:, h, :, :])
                        if q == 2:
                            last_scan.then_inc(scan1_set[h], 1)

                    if last and h == 1:
                        for q in range(QUADS):
                            with_quad(q)
                    else:
                        chunk_rows(layers[1], n + 1, 1 - h, last, with_quad)

            chunk_rows(layers[1], 0, 0, False)
            pair(0)
            with dve.Fori(1, PAIRS - 1) as i:
                pair(i)
            pair(PAIRS - 1, True)
            carries(1, D, scan1_set[1])
            sum_edges(1, D)

            PER1 = 4 + LN_STEPS

            def take_in_sums(i, h, ahead):
                g, half = i * 2 + (h + ahead), (h + ahead) % 2
                dve.tensor_copy(cat[:, half, :, D:2 * D], state[:, tiles(g), :])
                dve.wait_ge(sums1_in[half], (i + (h + ahead) // 2) * SUMS_IN + SUMS_IN)
                group_rows(g + 2, half, group1_set)
                dve.tensor_copy(cat[:, half, :, 0:D], sums1[:, half, :, :]).then_inc(m_set, 1)

            def pair(i, last=False):
                for h in range(2):
                    g = i * 2 + h
                    pre = gate_view(h)
                    old = cat[:, h, :, D:2 * D]

                    def done(k):
                        dve.wait_ge(ln_step, i * (2 * PER1) + (GROUPS * PER0 + h * PER1 + k))

                    wait_past(dve, out_set[1 - h], i + h)
                    dve.wait_ge(gates_set, g + 1)
                    dve.tensor_tensor(tmp[:, :, :], pre[:, :, 3 * D:4 * D], gates[:, :, 0:D], ALU.mult
                                      ).then_inc(ln_step, 1)
                    done(1)
                    dve.tensor_tensor(tmp[:, :, :], pre[:, :, 2 * D:3 * D], tmp[:, :, :], ALU.add).then_inc(pre_set, 1)
                    if not (last and h == 1):
                        take_in_sums(i, h, 1)
                    dve.wait_ge(cand_set, g + 1)
                    dve.tensor_tensor(val[:, :, :], old, cand[:, :, :], ALU.subtract).then_inc(ln_step, 1)
                    done(2)
                    dve.tensor_tensor(val[:, :, :], val[:, :, :], gates[:, :, D:2 * D], ALU.mult).then_inc(ln_step, 1)
                    done(3)
                    dve.tensor_tensor(val[:, :, :], val[:, :, :], cand[:, :, :], ALU.add).then_inc(gates_used, 1)
                    dve.wait_ge(gates_used, g + 1)
                    dve.tensor_tensor(val[:, :, :], val[:, :, :], old, ALU.add).then_inc(ln_step, 1)
                    done(4)
                    wait_past(dve, out_out[h], i * 16)
                    layernorm(lambda k: done(4 + k), g + GROUPS, out_buf[:, h, :, :]).then_inc(out_set[h], 1)

            take_in_sums(0, 0, 0)
            pair(0)
            with dve.Fori(1, GROUPS // 2 - 1) as i:
                pair(i)
            pair(GROUPS // 2 - 1, True)


INPUTS = ["x", "src", "dst", "edge_attr_16", "edge_type_8", "edge_type_90", "L0_gnn_Ws", "L0_gnn_Wa",
          "L0_gnn_weight", "L0_gnn_w_comp", "L1_gnn_edge_emb", "L1_gnn_w_ih", "L1_gnn_w_hh", "L1_gnn_b_ih",
          "L1_gnn_b_hh"]


def kernel(**inputs):
    import numpy as np
    import concourse.bacc as bacc
    from concourse.bass_utils import run_bass_kernel_spmd

    nc = bacc.Bacc("TRN2", target_bir_lowering=False, num_devices=1)
    arrays, args = {}, []
    for name in INPUTS:
        a = np.ascontiguousarray(inputs[name])
        arrays[f"in_{name}"] = a
        args.append(nc.dram_tensor(f"in_{name}", a.shape, mybir.dt.from_np(a.dtype), kind="ExternalInput").ap())
    result = nc.dram_tensor("result", inputs["x"].shape, F32, kind="ExternalOutput").ap()
    build(nc, *args, result)
    return run_bass_kernel_spmd(nc, [arrays], core_ids=[0]).results[0]["result"]
```
